# Optimizing a Trainium2 kernel written in Bass

```python
import numpy as np
import jax
import jax.numpy as jnp

def _softmax(x, axis=-1):
    return jax.nn.softmax(x, axis=axis)

def _gelu(x):
    return jax.nn.gelu(x, approximate=True)

def _silu(x):
    return jax.nn.silu(x)

def _sigmoid(x):
    return jax.nn.sigmoid(x)

def _layernorm(x, axis=-1, eps=1e-05):
    m = jnp.mean(x, axis=axis, keepdims=True)
    v = jnp.var(x, axis=axis, keepdims=True)
    return (x - m) / jnp.sqrt(v + eps)

def _scatter_add(tgt, idx, src, axis=0):
    return tgt.at[idx].add(src)

def _segment_sum(src, seg, n):
    return jax.ops.segment_sum(src, seg, n)
kernel_name = 'mk_adj_resnorm_d4_adj_r2_4502d5'

def setup_inputs(seed: int=0):
    np.random.seed(seed)
    _w = jnp.asarray

    def _rec_inputs():
        import jax
        import jax.numpy as jnp
        _gk = jax.random.key(seed)
        x = -0.0004776 + 1.001 * jax.random.normal(jax.random.fold_in(_gk, 1), (1354, 512), jnp.float32)
        _a = jax.random.bernoulli(jax.random.fold_in(_gk, 2), 0.00590842, (1354, 1354))
        _a = jnp.logical_or(_a, jnp.eye(1354, dtype=bool))
        _af = _a.astype(jnp.float32)
        adj = _af
        return (x, adj)
    x, adj = _rec_inputs()

    def _L0_gnn_setup():
        import jax, jax.numpy as jnp
        import numpy as np
        N, H, E, HEADS = (1500, 512, 10000, 8)
        DK = H // HEADS
        key = jax.random.key(seed)
        k1, k2, k3, k4 = jax.random.split(key, 4)
        inst_feature = jax.random.normal(k1, (N, H), dtype=jnp.float32)
        rel_pair_index = jax.random.randint(k2, (E, 2), 0, N, dtype=jnp.int64)
        agg = jnp.zeros((N, N), dtype=jnp.float32)
        agg = agg.at[rel_pair_index[:, 0], rel_pair_index[:, 1]].set(1.0)
        agg = agg.at[jnp.arange(N), jnp.arange(N)].set(1.0)
        std = float(np.sqrt(2.0 / (H + DK)))
        Wq = jax.random.normal(k3, (H, H), dtype=jnp.float32) * std
        Wk = jax.random.normal(k4, (H, H), dtype=jnp.float32) * std
        bq = jnp.zeros((H,), dtype=jnp.float32)
        bk = jnp.zeros((H,), dtype=jnp.float32)
        return {'inst_feature': inst_feature, 'aggregator_matrix': agg, 'rel_pair_index': rel_pair_index, 'Wq': Wq, 'bq': bq, 'Wk': Wk, 'bk': bk}
    _L0_gnn_all = _L0_gnn_setup()
    _L0_gnn_in = {k: v for k, v in _L0_gnn_all.items() if k in ('rel_pair_index', 'Wq', 'bq', 'Wk', 'bk')}
    del _L0_gnn_all

    def _L1_gnn_setup():
        import jax, jax.numpy as jnp
        import numpy as np
        N = 4096
        D = 512

        def adjacent_mat(adj):
            adj = adj + jnp.eye(adj.shape[0], dtype=adj.dtype)
            deg = jnp.sum(adj, axis=1)
            dinv = jnp.where(deg > 0, deg ** (-0.5), 0.0).astype(adj.dtype)
            return dinv[:, None] * adj * dinv[None, :]
        key = jax.random.key(seed)
        k1, k2 = jax.random.split(key)
        x = jax.random.normal(k1, (N, D), dtype=jnp.float32)
        Coefficient2 = 1e-08 * jnp.ones((N, N), dtype=jnp.float32)
        A = jax.random.uniform(k2, (N, N), dtype=jnp.float32)
        return {'x': x, 'Coefficient2': Coefficient2, 'A': A}
    _L1_gnn_all = _L1_gnn_setup()
    _L1_gnn_in = {k: v for k, v in _L1_gnn_all.items() if k in ()}
    del _L1_gnn_all

    def _L2_gnn_setup():
        import jax, jax.numpy as jnp
        import numpy as np
        N = 4096
        IN_FEATURES = 512
        OUT_FEATURES = 512
        key = jax.random.key(seed)
        k_x, k_adj, k_w, k_b = jax.random.split(key, 4)
        x = jax.random.normal(k_x, (N, IN_FEATURES), dtype=jnp.float32)
        adj = jax.random.uniform(k_adj, (N, N), dtype=jnp.float32)
        stdv = 1.0 / np.sqrt(OUT_FEATURES)
        weight = jax.random.uniform(k_w, (IN_FEATURES, OUT_FEATURES), dtype=jnp.float32, minval=-stdv, maxval=stdv)
        bias = jax.random.uniform(k_b, (OUT_FEATURES,), dtype=jnp.float32, minval=-stdv, maxval=stdv)
        return {'x': x, 'adj': adj, 'weight': weight, 'bias': bias}
    _L2_gnn_all = _L2_gnn_setup()
    _L2_gnn_in = {k: v for k, v in _L2_gnn_all.items() if k in ('weight', 'bias')}
    del _L2_gnn_all

    def _L3_gnn_setup():
        import jax, jax.numpy as jnp
        import numpy as np
        import math
        SENT_DIM = 512
        N_SENT = 2048
        key = jax.random.key(seed)
        ks = jax.random.split(key, 8)
        D = SENT_DIM
        s = 1.0 / math.sqrt(D)
        return {'sent_embed': jax.random.normal(ks[0], (N_SENT, D), dtype=jnp.float32), 'adj_tensor': jax.random.randint(ks[1], (N_SENT, N_SENT), 0, 2).astype(jnp.float32), 'W_q': jax.random.uniform(ks[2], (D, D), jnp.float32, -s, s), 'b_q': jax.random.uniform(ks[3], (D,), jnp.float32, -s, s), 'W_k': jax.random.uniform(ks[4], (D, D), jnp.float32, -s, s), 'b_k': jax.random.uniform(ks[5], (D,), jnp.float32, -s, s), 'W_v': jax.random.uniform(ks[6], (D, D), jnp.float32, -s, s), 'b_v': jax.random.uniform(ks[7], (D,), jnp.float32, -s, s)}
    _L3_gnn_all = _L3_gnn_setup()
    _L3_gnn_in = {k: v for k, v in _L3_gnn_all.items() if k in ('W_q', 'b_q', 'W_k', 'b_k', 'W_v', 'b_v')}
    del _L3_gnn_all
    return {'x': x, 'adj': adj, 'L0_gnn_rel_pair_index': _L0_gnn_in['rel_pair_index'], 'L0_gnn_Wq': _L0_gnn_in['Wq'], 'L0_gnn_bq': _L0_gnn_in['bq'], 'L0_gnn_Wk': _L0_gnn_in['Wk'], 'L0_gnn_bk': _L0_gnn_in['bk'], 'L2_gnn_weight': _L2_gnn_in['weight'], 'L2_gnn_bias': _L2_gnn_in['bias'], 'L3_gnn_W_q': _L3_gnn_in['W_q'], 'L3_gnn_b_q': _L3_gnn_in['b_q'], 'L3_gnn_W_k': _L3_gnn_in['W_k'], 'L3_gnn_b_k': _L3_gnn_in['b_k'], 'L3_gnn_W_v': _L3_gnn_in['W_v'], 'L3_gnn_b_v': _L3_gnn_in['b_v']}

def reference(x, adj, L0_gnn_rel_pair_index, L0_gnn_Wq, L0_gnn_bq, L0_gnn_Wk, L0_gnn_bk, L2_gnn_weight, L2_gnn_bias, L3_gnn_W_q, L3_gnn_b_q, L3_gnn_W_k, L3_gnn_b_k, L3_gnn_W_v, L3_gnn_b_v):
    import jax
    import jax.numpy as jnp

    def _L0_gnn_ref(inst_feature, aggregator_matrix, rel_pair_index, Wq, bq, Wk, bk):
        import jax, jax.numpy as jnp
        import numpy as np
        N, H, E, HEADS = (1500, 512, 10000, 8)
        DK = H // HEADS
        n = inst_feature.shape[0]
        sub = rel_pair_index[:, 0]
        obj = rel_pair_index[:, 1]
        q = (inst_feature[sub] @ Wq.T + bq).reshape(-1, HEADS, DK)
        k = (inst_feature[obj] @ Wk.T + bk).reshape(-1, HEADS, DK)
        att = ((q * k).sum(-1) / np.sqrt(DK)).T.astype(inst_feature.dtype)
        scores = jnp.zeros((HEADS, n, n), dtype=inst_feature.dtype)
        scores = scores.at[:, sub, obj].set(att)
        mask = (1.0 - aggregator_matrix).astype(bool)
        scores = jnp.where(mask[None], -jnp.inf, scores)
        di = jnp.arange(n)
        scores = scores.at[:, di, di].set(1e-07)
        attn = jax.nn.softmax(scores, axis=2)
        aggregator_factor = attn.sum(axis=0) / HEADS
        return aggregator_factor @ inst_feature

    def _L1_gnn_ref(x, Coefficient2, A):
        import jax, jax.numpy as jnp
        import numpy as np
        N = 4096
        D = 512

        def adjacent_mat(adj):
            adj = adj + jnp.eye(adj.shape[0], dtype=adj.dtype)
            deg = jnp.sum(adj, axis=1)
            dinv = jnp.where(deg > 0, deg ** (-0.5), 0.0).astype(adj.dtype)
            return dinv[:, None] * adj * dinv[None, :]
        A_c = jax.lax.stop_gradient(A)
        adj = adjacent_mat((A_c + A_c.T) * 0.5)
        y = Coefficient2 @ adj
        y = y @ x
        return y

    def _L2_gnn_ref(x, adj, weight, bias):
        import jax, jax.numpy as jnp
        import numpy as np
        N = 4096
        IN_FEATURES = 512
        OUT_FEATURES = 512
        support = jnp.matmul(x, weight)
        output = jnp.matmul(adj, support)
        return output + bias

    def _L3_gnn_ref(sent_embed, adj_tensor, W_q, b_q, W_k, b_k, W_v, b_v):
        import jax, jax.numpy as jnp
        import numpy as np
        import math
        SENT_DIM = 512
        N_SENT = 2048
        q = sent_embed @ W_q.T + b_q
        k = sent_embed @ W_k.T + b_k
        v = sent_embed @ W_v.T + b_v
        scale = 1.0 / math.sqrt(sent_embed.shape[-1])
        z = scale * (q @ k.T)
        spare_z = z * adj_tensor
        spare_z = jnp.where(spare_z == 0.0, jnp.asarray(-10000.0, spare_z.dtype), spare_z)
        attn = jax.nn.softmax(spare_z, axis=1)
        out = attn @ v
        return jax.nn.relu(out)
    x = _layernorm(x + _L0_gnn_ref(x, adj, L0_gnn_rel_pair_index, L0_gnn_Wq, L0_gnn_bq, L0_gnn_Wk, L0_gnn_bk), axis=-1)
    x = _layernorm(x + _L1_gnn_ref(x, adj, adj), axis=-1)
    x = _layernorm(x + _L2_gnn_ref(x, adj, L2_gnn_weight, L2_gnn_bias), axis=-1)
    x = _layernorm(x + _L3_gnn_ref(x, adj, L3_gnn_W_q, L3_gnn_b_q, L3_gnn_W_k, L3_gnn_b_k, L3_gnn_W_v, L3_gnn_b_v), axis=-1)
    return x

_drawn_inputs = setup_inputs


def setup_inputs(seed=0):
    import zlib

    import numpy as np

    out = dict(_drawn_inputs(seed))
    spreads = {'L0_gnn_bq': (0.0, 2.0), 'L0_gnn_bk': (0.0, 2.0)}
    factors = {'L0_gnn_Wq': 15.167,
     'L0_gnn_Wk': 49.647,
     'L2_gnn_bias': 5.186,
     'L3_gnn_b_q': 35.77,
     'L3_gnn_b_k': 200.0,
     'L3_gnn_b_v': 3.162}
    for name, (base, spread) in spreads.items():
        noise = np.random.default_rng([zlib.crc32(name.encode()), seed]).standard_normal(out[name].shape)
        drawn = base * np.exp(spread * noise) if base else spread * noise
        out[name] = jnp.asarray(drawn.astype(out[name].dtype))
    for name, factor in factors.items():
        out[name] = (out[name] * factor).astype(out[name].dtype)
    return out
```

```python
from contextlib import ExitStack

import concourse.bass as bass
from concourse import mybir

ALU = mybir.AluOpType
ACT = mybir.ActivationFunctionType
F32 = mybir.dt.float32
F16 = mybir.dt.float16
BF16 = mybir.dt.bfloat16
I32 = mybir.dt.int32
U32 = mybir.dt.uint32
ds = bass.ds

P = 128
N = 1354
D = 512
T = -(-N // P)
NP = T * P
TAIL = N - (T - 1) * P
C = D // P
G = 3
GW = 452
NG = G * GW
HEADS = 8
E = 10000
EP, EC = 125, 80
OC = 16

SX = 256.0
SW0 = 64.0
SK = 16.0
SW = 1024.0
SP_ = 4096.0
SB = 16.0
EPS = 1e-5
DIAG = 1e-7
E_DIAG = 0.9999999
OFF = 1e30
FAR = 8.0e6
FILL = -10000.0
Z_SCALE = float(D) ** -0.5 / (SX * SW)



def build(nc, x_d, adj_d, rel_d, wq0_d, bq0_d, wk0_d, bk0_d, w2_d, b2_d, wq3_d, bq3_d, wk3_d, bk3_d,
          wv3_d, bv3_d, out_d):
    ctx = ExitStack()
    with ctx:
        def sb(name, shape, dt):
            return ctx.enter_context(nc.sbuf_tensor(name, shape, dt))

        def sem(name):
            return ctx.enter_context(nc.semaphore(name))

        A = sb("A", [P, T, NP], F16)
        AT = sb("AT", [P, T, NP], F16)
        X = sb("X", [P, T, D], F32)
        R1 = sb("R1", [P, T * NP], F16)
        R2 = sb("R2", [P, 2 * T * D], F16)
        R3 = sb("R3", [P, 2 * T * D], F16)
        R4 = sb("R4", [P, 2 * C * NP], F16)
        WA = sb("WA", [P, 2 * C * D], F16)
        WB = sb("WB", [P, 2 * C * D], F16)

        ident = sb("ident", [P, P], F16)
        identb = sb("identb", [P, P], BF16)
        iota = sb("iota", [P, NP], F16)
        before = sb("before", [P, P], F16)
        after = sb("after", [P, P], F16)
        ones = sb("ones", [P, P], F16)
        rel = sb("rel", [EP, 2 * EC], I32)
        subf = sb("subf", [EP, EC], F32)
        objf = sb("objf", [EP, EC], F32)
        bad = sb("bad", [EP, EC], F32)
        rel_ix = sb("rel_ix", [EP, EC], U32)
        hit = sb("hit", [EP, EC], F32)
        act16 = sb("act16", [EP, EC], F16)
        rank = sb("rank", [EP, EC], F16)
        pair = sb("pair", [EP, EC, 2], F16)
        tot16 = sb("tot16", [EC, P], F16)
        n_act = sb("n_act", [1, 1], I32)
        small = sb("small", [P, 256], F32)
        slot_ix = sb("slot_ix", [P, 1], U32)
        b_hl = sb("b_hl", [P, 2, 2 * C], F16)
        ident2 = sb("ident2", [P, P], F16)

        PS = ctx.enter_context(nc.psum_tensor("PS", [P, 8, 512], F32))
        PS16 = PS[:, :, :].rearrange("p b n -> p (b n)").bitcast(F16)

        n_cols = [0]

        def cols(n=1):
            n_cols[0] += n
            return small[:, n_cols[0] - n:n_cols[0]]

        bk0, bq0, bk3, bq3, c2 = (cols(C) for _ in range(5))
        mx, nb, zs, em, rz, g_tmp = (cols(HEADS) for _ in range(6))
        slot_row, slot_obj, slot_far, slot_low, rep, g_sum, row_id = (cols() for _ in range(7))
        beta, r_acc, r3, m3, nm3, z3 = (cols() for _ in range(6))
        row_n, col_n, c_a, c_b, nohas, dinv, dinv_half, dinv_s, mhalfs, rz_all = (cols(T) for _ in range(10))
        ln_st, ln_mv, ln_var, ln_rstd = cols(6), cols(2), cols(), cols()

        def parts(region, at, *shape):
            n = 1
            for k in shape:
                n *= k
            v = region[:, at:at + n]
            if len(shape) == 2:
                return v.rearrange("p (a b) -> p a b", a=shape[0])
            if len(shape) == 3:
                return v.rearrange("p (a b c) -> p a b c", a=shape[0], b=shape[1])
            return v

        def words(region, at, *shape):
            n = 2
            for k in shape:
                n *= k
            v = region[:, 2 * at:2 * at + n].bitcast(F32)
            if len(shape) == 2:
                return v.rearrange("p (a b) -> p a b", a=shape[0])
            return v

        def flat(v):
            return v.rearrange("p a b -> p (a b)")

        KT = parts(R1, 0, 2, C, NG)
        kf = words(R1, 5424, G, GW)
        bmask = R1[:, 10848:10848 + NG].bitcast(BF16)
        wmask = parts(R1, 12204, NG)
        dmask = parts(R1, 13560, NP)
        SYM = parts(R1, 0, T, NP)
        XHL = parts(R1, 0, 2, T, D)
        WVT = parts(R1, 2 * T * D, 2, C, D)
        score = words(R1, 0, NG)
        zero_fill = words(R1, NG, NG)
        prob_hl = parts(R1, 4 * NG, 2, NP)
        prob_t = parts(R1, 4 * NG + 2 * NP, 2, T, P)
        UHL = parts(R2, 0, 2, T, D)
        wv_f = words(R2, 0, C, D)
        wv_hl = parts(R2, 4096, 2, C, D)
        a_row, b2_row, bv_row = (words(R2, 4096 + D * i, D) for i in range(3))
        out_t = words(R2, 0, D)
        wk0_f = words(R3, 0, C, D)
        w0_hl = parts(R3, 4096, 2, C, D)
        BASE = words(R3, 0, T, D)
        VHL = parts(R3, 0, 2, T, D)
        wq0_f = words(AT[:, :, :].rearrange("p a b -> p (a b)"), 0, C, D)
        w0q_hl = parts(AT[:, :, :].rearrange("p a b -> p (a b)"), 4096, 2, C, D)
        XT = parts(R4, 0, 2, C, NP)
        prob = [words(R4, NG * i, NG) for i in range(3)]
        fsum = words(R4, 3 * NG, NG)
        sub_b = parts(R4, 8 * NG, P)
        same = parts(R4, 8 * NG + P, P)
        obj_hot = parts(R4, 0, NG)
        adj_c = prob[1]
        qf0 = words(R4, 0, C, P)
        x_c = words(R4, 2 * NG, D)
        f_hl = parts(R4, 0, 2, NP)
        f_t = parts(R4, 2 * NP, 2, T, P)
        all_sub = [sub_b, same]
        all_obj = [parts(R4, 0, NG), parts(R4, NG, NG)]
        wq3_hl = parts(R4, 0, 2, C, D)
        wk3_hl = parts(R4, 4096, 2, C, D)
        w_stage = words(R4, 4096, 2, D)
        bk_b = parts(R4, 10240, 2, C, P)
        WKT = parts(WA, 0, 2, C, D)
        WQT = parts(WB, 0, 2, C, D)
        hot = [parts(WA, 2048 * i, OC, P) for i in range(2)]
        q_hl = parts(WA, 0, 2, C, P)
        xc_hl = parts(WA, 1024, 2, D)
        xct = parts(WA, 2048, 2, C, P)
        y_hl = parts(WA, 3072, 2, D)
        W2HL = parts(WA, 0, 2, C, D)
        GHL = parts(WB, 0, 2, C, D)
        ATF = AT[:, :, :].rearrange("p a b -> p (a b)")
        QT = parts(ATF, 0, 2, C, NP)
        qf = words(R2, C * D, G, GW)

        s_rel_in = sem("rel_in")
        s_x_in0 = sem("x_in0")
        s_x_in = sem("x_in")
        s_x_pad = sem("x_pad")
        s_wk0_in = sem("wk0_in")
        s_wq0_in = sem("wq0_in")
        s_b_in = sem("b_in")
        s_all_done = sem("all_done")
        s_wst_lo = sem("wst_lo")
        s_wst_in = sem("wst_in")
        s_prod_mm = sem("prod_mm")
        s_wv_in = sem("wv_in")
        s_b3_in = sem("b3_in")
        s_o_norm = sem("o_norm")
        s_stored = sem("stored")
        s_a_pad = sem("a_pad")
        s_adj_in = sem("adj_in")
        s_blank = sem("blank")
        s_ident_ready = sem("ident_ready")
        s_const = sem("const")
        s_ix_ready = sem("ix_ready")
        s_hit_in = sem("hit_in")
        s_deg_ready = sem("deg_ready")
        s_dinv_ready = sem("dinv_ready")
        s_slots_ready = sem("slots_ready")
        s_slot_fill = sem("slot_fill")
        s_gathered = sem("gathered")
        s_n_ready = sem("n_ready")
        s_ln_v = sem("ln_v")
        s_ln_rstd = sem("ln_rstd")
        s_sym_sum = sem("sym_sum")
        s_sym_ready = sem("sym_ready")
        s_at_v = sem("at_v")
        s_at_a = sem("at_a")
        s_x_hi = sem("x_hi")
        s_w0_hi = sem("w0_hi")
        s_xt_out = sem("xt_out")
        s_xt_mm = sem("xt_mm")
        s_kf_ready = sem("kf_ready")
        s_bias0 = sem("bias0")
        s_kp_mm = sem("kp_mm")
        s_kt_done = sem("kt_done")
        s_at_mm = sem("at_mm")
        s_base_scaled = sem("base_scaled")
        s_closed_ready = sem("closed_ready")
        s_xc_hi = sem("xc_hi")
        s_xct_mm = sem("xct_mm")
        s_xct_out = sem("xct_out")
        s_q_mm = sem("q_mm")
        s_q_full = sem("q_full")
        s_nb_ready = sem("nb_ready")
        s_p_ready = sem("p_ready")
        s_em_ready = sem("em_ready")
        s_f_done = sem("f_done")
        s_f_hi = sem("f_hi")
        s_ft_mm = sem("ft_mm")
        s_ft_hi = sem("ft_hi")
        s_y_mm = sem("y_mm")
        s_y_hi = sem("y_hi")
        s_ln_x = sem("ln_x")
        s_u_hi = sem("u_hi")
        s_wst_hi = sem("wst_hi")
        s_w1_hi = sem("w1_hi")
        s_wv_hi = sem("wv_hi")
        s_g_mm = sem("g_mm")
        s_g_hi = sem("g_hi")
        s_vec_mm = sem("vec_mm")
        s_vec_out = sem("vec_out")
        s_rows_mm = sem("rows_mm")
        s_rows_hi = sem("rows_hi")
        s_qf_ready = sem("qf_ready")
        s_qt_mm = sem("qt_mm")
        s_qt_done = sem("qt_done")
        s_nm3_ready = sem("nm3_ready")
        s_p3_ready = sem("p3_ready")
        s_pt_mm = sem("pt_mm")
        s_ph_ready = sem("ph_ready")
        s_o_mm = sem("o_mm")
        s_pt_hi = sem("pt_hi")
        s_w0_out = sem("w0_out")
        s_put_done = sem("put_done")
        s_step = sem("step")
        s_x_lo = sem("x_lo")
        s_w0_lo = sem("w0_lo")
        s_w0_mm = sem("w0_mm")
        s_kh_done = sem("kh_done")
        s_sums_mm = sem("sums_mm")
        s_base_done = sem("base_done")
        s_dinv_s_ready = sem("dinv_s_ready")
        s_act_ready = sem("act_ready")
        s_tot_mm = sem("tot_mm")
        s_tot_ready = sem("tot_ready")
        s_rank_mm = sem("rank_mm")
        s_rank_ready = sem("rank_ready")
        s_d_ready = sem("d_ready")
        s_w_mm = sem("w_mm")
        s_w_step = sem("w_step")
        s_mask_ready = sem("mask_ready")
        s_xc_lo = sem("xc_lo")
        s_q_hi = sem("q_hi")
        s_q_lo = sem("q_lo")
        s_z_ready = sem("z_ready")
        s_rz_ready = sem("rz_ready")
        s_f_step = sem("f_step")
        s_s_mm = sem("s_mm")
        s_t_ready = sem("t_ready")
        s_f_pad = sem("f_pad")
        s_g_step = sem("g_step")
        s_f_lo = sem("f_lo")
        s_ft_lo = sem("ft_lo")
        s_all_step = sem("all_step")
        s_slot_step = sem("slot_step")
        s_hots_free = sem("hots_free")
        s_hots_sub = sem("hots_sub")
        s_hots_obj = sem("hots_obj")
        s_slots_mm = sem("slots_mm")
        s_hot_ready = sem("hot_ready")
        s_sub_ready = sem("sub_ready")
        s_obj_ready = sem("obj_ready")
        s_sub_mm = sem("sub_mm")
        s_same_ready = sem("same_ready")
        s_rep_ready = sem("rep_ready")
        s_y_lo = sem("y_lo")
        s_put_ready = sem("put_ready")
        s_has_mm = sem("has_mm")
        s_has_ready = sem("has_ready")
        s_put_mm = sem("put_mm")
        s_ln_r = sem("ln_r")
        s_ln_s = sem("ln_s")
        s_ln_m = sem("ln_m")
        s_u_lo = sem("u_lo")
        s_w1_lo = sem("w1_lo")
        s_bkb_ready = sem("bkb_ready")
        s_wv_lo = sem("wv_lo")
        s_g_lo = sem("g_lo")
        s_wvt_mm = sem("wvt_mm")
        s_wvt_out = sem("wvt_out")
        s_rows_lo = sem("rows_lo")
        s_x3_add = sem("x3_add")
        s_qh_done = sem("qh_done")
        s_pad3 = sem("pad3")
        s_t3_ready = sem("t3_ready")
        s_r_step = sem("r_step")
        s_r_ready = sem("r_ready")
        s_z_mm = sem("z_mm")
        s_nz_ready = sem("nz_ready")
        s_m3_ready = sem("m3_ready")
        s_pl_ready = sem("pl_ready")
        s_rz3_step = sem("rz3_step")
        s_rz3_ready = sem("rz3_ready")
        s_pt_lo = sem("pt_lo")
        s_o_ready = sem("o_ready")
        block = ctx.enter_context(nc.Block())

        def row(buf, t):
            return buf[:, ds(t, 1), :].rearrange("p a n -> p (a n)")

        def part_row(buf, i, t):
            return buf[:, i, ds(t, 1), :].rearrange("p a n -> p (a n)")

        def one(c, t):
            return c[:, ds(t, 1)]


        PAIRS = ((0, 0), (0, 1), (1, 0))

        @block.sync
        def _(sp):
            sp.dma_start(rel[:, :], rel_d.rearrange("(p i) two -> p (i two)", p=EP)).then_inc(s_rel_in, 16)
            half = (T - 1) // 2
            sp.dma_start(X[:, 0:half, :], x_d[0:half * P].rearrange("(t p) d -> p t d", p=P)).then_inc(s_x_in0, 16)
            sp.dma_start(X[:, half:T - 1, :],
                         x_d[half * P:(T - 1) * P].rearrange("(t p) d -> p t d", p=P)).then_inc(s_x_in, 16)
            sp.wait_ge(s_x_pad, 1)
            sp.dma_start(X[0:TAIL, T - 1, :], x_d[(T - 1) * P:N]).then_inc(s_x_in, 16)
            sp.dma_start(wk0_f, wk0_d.rearrange("(m p) d -> p m d", p=P)).then_inc(s_wk0_in, 16)
            sp.dma_start(wq0_f, wq0_d.rearrange("(m p) d -> p m d", p=P)).then_inc(s_wq0_in, 16)
            for dst, src in ((bk0, bk0_d), (bq0, bq0_d), (bk3, bk3_d), (bq3, bq3_d)):
                sp.dma_start(dst, src.rearrange("(m p) -> p m", p=P),
                             allow_slow_non_contiguous=True).then_inc(s_b_in, 16)
            sp.wait_ge(s_all_done, 1)
            n = 0
            for src in (wq3_d, wk3_d, w2_d):
                for i in range(2):
                    if n:
                        sp.wait_ge(s_wst_lo, n)
                    sp.dma_start(w_stage, src[i * 2 * P:(i + 1) * 2 * P].rearrange("(m p) d -> p m d", p=P))\
                        .then_inc(s_wst_in, 16)
                    n += 1
            sp.wait_ge(s_prod_mm, 2 * T)
            sp.dma_start(wv_f, wv3_d.rearrange("(m p) d -> p m d", p=P)).then_inc(s_wv_in, 16)
            for dst, src in ((b2_row, b2_d), (bv_row, bv3_d)):
                sp.dma_start(dst, src.rearrange("(o n) -> o n", o=1).to_broadcast([P, D])).then_inc(s_b3_in, 16)
            with sp.Fori(0, T - 1) as t:
                sp.wait_ge(s_o_norm, t + 1)
                sp.dma_start(out_d[ds(t * P, P)], row(X, t)).then_inc(s_stored, 16)
            sp.wait_ge(s_o_norm, T)
            sp.dma_start(out_d[(T - 1) * P:N], X[0:TAIL, T - 1, :]).then_inc(s_stored, 16)
            sp.wait_ge(s_stored, 16 * T)

        @block.gpsimd
        def _(pool):
            nc.gpsimd.memset(X[:, T - 1, :], 0.0).then_inc(s_x_pad, 1)
            nc.gpsimd.memset(A[:, T - 1, :], 0.0).then_inc(s_a_pad, 1)
            nc.gpsimd.memset(A[:, 0:T - 1, N:NP], 0.0).then_inc(s_a_pad, 1)
            pool.wait_ge(s_a_pad, 2)
            for a, b in ((0, 4), (4, 7), (7, T - 1)):
                pool.dma_start(A[:, a:b, 0:N], adj_d[a * P:b * P].rearrange("(t p) n -> p t n", p=P))\
                    .then_inc(s_adj_in, 16)
            pool.dma_start(A[0:TAIL, T - 1, 0:N], adj_d[(T - 1) * P:N]).then_inc(s_adj_in, 16)
            nc.gpsimd.memset(ident[:, :], 0.0).then_inc(s_blank, 1)
            nc.gpsimd.memset(ones[:, :], 1.0).then_inc(s_blank, 1)
            pool.wait_ge(s_blank, 2)
            nc.gpsimd.affine_select(out=ident[:, :], in_=ident[:, :], compare_op=ALU.not_equal, fill=1.0, base=0,
                                    pattern=[[-1, P]], channel_multiplier=1).then_inc(s_ident_ready, 1)
            nc.gpsimd.iota(iota[:, :], [[1, NP]], channel_multiplier=0,
                           allow_small_or_imprecise_dtypes=True).then_inc(s_const, 1)
            nc.gpsimd.affine_select(out=before[:, :], in_=ones[:, :], compare_op=ALU.is_gt, fill=0.0, base=0,
                                    pattern=[[1, P]], channel_multiplier=-1).then_inc(s_const, 1)
            nc.gpsimd.affine_select(out=after[:, :], in_=ones[:, :], compare_op=ALU.is_gt, fill=0.0, base=0,
                                    pattern=[[-1, P]], channel_multiplier=1).then_inc(s_const, 1)
            nc.gpsimd.iota(row_id, [[0, 1]], channel_multiplier=1,
                           allow_small_or_imprecise_dtypes=True).then_inc(s_const, 1)
            nc.gpsimd.memset(mhalfs, -0.5).then_inc(s_const, 1)
            pool.wait_ge(s_ident_ready, 1)
            nc.gpsimd.tensor_copy(identb[:, :], ident[:, :]).then_inc(s_const, 1)
            nc.gpsimd.tensor_tensor(ident2[:, :], ident[:, :], ident[:, :], ALU.add).then_inc(s_const, 1)
            pool.wait_ge(s_ix_ready, 1)
            for i in range(EC):
                nc.gpsimd.indirect_dma_start(
                    out=hit[:, i:i + 1], out_offset=None, in_=adj_d.rearrange("a (b o) -> (a b) o", o=1),
                    in_offset=bass.IndirectOffsetOnAxis(ap=rel_ix[:, i:i + 1], axis=0),
                    bounds_check=N * N - 1, oob_is_err=False).then_inc(s_hit_in, 16)
            pool.wait_ge(s_deg_ready, 1)
            pool.wait_ge(s_const, 7)
            nc.gpsimd.tensor_tensor(dinv, dinv, mhalfs, ALU.pow).then_inc(s_dinv_ready, 1)

            def gather_rows(r):
                pool.wait_ge(s_slots_ready, r + 1)
                pool.nop(nofuse=True)
                nc.gpsimd.memset(adj_c, 0.0).then_inc(s_slot_fill, 1)
                nc.gpsimd.memset(x_c, 0.0).then_inc(s_slot_fill, 1)
                pool.wait_ge(s_slot_fill, 2 * r + 2)
                pool.nop(nofuse=True)
                nc.gpsimd.indirect_dma_start(
                    out=x_c, out_offset=None, in_=x_d,
                    in_offset=bass.IndirectOffsetOnAxis(ap=slot_ix[:, 0:1], axis=0),
                    bounds_check=N - 1, oob_is_err=False).then_inc(s_gathered, 16)
                nc.gpsimd.indirect_dma_start(
                    out=adj_c[:, 0:N], out_offset=None, in_=adj_d,
                    in_offset=bass.IndirectOffsetOnAxis(ap=slot_ix[:, 0:1], axis=0),
                    bounds_check=N - 1, oob_is_err=False).then_inc(s_gathered, 16)

            pool.wait_ge(s_n_ready, 1)
            many = pool.value_load(n_act[0:1, 0:1])
            with pool.If(many > P):
                with pool.Fori(0, T) as t:
                    gather_rows(t)
            with pool.Else():
                gather_rows(0)

            def rstd(n):
                pool.wait_ge(s_ln_v, n + 1)
                nc.gpsimd.tensor_tensor(ln_rstd, ln_var, mhalfs[:, 0:1], ALU.pow).then_inc(s_ln_rstd, 1)

            def symmetric(t):
                blk = ds(t * P, P)
                nc.gpsimd.tensor_tensor(SYM[:, :, blk], A[:, :, blk], AT[:, :, blk], ALU.add).then_inc(s_sym_sum, 1)
                pool.wait_ge(s_sym_sum, t + 1)
                diag = SYM[:, ds(t, 1), blk].rearrange("p a n -> p (a n)")
                nc.gpsimd.tensor_tensor(diag, diag, ident2[:, :], ALU.add).then_inc(s_sym_ready, 1)

            pool.wait_ge(s_all_done, 1)
            pool.wait_ge(s_at_v, 1 + (T + 1) // 2)
            pool.wait_ge(s_at_a, 1 + T // 2)
            with pool.Fori(0, T) as t:
                symmetric(t)
                rstd(t)
            with pool.Fori(T, 4 * T) as n:
                rstd(n)

        @block.scalar
        def _(act):
            half = (T - 1) // 2

            def x_hi(t):
                nc.scalar.activation(part_row(UHL, 0, t), row(X, t), ACT.Copy, scale=SX).then_inc(s_x_hi, 1)

            act.wait_ge(s_x_in0, 16)
            with act.Fori(0, half) as t:
                x_hi(t)
            act.wait_ge(s_x_in, 32)
            with act.Fori(half, T) as t:
                x_hi(t)
            act.wait_ge(s_wk0_in, 16)
            nc.scalar.activation(w0_hl[:, 0], wk0_f, ACT.Copy, scale=SW0).then_inc(s_w0_hi, 1)
            act.wait_ge(s_wq0_in, 16)
            nc.scalar.activation(w0q_hl[:, 0], wq0_f, ACT.Copy, scale=SW0).then_inc(s_w0_hi, 1)
            act.sem_inc(s_xt_out, 2)
            with act.Fori(0, T) as t:
                act.wait_ge(s_xt_mm, t + 1)
                nc.scalar.copy(XT[:, :, :, ds(t * P, P)],
                               PS16[:, ds((t % 2) * 1024, 1024)].rearrange("p (h c n) -> p h c n", h=2, c=C))\
                    .then_inc(s_xt_out, 1)
            act.sem_inc(s_kf_ready, G)
            act.wait_ge(s_bias0, 2)
            with act.Fori(0, C) as m:
                for n in range(G):
                    act.wait_ge(s_kp_mm, G * m + n + 1)
                    act.wait_ge(s_kt_done, G * m + n + 1)
                    act.nop(nofuse=True)
                    nc.scalar.activation(kf[:, n, :], PS[:, 2 + n, 0:GW], ACT.Identity, bias=one(bk0, m),
                                         scale=SK / (SX * SW0)).then_inc(s_kf_ready, 1)
            act.sem_inc(s_at_a, 1)
            with act.Fori(0, T // 2) as j:
                act.wait_ge(s_at_mm, 2 * j + 2)
                nc.scalar.copy(AT[:, :, ds(j * 2 * P + P, P)],
                               PS16[:, 4096:4096 + NP].rearrange("p (a n) -> p a n", n=P)).then_inc(s_at_a, 1)
            act.sem_inc(s_base_scaled, 2)
            act.wait_ge(s_closed_ready, 1)
            with act.Fori(0, T) as t:
                act.wait_ge(s_prod_mm, t + 1)
                act.nop(nofuse=True)
                nc.scalar.activation(row(BASE, t), PS[:, ds(t % 2, 1), :].rearrange("p a n -> p (a n)"), ACT.Copy,
                                     scale=one(c_a, t)).then_inc(s_base_scaled, 1)

            def attend(r):
                act.wait_ge(s_gathered, 32 * r + 32)
                act.nop(nofuse=True)
                nc.scalar.activation(xc_hl[:, 0], x_c, ACT.Copy, scale=SX).then_inc(s_xc_hi, 1)
                act.wait_ge(s_xct_mm, r + 1)
                nc.scalar.copy(xct, PS16[:, 0:1024].rearrange("p (h c n) -> p h c n", h=2, c=C)).then_inc(s_xct_out, 1)
                act.wait_ge(s_q_mm, r + 1)
                for m in range(C):
                    nc.scalar.activation(qf0[:, m, :], PS[:, 1, m * P:(m + 1) * P], ACT.Identity,
                                         bias=bq0[:, m:m + 1], scale=SK / (SX * SW0)).then_inc(s_q_full, 1)
                for h in range(HEADS):
                    act.wait_ge(s_nb_ready, HEADS * r + h + 1)
                    act.nop(nofuse=True)
                    nc.scalar.activation(prob[h % 3], prob[h % 3], ACT.Exp, bias=nb[:, h:h + 1],
                                         scale=1.0 / (SK * SK * 8.0), accum_out=zs[:, h:h + 1]).then_inc(s_p_ready, 1)
                    nc.scalar.activation(em[:, h:h + 1], nb[:, h:h + 1], ACT.Exp).then_inc(s_em_ready, 1)
                act.wait_ge(s_f_done, r + 1)
                act.nop(nofuse=True)
                nc.scalar.activation(f_hl[:, 0, 0:NG], fsum, ACT.Copy, scale=SP_ / HEADS).then_inc(s_f_hi, 1)
                act.wait_ge(s_ft_mm, 2 * r + 1)
                nc.scalar.copy(f_t[:, 0], PS16[:, 2048:2048 + NP].rearrange("p (a n) -> p a n", n=P)).then_inc(s_ft_hi, 1)

            act.wait_ge(s_n_ready, 1)
            many = act.value_load(n_act[0:1, 0:1])
            with act.If(many > P):
                with act.Fori(0, T) as t:
                    attend(t)
            with act.Else():
                attend(0)
                act.wait_ge(s_y_mm, 1)
                nc.scalar.activation(y_hl[:, 0], PS[:, 0, :], ACT.Copy, scale=1.0 / SP_).then_inc(s_y_hi, 1)

            with act.Fori(0, T) as t:
                act.wait_ge(s_ln_x, t + 1)
                act.nop(nofuse=True)
                nc.scalar.activation(part_row(UHL, 0, t), row(X, t), ACT.Copy, scale=one(dinv_s, t)).then_inc(s_u_hi, 1)

            def stage_hi(n, dst):
                act.wait_ge(s_wst_in, 16 * (n + 1))
                act.nop(nofuse=True)
                nc.scalar.activation(dst, w_stage, ACT.Copy, scale=SW).then_inc(s_wst_hi, 1)

            stage = [wq3_hl, wq3_hl, wk3_hl, wk3_hl, W2HL, W2HL]

            def w1_hi(t):
                act.wait_ge(s_prod_mm, T + t + 1)
                act.nop(nofuse=True)
                nc.scalar.activation(part_row(VHL, 0, t), PS[:, ds(t % 2, 1), :].rearrange("p a n -> p (a n)"),
                                     ACT.Copy, scale=one(dinv_half, t)).then_inc(s_w1_hi, 1)

            for n in range(6):
                stage_hi(n, stage[n][:, 0, 2 * (n % 2):2 * (n % 2) + 2, :])
                w1_hi(n)
            with act.Fori(6, T) as t:
                w1_hi(t)
            act.wait_ge(s_wv_in, 16)
            nc.scalar.activation(wv_hl[:, 0], wv_f, ACT.Copy, scale=SW).then_inc(s_wv_hi, 1)
            for d in range(C):
                act.wait_ge(s_g_mm, d + 1)
                nc.scalar.activation(GHL[:, 0, d, :], PS[:, 2 + d % 2, :], ACT.Copy, scale=1.0 / SW).then_inc(s_g_hi, 1)
            act.wait_ge(s_vec_mm, 1)
            nc.scalar.activation(a_row, PS[:, 4, :], ACT.Copy, scale=SX * SW / (SB * SW)).then_inc(s_vec_out, 1)
            nc.scalar.activation(c2, PS[:, 5, 0:C], ACT.Copy, scale=1.0 / SB).then_inc(s_vec_out, 1)
            nc.scalar.activation(beta, PS[:, 5, C:C + 1], ACT.Copy, scale=SX * SW / (SB * SB)).then_inc(s_vec_out, 1)
            with act.Fori(0, T) as t:
                act.wait_ge(s_ln_x, T + t + 1)
                act.nop(nofuse=True)
                nc.scalar.activation(part_row(XHL, 0, t), row(X, t), ACT.Copy, scale=SX).then_inc(s_x_hi, 1)
            act.sem_inc(s_xt_out, 2)

            def xt_out(t, before):
                act.wait_ge(s_xt_mm, before + t + 1)
                nc.scalar.copy(XT[:, :, :, ds(t * P, P)],
                               PS16[:, ds(2048 + (t % 2) * 1024, 1024)].rearrange("p (h c n) -> p h c n", h=2, c=C))\
                    .then_inc(s_xt_out, 1)

            with act.Fori(0, T) as t:
                xt_out(t, T)
            with act.Fori(0, T) as t:
                act.wait_ge(s_rows_mm, t + 1)
                act.nop(nofuse=True)
                nc.scalar.activation(part_row(VHL, 0, t), PS[:, ds(4 + t % 2, 1), :].rearrange("p a n -> p (a n)"),
                                     ACT.Copy, scale=1.0 / SX).then_inc(s_rows_hi, 1)
            with act.Fori(0, T) as t:
                act.wait_ge(s_ln_x, 2 * T + t + 1)
                act.nop(nofuse=True)
                nc.scalar.activation(part_row(XHL, 0, t), row(X, t), ACT.Copy, scale=SX).then_inc(s_x_hi, 1)
            act.sem_inc(s_xt_out, 2)
            with act.Fori(0, T) as t:
                xt_out(t, 2 * T)
            act.sem_inc(s_qf_ready, G)
            with act.Fori(0, C) as m:
                for n in range(G):
                    act.wait_ge(s_qt_mm, G * m + n + 1)
                    act.wait_ge(s_qt_done, G * m + n + 1)
                    act.nop(nofuse=True)
                    nc.scalar.activation(qf[:, n, :], PS[:, 4 + n, 0:GW], ACT.Identity, bias=one(c2, m),
                                         scale=1.0 / SX).then_inc(s_qf_ready, 1)
            with act.Fori(0, T) as t:
                act.wait_ge(s_rows_mm, T + t + 1)
                act.nop(nofuse=True)
                nc.scalar.activation(part_row(VHL, 0, t), PS[:, ds(t % 2, 1), :].rearrange("p a n -> p (a n)"),
                                     ACT.Copy, scale=1.0 / SX).then_inc(s_rows_hi, 1)

            def soft(t):
                act.wait_ge(s_nm3_ready, t + 1)
                act.nop(nofuse=True)
                nc.scalar.activation(zero_fill[:, 0:N], score[:, 0:N], ACT.Exp, bias=nm3, scale=Z_SCALE,
                                     accum_out=z3).then_inc(s_p3_ready, 1)
                act.wait_ge(s_p3_ready, t + 1)
                if not isinstance(t, int) or t > 0:
                    act.wait_ge(s_pt_mm, 2 * t)
                    act.nop(nofuse=True)
                nc.scalar.activation(prob_hl[:, 0, 0:N], zero_fill[:, 0:N], ACT.Copy, scale=SP_).then_inc(s_ph_ready, 1)

            def turn(t):
                act.wait_ge(s_pt_mm, 2 * t + 1)
                if not isinstance(t, int) or t > 0:
                    act.wait_ge(s_o_mm, t)
                nc.scalar.copy(prob_t[:, 0], PS16[:, 3072:3072 + NP].rearrange("p (a n) -> p a n", n=P))\
                    .then_inc(s_pt_hi, 1)

            soft(0)
            soft(1)
            turn(0)
            with act.Fori(2, T) as t:
                soft(t)
                turn(t - 1)
            turn(T - 1)

        @block.vector
        def _(dve):
            dve.sem_inc(s_w0_out, 2)
            dve.sem_inc(s_kt_done, G)
            dve.sem_inc(s_at_v, 1)
            dve.sem_inc(s_put_done, 2)
            dve.wait_ge(s_rel_in, 16)
            rel_v = rel[:, :].rearrange("p (i two) -> p two i", two=2)
            nc.vector.tensor_copy(subf[:, :], rel_v[:, 0]).then_inc(s_step, 1)
            nc.vector.tensor_copy(objf[:, :], rel_v[:, 1]).then_inc(s_step, 1)
            dve.wait_ge(s_step, 2)
            nc.vector.tensor_scalar(bad[:, :], subf[:, :], float(N), None, ALU.is_ge).then_inc(s_step, 1)
            nc.vector.tensor_tensor(hit[:, :], subf[:, :], objf[:, :], ALU.is_equal).then_inc(s_step, 1)
            nc.vector.tensor_scalar(pair[:, :, 0], subf[:, :], 1.0, None, ALU.add).then_inc(s_step, 1)
            nc.vector.tensor_scalar(pair[:, :, 1], objf[:, :], 1.0, None, ALU.add).then_inc(s_step, 1)
            dve.wait_ge(s_step, 6)
            nc.vector.scalar_tensor_tensor(out=bad[:, :], in0=objf[:, :], scalar=float(N), in1=bad[:, :],
                                           op0=ALU.is_ge, op1=ALU.add).then_inc(s_step, 1)
            dve.wait_ge(s_step, 7)
            nc.vector.tensor_tensor(bad[:, :], bad[:, :], hit[:, :], ALU.add).then_inc(s_step, 1)
            dve.wait_ge(s_step, 8)
            nc.vector.scalar_tensor_tensor(out=hit[:, :], in0=subf[:, :], scalar=float(N), in1=objf[:, :],
                                           op0=ALU.mult, op1=ALU.add).then_inc(s_step, 1)
            dve.wait_ge(s_step, 9)
            nc.vector.scalar_tensor_tensor(out=rel_ix[:, :], in0=bad[:, :], scalar=FAR, in1=hit[:, :],
                                           op0=ALU.mult, op1=ALU.add).then_inc(s_step, 1)
            dve.wait_ge(s_step, 10)
            nc.vector.memset(hit[:, :], 0.0).then_inc(s_ix_ready, 1)
            dve.wait_ge(s_b_in, 64)
            nc.vector.tensor_scalar(bk0, bk0, SK, None, ALU.mult).then_inc(s_bias0, 1)
            nc.vector.tensor_scalar(bq0, bq0, SK, None, ALU.mult).then_inc(s_bias0, 1)
            with dve.Fori(0, T) as t:
                dve.wait_ge(s_x_hi, t + 1)
                nc.vector.scalar_tensor_tensor(out=part_row(UHL, 1, t), in0=row(X, t), scalar=SX,
                                               in1=part_row(UHL, 0, t), op0=ALU.mult, op1=ALU.subtract)\
                    .then_inc(s_x_lo, 1)
            for n, (full, hl) in enumerate(((wk0_f, w0_hl), (wq0_f, w0q_hl))):
                dve.wait_ge(s_w0_hi, n + 1)
                nc.vector.scalar_tensor_tensor(out=flat(hl[:, 1]), in0=flat(full), scalar=SW0, in1=flat(hl[:, 0]),
                                               op0=ALU.mult, op1=ALU.subtract).then_inc(s_w0_lo, 1)

            def weights_out(n, dst, m):
                dve.wait_ge(s_w0_mm, n + 1)
                nc.vector.tensor_copy(dst[:, :, :, m * P:(m + 1) * P],
                                      PS16[:, 4096 + (n % 2) * 1024:4096 + (n % 2) * 1024 + 1024]
                                      .rearrange("p (h c n) -> p h c n", h=2, c=C)).then_inc(s_w0_out, 1)

            for m in range(C):
                weights_out(m, WKT, m)
            with dve.Fori(0, C) as m:
                for n in range(G):
                    dve.wait_ge(s_kf_ready, G * m + n + 1 + G)
                    k_at = [KT[:, i, ds(m, 1), n * GW:(n + 1) * GW].rearrange("p a n -> p (a n)") for i in range(2)]
                    nc.vector.tensor_copy(k_at[0], kf[:, n, :]).then_inc(s_kh_done, 1)
                    dve.wait_ge(s_kh_done, G * m + n + 1)
                    nc.vector.tensor_tensor(k_at[1], kf[:, n, :], k_at[0], ALU.subtract).then_inc(s_kt_done, 1)
            for m in range(C):
                weights_out(C + m, WQT, m)
            with dve.Fori(0, (T + 1) // 2) as j:
                dve.wait_ge(s_at_mm, 2 * j + 1)
                nc.vector.tensor_copy(AT[:, :, ds(j * 2 * P, P)],
                                      PS16[:, 0:NP].rearrange("p (a n) -> p a n", n=P)).then_inc(s_at_v, 1)
            dve.wait_ge(s_sums_mm, 1)
            nc.vector.tensor_copy(row_n, PS[:, 2, 0:T]).then_inc(s_step, 1)
            nc.vector.tensor_copy(col_n, PS[:, 3, 0:T]).then_inc(s_step, 1)
            dve.wait_ge(s_step, 12)
            nc.vector.tensor_tensor(dinv, row_n, col_n, ALU.add).then_inc(s_step, 1)
            nc.vector.tensor_scalar(c_b, row_n, E_DIAG, DIAG, ALU.mult, ALU.add).then_inc(s_step, 1)
            dve.wait_ge(s_step, 14)
            nc.vector.tensor_scalar(dinv, dinv, 0.5, 1.0, ALU.mult, ALU.add).then_inc(s_deg_ready, 1)
            nc.vector.reciprocal(c_b, c_b).then_inc(s_step, 1)
            dve.wait_ge(s_step, 15)
            nc.vector.tensor_scalar(c_a, c_b, E_DIAG, None, ALU.mult).then_inc(s_step, 1)
            dve.wait_ge(s_step, 16)
            nc.vector.tensor_scalar(c_b, c_b, SX * DIAG, None, ALU.mult).then_inc(s_closed_ready, 1)
            dve.wait_ge(s_closed_ready, 1)
            with dve.Fori(0, T) as t:
                dve.wait_ge(s_base_scaled, t + 3)
                nc.vector.scalar_tensor_tensor(out=row(BASE, t), in0=row(X, t), scalar=one(c_b, t), in1=row(BASE, t),
                                               op0=ALU.mult, op1=ALU.add).then_inc(s_base_done, 1)
            dve.wait_ge(s_dinv_ready, 1)
            nc.vector.tensor_scalar(dinv_half, dinv, 0.5, None, ALU.mult).then_inc(s_dinv_s_ready, 1)
            nc.vector.tensor_scalar(dinv_s, dinv, SX, None, ALU.mult).then_inc(s_dinv_s_ready, 1)
            dve.wait_ge(s_hit_in, 16 * EC)
            dve.wait_ge(s_const, 7)
            nc.vector.tensor_scalar(act16[:, :], hit[:, :], 1.0, None, ALU.is_equal).then_inc(s_act_ready, 1)
            dve.wait_ge(s_act_ready, 1)
            nc.vector.tensor_scalar(bad[:, :], act16[:, :], -20000.0, 20000.0, ALU.mult, ALU.add)\
                .then_inc(s_step, 1)
            dve.wait_ge(s_tot_mm, 1)
            nc.vector.tensor_copy(tot16[:, :], PS[0:EC, 1, 0:P]).then_inc(s_tot_ready, 1)
            dve.wait_ge(s_rank_mm, 1)
            nc.vector.tensor_copy(n_act[:, :], PS[0:1, 2, 0:1]).then_inc(s_n_ready, 1)
            dve.wait_ge(s_step, 17)
            nc.vector.tensor_tensor(rank[:, :], PS[0:EP, 0, 0:EC], bad[:, :], ALU.add).then_inc(s_rank_ready, 1)
            dve.wait_ge(s_rank_ready, 1)
            dve.wait_ge(s_n_ready, 1)
            many = dve.value_load(n_act[0:1, 0:1])

            def attend(r):
                nc.vector.tensor_scalar(dmask, iota[:, :], slot_row, None, ALU.is_equal).then_inc(s_d_ready, 1)
                dve.wait_ge(s_w_mm, r + 1)
                nc.vector.tensor_scalar(wmask.rearrange("p (g n) -> p g n", g=G), PS[:, 2:5, 0:GW], 1.0, 1.0,
                                        ALU.min, ALU.add).then_inc(s_w_step, 1)
                dve.wait_ge(s_w_step, r + 1)
                dve.wait_ge(s_gathered, 32 * r + 32)
                nc.vector.tensor_tensor(wmask, wmask, adj_c, ALU.subtract).then_inc(s_mask_ready, 1)
                nc.vector.tensor_scalar(bmask, adj_c, -1.0, OFF, ALU.add, ALU.mult).then_inc(s_mask_ready, 1)
                dve.wait_ge(s_xc_hi, r + 1)
                nc.vector.scalar_tensor_tensor(out=xc_hl[:, 1], in0=x_c, scalar=SX, in1=xc_hl[:, 0], op0=ALU.mult,
                                               op1=ALU.subtract).then_inc(s_xc_lo, 1)
                dve.wait_ge(s_q_full, C * r + C)
                nc.vector.tensor_copy(flat(q_hl[:, 0]), flat(qf0)).then_inc(s_q_hi, 1)
                dve.wait_ge(s_q_hi, r + 1)
                nc.vector.tensor_tensor(flat(q_hl[:, 1]), flat(qf0), flat(q_hl[:, 0]), ALU.subtract)\
                    .then_inc(s_q_lo, 1)
                dve.wait_ge(s_q_lo, r + 1)
                dve.wait_ge(s_mask_ready, 2 * r + 2)

                def add_head(h):
                    one_h = slice(h, h + 1)
                    dve.wait_ge(s_em_ready, HEADS * r + h + 1)
                    nc.vector.scalar_tensor_tensor(out=zs[:, one_h], in0=em[:, one_h], scalar=DIAG, in1=zs[:, one_h],
                                                   op0=ALU.mult, op1=ALU.add).then_inc(s_z_ready, 1)
                    dve.wait_ge(s_z_ready, HEADS * r + h + 1)
                    nc.vector.reciprocal(rz[:, one_h], zs[:, one_h]).then_inc(s_rz_ready, 1)
                    dve.wait_ge(s_rz_ready, HEADS * r + h + 1)
                    if h == 0:
                        nc.vector.tensor_scalar(fsum, prob[0], rz[:, one_h], None, ALU.mult).then_inc(s_f_step, 1)
                    else:
                        dve.wait_ge(s_f_step, HEADS * r + h)
                        nc.vector.scalar_tensor_tensor(out=fsum, in0=prob[h % 3], scalar=rz[:, one_h], in1=fsum,
                                                       op0=ALU.mult, op1=ALU.add).then_inc(s_f_step, 1)

                for h in range(HEADS):
                    b = 2 + G * (h % 2)
                    dve.wait_ge(s_s_mm, HEADS * r + h + 1)
                    if h >= 3:
                        dve.wait_ge(s_f_step, HEADS * r + h - 2)
                    dve.nop(nofuse=True)
                    nc.vector.tensor_tensor_reduce(
                        out=prob[h % 3].rearrange("p (g n) -> p g n", g=G), in0=PS[:, b:b + G, 0:GW],
                        in1=wmask.rearrange("p (g n) -> p g n", g=G), scale=1.0, scalar=-3.0e38, op0=ALU.mult,
                        op1=ALU.max, accum_out=mx[:, h:h + 1]).then_inc(s_t_ready, 1)
                    dve.wait_ge(s_t_ready, HEADS * r + h + 1)
                    nc.vector.tensor_scalar(nb[:, h:h + 1], mx[:, h:h + 1], -1.0 / (SK * SK * 8.0), -DIAG, ALU.mult,
                                            ALU.min).then_inc(s_nb_ready, 1)
                    if h >= 1:
                        add_head(h - 1)
                add_head(HEADS - 1)
                dve.wait_ge(s_f_step, HEADS * r + HEADS)
                nc.vector.memset(f_hl[:, :, NG:NP], 0.0).then_inc(s_f_pad, 1)
                nc.vector.tensor_tensor(g_tmp, em, rz, ALU.mult).then_inc(s_g_step, 1)
                dve.wait_ge(s_g_step, 3 * r + 1)
                nc.vector.reduce_sum(g_sum, g_tmp, mybir.AxisListType.X).then_inc(s_g_step, 1)
                dve.wait_ge(s_g_step, 3 * r + 2)
                nc.vector.tensor_scalar(g_sum, g_sum, DIAG, None, ALU.mult).then_inc(s_g_step, 1)
                dve.wait_ge(s_g_step, 3 * r + 3)
                dve.wait_ge(s_d_ready, r + 1)
                nc.vector.scalar_tensor_tensor(out=fsum, in0=dmask[:, 0:NG], scalar=g_sum, in1=fsum, op0=ALU.mult,
                                               op1=ALU.add).then_inc(s_f_done, 1)
                dve.wait_ge(s_f_hi, r + 1)
                nc.vector.scalar_tensor_tensor(out=f_hl[:, 1, 0:NG], in0=fsum, scalar=SP_ / HEADS, in1=f_hl[:, 0, 0:NG],
                                               op0=ALU.mult, op1=ALU.subtract).then_inc(s_f_lo, 1)
                dve.wait_ge(s_ft_mm, 2 * r + 2)
                nc.vector.tensor_copy(f_t[:, 1], PS16[:, 4096:4096 + NP].rearrange("p (a n) -> p a n", n=P))\
                    .then_inc(s_ft_lo, 1)
                dve.wait_ge(s_y_mm, r + 1)

            with dve.If(many > P):
                nc.vector.tensor_scalar(bad[:, :], act16[:, :], 5000.0, -5000.0, ALU.mult, ALU.add)\
                    .then_inc(s_all_step, 1)
                nc.vector.tensor_copy(slot_row, row_id).then_inc(s_all_step, 1)
                dve.wait_ge(s_all_step, 2)
                nc.vector.tensor_tensor(subf[:, :], subf[:, :], bad[:, :], ALU.add).then_inc(s_all_step, 1)
                dve.wait_ge(s_all_step, 3)
                dve.wait_ge(s_base_done, T)
                with dve.Fori(0, T) as t:
                    nc.vector.tensor_scalar(slot_far, slot_row, 0.0, FAR, ALU.is_lt, ALU.mult)\
                        .then_inc(s_slot_step, 1)
                    dve.wait_ge(s_slot_step, t + 1)
                    nc.vector.tensor_tensor(slot_ix[:, :], slot_far, slot_row, ALU.add).then_inc(s_slots_ready, 1)
                    with dve.Fori(0, EC // 2) as j:
                        for i in range(2):
                            dve.wait_ge(s_hots_free, t * EC + j * 2 + i + 1)
                            nc.vector.tensor_scalar(all_sub[i][0:EP, :], iota[0:EP, 0:P], one(subf, j * 2 + i), None,
                                                    ALU.is_equal).then_inc(s_hots_sub, 1)
                            nc.vector.tensor_scalar(all_obj[i][0:EP, :], iota[0:EP, 0:NG], one(objf, j * 2 + i), None,
                                                    ALU.is_equal).then_inc(s_hots_obj, 1)
                    attend(t)
                    nc.vector.tensor_scalar(row(BASE, t), PS[:, 0, :], 1.0 / SP_, None, ALU.mult)\
                        .then_inc(s_put_done, 1)
                    nc.vector.tensor_scalar(slot_row, slot_row, float(P), None, ALU.add).then_inc(s_all_step, 1)
                    nc.vector.tensor_scalar(subf[:, :], subf[:, :], float(-P), None, ALU.add).then_inc(s_all_step, 1)
                    dve.wait_ge(s_all_step, 2 * t + 5)
                    dve.wait_ge(s_put_done, t + 3)
            with dve.Else():
                for k in range(EC // OC):
                    if k >= 2:
                        dve.wait_ge(s_slots_mm, k - 1)
                    nc.vector.tensor_tensor(
                        hot[k % 2][0:EP], rank[:, k * OC:(k + 1) * OC].unsqueeze(2).to_broadcast([EP, OC, P]),
                        iota[0:EP, 0:P].unsqueeze(1).to_broadcast([EP, OC, P]), ALU.is_equal).then_inc(s_hot_ready, 1)
                dve.wait_ge(s_slots_mm, EC // OC)
                nc.vector.tensor_scalar(slot_row, PS[:, 5, 0:1], -1.0, None, ALU.add).then_inc(s_slot_step, 1)
                nc.vector.tensor_scalar(slot_obj, PS[:, 5, 1:2], -1.0, None, ALU.add).then_inc(s_slot_step, 1)
                dve.wait_ge(s_slot_step, 2)
                nc.vector.tensor_scalar(slot_far, slot_row, 0.0, FAR, ALU.is_lt, ALU.mult).then_inc(s_slot_step, 1)
                nc.vector.tensor_scalar(sub_b, ones[:, :], slot_row, None, ALU.mult).then_inc(s_sub_ready, 1)
                nc.vector.tensor_scalar(obj_hot, iota[:, 0:NG], slot_obj, None, ALU.is_equal).then_inc(s_obj_ready, 1)
                nc.vector.tensor_scalar(slot_low, slot_row, 0.0, None, ALU.is_ge).then_inc(s_slot_step, 1)
                dve.wait_ge(s_slot_step, 4)
                nc.vector.tensor_tensor(slot_ix[:, :], slot_far, slot_row, ALU.add).then_inc(s_slots_ready, 1)
                dve.wait_ge(s_sub_mm, 1)
                nc.vector.tensor_scalar(same, PS[:, 6, 0:P], slot_row, slot_low, ALU.is_equal, ALU.mult)\
                    .then_inc(s_same_ready, 1)
                dve.wait_ge(s_same_ready, 1)
                nc.vector.tensor_tensor_reduce(out=sub_b, in0=same, in1=after[:, :], scale=1.0, scalar=0.0,
                                               op0=ALU.mult, op1=ALU.add, accum_out=rep).then_inc(s_slot_step, 1)
                dve.wait_ge(s_slot_step, 5)
                nc.vector.tensor_scalar(rep, rep, 0.0, slot_low, ALU.is_equal, ALU.mult).then_inc(s_rep_ready, 1)
                attend(0)
                dve.wait_ge(s_y_hi, 1)
                nc.vector.scalar_tensor_tensor(out=y_hl[:, 1], in0=PS[:, 0, :], scalar=1.0 / SP_, in1=y_hl[:, 0],
                                               op0=ALU.mult, op1=ALU.subtract).then_inc(s_y_lo, 1)
                dve.wait_ge(s_rep_ready, 1)
                dve.wait_ge(s_f_done, 1)
                nc.vector.tensor_scalar(dmask, dmask, rep, None, ALU.mult).then_inc(s_put_ready, 1)
                dve.wait_ge(s_has_mm, 1)
                nc.vector.tensor_scalar(nohas, PS[:, 1, 0:T], -1.0, 1.0, ALU.mult, ALU.add).then_inc(s_has_ready, 1)
                dve.wait_ge(s_has_ready, 1)
                dve.wait_ge(s_base_done, T)
                with dve.Fori(0, T) as t:
                    dve.wait_ge(s_put_mm, t + 1)
                    nc.vector.scalar_tensor_tensor(
                        out=row(BASE, t), in0=row(BASE, t), scalar=one(nohas, t),
                        in1=PS[:, ds(2 + t % 2, 1), :].rearrange("p a n -> p (a n)"), op0=ALU.mult, op1=ALU.add)\
                        .then_inc(s_put_done, 1)
            dve.wait_ge(s_put_done, T + 2)
            nc.vector.memset(ln_mv, 0.0).then_inc(s_all_done, 1)

            def norm(n, x_t):
                dve.wait_ge(s_ln_r, n + 1)
                dve.nop(nofuse=True)
                nc.vector.bn_stats(ln_st, x_t).then_inc(s_ln_s, 1)
                dve.wait_ge(s_ln_s, n + 1)
                dve.nop(nofuse=True)
                nc.vector.bn_aggr(ln_mv, ln_st).then_inc(s_ln_m, 1)
                dve.wait_ge(s_ln_m, n + 1)
                nc.vector.tensor_scalar(ln_var, ln_mv[:, 1:2], EPS, None, ALU.add).then_inc(s_ln_v, 1)
                dve.wait_ge(s_ln_rstd, n + 1)
                return nc.vector.tensor_scalar(x_t, x_t, ln_mv[:, 0:1], ln_rstd, ALU.subtract, ALU.mult)

            dve.wait_ge(s_dinv_s_ready, 2)
            dve.wait_ge(s_all_done, 1)
            with dve.Fori(0, T) as t:
                nc.vector.scalar_tensor_tensor(out=row(X, t), in0=row(BASE, t), scalar=1.0 / SX, in1=row(X, t),
                                               op0=ALU.mult, op1=ALU.add).then_inc(s_ln_r, 1)
                norm(t, row(X, t)).then_inc(s_ln_x, 1)
                dve.wait_ge(s_u_hi, t + 1)
                nc.vector.scalar_tensor_tensor(out=part_row(UHL, 1, t), in0=row(X, t), scalar=one(dinv_s, t),
                                               in1=part_row(UHL, 0, t), op0=ALU.mult, op1=ALU.subtract)\
                    .then_inc(s_u_lo, 1)
            stage = [wq3_hl, wq3_hl, wk3_hl, wk3_hl, W2HL, W2HL]

            def w1_lo(t):
                dve.wait_ge(s_w1_hi, t + 1)
                nc.vector.scalar_tensor_tensor(
                    out=part_row(VHL, 1, t), in0=PS[:, ds(t % 2, 1), :].rearrange("p a n -> p (a n)"),
                    scalar=one(dinv_half, t), in1=part_row(VHL, 0, t), op0=ALU.mult, op1=ALU.subtract)\
                    .then_inc(s_w1_lo, 1)

            dve.sem_inc(s_w1_lo, 2)
            for n in range(6):
                at = slice(2 * (n % 2), 2 * (n % 2) + 2)
                dve.wait_ge(s_wst_hi, n + 1)
                nc.vector.scalar_tensor_tensor(out=flat(stage[n][:, 1, at, :]), in0=flat(w_stage), scalar=SW,
                                               in1=flat(stage[n][:, 0, at, :]), op0=ALU.mult, op1=ALU.subtract)\
                    .then_inc(s_wst_lo, 1)
                w1_lo(n)
            with dve.Fori(6, T) as t:
                w1_lo(t)
            nc.vector.tensor_scalar(b_hl[:, 0, 0:C], bk3, SB, None, ALU.mult).then_inc(s_step, 1)
            nc.vector.tensor_scalar(b_hl[:, 0, C:2 * C], bq3, SB, None, ALU.mult).then_inc(s_step, 1)
            dve.wait_ge(s_step, 19)
            nc.vector.scalar_tensor_tensor(out=b_hl[:, 1, 0:C], in0=bk3, scalar=SB, in1=b_hl[:, 0, 0:C], op0=ALU.mult,
                                           op1=ALU.subtract).then_inc(s_step, 1)
            nc.vector.scalar_tensor_tensor(out=b_hl[:, 1, C:2 * C], in0=bq3, scalar=SB, in1=b_hl[:, 0, C:2 * C],
                                           op0=ALU.mult, op1=ALU.subtract).then_inc(s_step, 1)
            dve.wait_ge(s_step, 21)
            for i in range(2):
                for m in range(C):
                    nc.vector.tensor_scalar(bk_b[:, i, m, :], ones[:, :], b_hl[:, i, m:m + 1], None, ALU.mult)\
                        .then_inc(s_bkb_ready, 1)
            dve.wait_ge(s_wv_hi, 1)
            nc.vector.scalar_tensor_tensor(out=flat(wv_hl[:, 1]), in0=flat(wv_f), scalar=SW, in1=flat(wv_hl[:, 0]),
                                           op0=ALU.mult, op1=ALU.subtract).then_inc(s_wv_lo, 1)
            for d in range(C):
                dve.wait_ge(s_g_hi, d + 1)
                nc.vector.scalar_tensor_tensor(out=GHL[:, 1, d, :], in0=PS[:, 2 + d % 2, :], scalar=1.0 / SW,
                                               in1=GHL[:, 0, d, :], op0=ALU.mult, op1=ALU.subtract)\
                    .then_inc(s_g_lo, 1)
            for m in range(C):
                dve.wait_ge(s_wvt_mm, m + 1)
                nc.vector.tensor_copy(WVT[:, :, :, m * P:(m + 1) * P],
                                      PS16[:, 6144 + (m % 2) * 1024:6144 + (m % 2) * 1024 + 1024]
                                      .rearrange("p (h c n) -> p h c n", h=2, c=C)).then_inc(s_wvt_out, 1)

            def add_rows(t, before, scale):
                dve.wait_ge(s_prod_mm, before + t + 1)
                return nc.vector.scalar_tensor_tensor(
                    out=row(X, t), in0=PS[:, ds(t % 2, 1), :].rearrange("p a n -> p (a n)"), scalar=scale,
                    in1=row(X, t), op0=ALU.mult, op1=ALU.add)

            def x_low(t, before):
                dve.wait_ge(s_x_hi, before + t + 1)
                nc.vector.scalar_tensor_tensor(out=part_row(XHL, 1, t), in0=row(X, t), scalar=SX,
                                               in1=part_row(XHL, 0, t), op0=ALU.mult, op1=ALU.subtract)\
                    .then_inc(s_x_lo, 1)

            dve.wait_ge(s_ln_x, T)
            with dve.Fori(0, T) as t:
                add_rows(t, 2 * T, 1.0 / SX).then_inc(s_ln_r, 1)
                norm(T + t, row(X, t)).then_inc(s_ln_x, 1)
                x_low(t, T)
            dve.sem_inc(s_rows_lo, 2)
            with dve.Fori(0, T) as t:
                dve.wait_ge(s_rows_hi, t + 1)
                nc.vector.scalar_tensor_tensor(
                    out=part_row(VHL, 1, t), in0=PS[:, ds(4 + t % 2, 1), :].rearrange("p a n -> p (a n)"),
                    scalar=1.0 / SX, in1=part_row(VHL, 0, t), op0=ALU.mult, op1=ALU.subtract).then_inc(s_rows_lo, 1)
            dve.wait_ge(s_b3_in, 32)
            with dve.Fori(0, T) as t:
                dve.wait_ge(s_ln_x, T + t + 1)
                nc.vector.tensor_tensor(row(X, t), row(X, t), b2_row, ALU.add).then_inc(s_x3_add, 1)
                dve.wait_ge(s_x3_add, t + 1)
                add_rows(t, 3 * T, 1.0 / SW).then_inc(s_ln_r, 1)
                norm(2 * T + t, row(X, t)).then_inc(s_ln_x, 1)
                x_low(t, 2 * T)
            dve.sem_inc(s_qt_done, G)
            with dve.Fori(0, C) as m:
                for n in range(G):
                    dve.wait_ge(s_qf_ready, G * m + n + 1 + G)
                    q_at = [QT[:, i, ds(m, 1), n * GW:(n + 1) * GW].rearrange("p a n -> p (a n)") for i in range(2)]
                    nc.vector.tensor_copy(q_at[0], qf[:, n, :]).then_inc(s_qh_done, 1)
                    dve.wait_ge(s_qh_done, G * m + n + 1)
                    nc.vector.tensor_tensor(q_at[1], qf[:, n, :], q_at[0], ALU.subtract).then_inc(s_qt_done, 1)
            dve.sem_inc(s_rows_lo, 2)
            with dve.Fori(0, T) as t:
                dve.wait_ge(s_rows_hi, T + t + 1)
                nc.vector.scalar_tensor_tensor(
                    out=part_row(VHL, 1, t), in0=PS[:, ds(t % 2, 1), :].rearrange("p a n -> p (a n)"),
                    scalar=1.0 / SX, in1=part_row(VHL, 0, t), op0=ALU.mult, op1=ALU.subtract).then_inc(s_rows_lo, 1)
            dve.wait_ge(s_vec_out, 3)
            nc.vector.memset(QT[:, :, :, NG:NP], 0.0).then_inc(s_pad3, 1)
            nc.vector.memset(prob_hl[:, :, N:NP], 0.0).then_inc(s_pad3, 1)
            dve.sem_inc(s_t3_ready, 1)

            def scores(t):
                dve.wait_ge(s_ln_x, 2 * T + t + 1)
                nc.vector.scalar_tensor_tensor(out=out_t, in0=row(X, t), scalar=1.0, in1=a_row, op0=ALU.mult,
                                               op1=ALU.mult, accum_out=r_acc).then_inc(s_r_step, 1)
                dve.wait_ge(s_r_step, t + 1)
                nc.vector.tensor_tensor(r3, r_acc, beta, ALU.add).then_inc(s_r_ready, 1)
                dve.wait_ge(s_r_ready, t + 1)
                dve.wait_ge(s_z_mm, t + 1)
                nc.vector.scalar_tensor_tensor(
                    out=score.rearrange("p (g n) -> p g n", g=G), in0=PS[:, 0:G, 0:GW], scalar=r3,
                    in1=A[:, ds(t, 1), 0:NG].rearrange("p a (g n) -> p (a g) n", g=G), op0=ALU.add, op1=ALU.mult)\
                    .then_inc(s_t3_ready, 1)
                dve.wait_ge(s_t3_ready, t + 2)
                nc.vector.tensor_scalar(zero_fill[:, 0:N], score[:, 0:N], 0.0, FILL / Z_SCALE, ALU.is_equal, ALU.mult)\
                    .then_inc(s_nz_ready, 1)
                dve.wait_ge(s_nz_ready, t + 1)
                dve.nop(nofuse=True)
                nc.vector.tensor_tensor_reduce(out=score[:, 0:N], in0=score[:, 0:N], in1=zero_fill[:, 0:N], scale=1.0,
                                               scalar=-3.0e38, op0=ALU.add, op1=ALU.max, accum_out=m3)\
                    .then_inc(s_m3_ready, 1)
                dve.wait_ge(s_m3_ready, t + 1)
                nc.vector.tensor_scalar(nm3, m3, -Z_SCALE, None, ALU.mult).then_inc(s_nm3_ready, 1)

            def prob_low(t):
                dve.wait_ge(s_ph_ready, t + 1)
                nc.vector.scalar_tensor_tensor(out=prob_hl[:, 1, 0:N], in0=zero_fill[:, 0:N], scalar=SP_,
                                               in1=prob_hl[:, 0, 0:N], op0=ALU.mult, op1=ALU.subtract)\
                    .then_inc(s_pl_ready, 1)
                nc.vector.reciprocal(one(rz_all, t), z3).then_inc(s_rz3_step, 1)
                dve.wait_ge(s_rz3_step, t + 1)
                nc.vector.tensor_scalar(one(rz_all, t), one(rz_all, t), 1.0 / (SP_ * SW), None, ALU.mult)\
                    .then_inc(s_rz3_ready, 1)

            def turn(t):
                dve.wait_ge(s_pt_mm, 2 * t + 2)
                nc.vector.tensor_copy(prob_t[:, 1], PS16[:, 5120:5120 + NP].rearrange("p (a n) -> p a n", n=P))\
                    .then_inc(s_pt_lo, 1)

            def finish(t):
                dve.wait_ge(s_o_mm, t + 1)
                dve.wait_ge(s_rz3_ready, t + 1)
                nc.vector.scalar_tensor_tensor(out=out_t, in0=PS[:, 7, :], scalar=one(rz_all, t), in1=bv_row,
                                               op0=ALU.mult, op1=ALU.add).then_inc(s_o_ready, 1)
                dve.wait_ge(s_o_ready, t + 1)
                nc.vector.scalar_tensor_tensor(out=row(X, t), in0=out_t, scalar=0.0, in1=row(X, t), op0=ALU.max,
                                               op1=ALU.add).then_inc(s_ln_r, 1)
                norm(3 * T + t, row(X, t)).then_inc(s_o_norm, 1)

            scores(0)
            prob_low(0)
            scores(1)
            prob_low(1)
            turn(0)
            with dve.Fori(2, T) as t:
                scores(t)
                prob_low(t)
                finish(t - 2)
                turn(t - 1)
            finish(T - 2)
            turn(T - 1)
            finish(T - 1)

        @block.tensor
        def _(pe):
            def turn_rows(t, at, hl):
                for i in range(2):
                    for c in range(C):
                        last = nc.tensor.transpose(
                            PS16[:, ds(at + (i * C + c) * P, P)],
                            hl[:, i, ds(t, 1), c * P:(c + 1) * P].rearrange("p a n -> p (a n)"), ident[:, :])
                return last

            def turn_weight(hl, m, at):
                for i in range(2):
                    for c in range(C):
                        last = nc.tensor.transpose(PS16[:, at + (i * C + c) * P:at + (i * C + c + 1) * P],
                                                   hl[:, i, m, c * P:(c + 1) * P], ident[:, :])
                return last

            def product(out, lhs, rhs, n):
                for k in range(n):
                    for j, (a, b) in enumerate(PAIRS):
                        last = nc.tensor.matmul(out, lhs(a, k), rhs(b, k), start=(k == 0 and j == 0),
                                                stop=(k == n - 1 and j == len(PAIRS) - 1))
                return last

            def graph_product(out, mat, t, rhs):
                for k in range(T):
                    for i in range(2):
                        last = nc.tensor.matmul(out, mat[:, k, ds(t * P, P)], rhs[:, i, k, :],
                                                start=(k == 0 and i == 0), stop=(k == T - 1 and i == 1))
                return last

            def bank(t, first=0):
                return PS[:, ds(first + t % 2, 1), :].rearrange("p a n -> p (a n)")

            pe.wait_ge(s_ident_ready, 1)
            with pe.Fori(0, T) as t:
                pe.wait_ge(s_x_lo, t + 1)
                pe.wait_ge(s_xt_out, t + 1)
                turn_rows(t, (t % 2) * 1024, UHL).then_inc(s_xt_mm, 1)
            pe.wait_ge(s_w0_lo, 1)
            for m in range(C):
                pe.wait_ge(s_w0_out, m + 1)
                turn_weight(w0_hl, m, 4096 + (m % 2) * 1024).then_inc(s_w0_mm, 1)
            pe.wait_ge(s_w0_out, 2 + C)
            pe.wait_ge(s_xt_out, 2 + T)
            with pe.Fori(0, C) as m:
                for n in range(G):
                    pe.wait_ge(s_kf_ready, G * m + n + 1)
                    product(PS[:, 2 + n, 0:GW], lambda i, c: WKT[:, i, c, ds(m * P, P)],
                            lambda i, c: XT[:, i, c, n * GW:(n + 1) * GW], C).then_inc(s_kp_mm, 1)
            pe.wait_ge(s_w0_lo, 2)
            pe.wait_ge(s_kf_ready, G * C + G)
            for m in range(C):
                pe.wait_ge(s_w0_out, C + m + 1)
                turn_weight(w0q_hl, m, 4096 + (m % 2) * 1024).then_inc(s_w0_mm, 1)
            pe.wait_ge(s_w0_out, 2 + 2 * C)
            pe.wait_ge(s_adj_in, 64)

            def turn_adj(t, at):
                for k in range(T):
                    last = nc.tensor.transpose(PS16[:, at + k * P:at + (k + 1) * P],
                                               A[:, ds(t, 1), k * P:(k + 1) * P].rearrange("p a n -> p (a n)"),
                                               ident[:, :])
                last.then_inc(s_at_mm, 1)

            with pe.Fori(0, T // 2) as j:
                pe.wait_ge(s_at_v, j + 1)
                turn_adj(j * 2, 0)
                pe.wait_ge(s_at_a, j + 1)
                turn_adj(j * 2 + 1, 4096)
            pe.wait_ge(s_at_v, T // 2 + 1)
            turn_adj(T - 1, 0)
            pe.wait_ge(s_at_v, 1 + (T + 1) // 2)
            pe.wait_ge(s_at_a, 1 + T // 2)
            for b, mat in ((2, AT), (3, A)):
                for t in range(T):
                    for k in range(T):
                        last = nc.tensor.matmul(PS[:, b, t:t + 1], mat[:, k, t * P:(t + 1) * P], ones[:, 0:1],
                                                start=(k == 0), stop=(k == T - 1))
            last.then_inc(s_sums_mm, 1)
            with pe.Fori(0, T) as t:
                pe.wait_ge(s_base_scaled, t + 1)
                graph_product(bank(t), AT, t, UHL).then_inc(s_prod_mm, 1)
            pe.wait_ge(s_const, 7)
            pe.wait_ge(s_act_ready, 1)
            pe.wait_ge(s_base_scaled, 2 + T)
            nc.tensor.matmul(PS[0:EC, 1, 0:P], act16[:, :], ones[0:EP, :], start=True, stop=True).then_inc(s_tot_mm, 1)
            nc.tensor.matmul(PS[0:EP, 0, 0:EC], before[0:EP, 0:EP], act16[:, :], start=True, stop=False)
            pe.wait_ge(s_tot_ready, 1)
            nc.tensor.matmul(PS[0:EP, 0, 0:EC], tot16[:, 0:EP], before[0:EC, 0:EC], start=False, stop=True)
            nc.tensor.matmul(PS[:, 2, 0:1], tot16[:, :], ones[0:EC, 0:1], start=True, stop=True).then_inc(s_rank_mm, 1)
            pe.wait_ge(s_n_ready, 1)
            many = pe.value_load(n_act[0:1, 0:1])

            def attend(r):
                pe.wait_ge(s_xc_lo, r + 1)
                for i in range(2):
                    for c in range(C):
                        last = nc.tensor.transpose(PS16[:, (i * C + c) * P:(i * C + c + 1) * P],
                                                   xc_hl[:, i, c * P:(c + 1) * P], ident[:, :])
                last.then_inc(s_xct_mm, 1)
                pe.wait_ge(s_xct_out, r + 1)
                for m in range(C):
                    last = product(PS[:, 1, m * P:(m + 1) * P], lambda i, c: WQT[:, i, c, m * P:(m + 1) * P],
                                   lambda i, c: xct[:, i, c, :], C)
                last.then_inc(s_q_mm, 1)
                pe.wait_ge(s_q_lo, r + 1)
                pe.wait_ge(s_mask_ready, 2 * r + 2)
                for h in range(HEADS):
                    lanes = slice(64 * (h % 2), 64 * (h % 2) + 64)
                    if h >= 2:
                        pe.wait_ge(s_t_ready, HEADS * r + h - 1)
                    for n in range(G):
                        out, cols = PS[:, 2 + G * (h % 2) + n, 0:GW], slice(n * GW, (n + 1) * GW)
                        nc.tensor.matmul(out, identb[:, :], bmask[:, cols], start=True, stop=False)
                        for j, (a, b) in enumerate(PAIRS):
                            last = nc.tensor.matmul(out, q_hl[lanes, a, h // 2, :], KT[lanes, b, h // 2, cols],
                                                    start=False, stop=(j == len(PAIRS) - 1))
                    last.then_inc(s_s_mm, 1)
                for i, ready in enumerate((s_f_hi, s_f_lo)):
                    pe.wait_ge(s_f_pad, r + 1)
                    pe.wait_ge(ready, r + 1)
                    for k in range(T):
                        at = 2048 * (i + 1) + k * P
                        last = nc.tensor.transpose(PS16[:, at:at + P], f_hl[:, i, k * P:(k + 1) * P], ident[:, :])
                    last.then_inc(s_ft_mm, 1)
                pe.wait_ge(s_ft_hi, r + 1)
                pe.wait_ge(s_ft_lo, r + 1)
                product(PS[:, 0, :], lambda i, k: f_t[:, i, k, :], lambda i, k: UHL[:, i, k, :], T)\
                    .then_inc(s_y_mm, 1)

            with pe.If(many > P):
                pe.sem_inc(s_hots_free, 2)

                def relations(t, j, first=False, end=False):
                    for i in range(2):
                        pe.wait_ge(s_hots_obj, t * EC + j * 2 + i + 1)
                        for n in range(G):
                            last = nc.tensor.matmul(PS[:, 2 + n, 0:GW], all_sub[i][0:EP, :],
                                                    all_obj[i][0:EP, n * GW:(n + 1) * GW],
                                                    start=(first and i == 0), stop=(end and i == 1))
                        last.then_inc(s_hots_free, 1)
                    if end:
                        return last

                with pe.Fori(0, T) as t:
                    relations(t, 0, first=True)
                    with pe.Fori(1, EC // 2 - 1) as j:
                        relations(t, j)
                    relations(t, EC // 2 - 1, end=True)
                    pe.wait_ge(s_hots_free, (t + 1) * EC + 2)
                    nc.tensor.matmul(PS[:, 5, 0:1], ident[:, :], ones[:, 0:1], start=True, stop=True)\
                        .then_inc(s_w_mm, 1)
                    attend(t)
            with pe.Else():
                for k in range(EC // OC):
                    pe.wait_ge(s_hot_ready, k + 1)
                    for i in range(OC):
                        e = k * OC + i
                        last = nc.tensor.matmul(PS[:, 5, 0:2], hot[k % 2][0:EP, i, :], pair[:, e, :], start=(e == 0),
                                                stop=(e == EC - 1))
                    last.then_inc(s_slots_mm, 1)
                pe.wait_ge(s_sub_ready, 1)
                nc.tensor.matmul(PS[:, 6, 0:P], sub_b, ident[:, :], start=True, stop=True).then_inc(s_sub_mm, 1)
                pe.wait_ge(s_obj_ready, 1)
                pe.wait_ge(s_same_ready, 1)
                for n in range(G):
                    last = nc.tensor.matmul(PS[:, 2 + n, 0:GW], same, obj_hot[:, n * GW:(n + 1) * GW], start=True,
                                            stop=True)
                last.then_inc(s_w_mm, 1)
                attend(0)
                pe.wait_ge(s_put_ready, 1)
                for t in range(T):
                    last = nc.tensor.matmul(PS[:, 1, t:t + 1], dmask[:, t * P:(t + 1) * P], ones[:, 0:1], start=True,
                                            stop=True)
                last.then_inc(s_has_mm, 1)
                pe.wait_ge(s_y_lo, 1)
                with pe.Fori(0, T) as t:
                    pe.wait_ge(s_put_done, t + 1)
                    for i in range(2):
                        last = nc.tensor.matmul(bank(t, 2), dmask[:, ds(t * P, P)], y_hl[:, i, :], start=(i == 0),
                                                stop=(i == 1))
                    last.then_inc(s_put_mm, 1)

            pe.wait_ge(s_u_lo, T)
            with pe.Fori(0, T) as t:
                pe.wait_ge(s_sym_ready, t + 1)
                pe.wait_ge(s_w1_lo, t + 1)
                graph_product(bank(t), SYM, t, UHL).then_inc(s_prod_mm, 1)
            pe.wait_ge(s_wst_lo, 6)
            for d in range(C):
                if d >= 2:
                    pe.wait_ge(s_g_lo, d - 1)
                product(PS[:, 2 + d % 2, :], lambda i, c: wq3_hl[:, i, c, d * P:(d + 1) * P],
                        lambda i, c: wk3_hl[:, i, c, :], C).then_inc(s_g_mm, 1)
            pe.wait_ge(s_bkb_ready, 2 * C)
            product(PS[:, 4, :], lambda i, c: bk_b[:, i, c, :], lambda i, c: wq3_hl[:, i, c, :], C)
            for m in range(C):
                product(PS[:, 5, m:m + 1], lambda i, c: wk3_hl[:, i, c, m * P:(m + 1) * P],
                        lambda i, c: b_hl[:, i, C + c:C + c + 1], C)
            product(PS[:, 5, C:C + 1], lambda i, c: bk_b[:, i, c, :], lambda i, c: b_hl[:, i, C + c:C + c + 1], C)\
                .then_inc(s_vec_mm, 1)
            pe.wait_ge(s_wv_lo, 1)
            for m in range(C):
                if m >= 2:
                    pe.wait_ge(s_wvt_out, m - 1)
                turn_weight(wv_hl, m, 6144 + (m % 2) * 1024).then_inc(s_wvt_mm, 1)
            pe.wait_ge(s_w1_lo, 2 + T)
            with pe.Fori(0, T) as t:
                pe.wait_ge(s_ln_r, t + T - 1)
                graph_product(bank(t), AT, t, VHL).then_inc(s_prod_mm, 1)
            pe.wait_ge(s_g_lo, C)
            pe.wait_ge(s_vec_out, 3)
            with pe.Fori(0, T) as t:
                pe.wait_ge(s_x_lo, T + t + 1)
                pe.wait_ge(s_xt_out, T + 2 + t + 1)
                turn_rows(t, 2048 + (t % 2) * 1024, XHL).then_inc(s_xt_mm, 1)
            pe.wait_ge(s_xt_out, 2 * T + 4)
            with pe.Fori(0, T) as t:
                pe.wait_ge(s_rows_lo, t + 1)
                product(bank(t, 4), lambda i, c: XT[:, i, c, ds(t * P, P)], lambda i, c: W2HL[:, i, c, :], C)\
                    .then_inc(s_rows_mm, 1)
            pe.wait_ge(s_rows_lo, 2 + T)
            with pe.Fori(0, T) as t:
                pe.wait_ge(s_ln_r, t + 2 * T - 1)
                graph_product(bank(t), AT, t, VHL).then_inc(s_prod_mm, 1)
            with pe.Fori(0, T) as t:
                pe.wait_ge(s_x_lo, 2 * T + t + 1)
                pe.wait_ge(s_xt_out, 2 * T + 4 + t + 1)
                turn_rows(t, 2048 + (t % 2) * 1024, XHL).then_inc(s_xt_mm, 1)
            pe.wait_ge(s_xt_out, 3 * T + 6)
            with pe.Fori(0, C) as m:
                for n in range(G):
                    pe.wait_ge(s_qf_ready, G * m + n + 1)
                    product(PS[:, 4 + n, 0:GW], lambda i, c: GHL[:, i, c, ds(m * P, P)],
                            lambda i, c: XT[:, i, c, n * GW:(n + 1) * GW], C).then_inc(s_qt_mm, 1)
            pe.wait_ge(s_wvt_out, C)
            with pe.Fori(0, T) as t:
                pe.wait_ge(s_rows_lo, T + 2 + t + 1)
                product(bank(t), lambda i, c: XT[:, i, c, ds(t * P, P)], lambda i, c: WVT[:, i, c, :], C)\
                    .then_inc(s_rows_mm, 1)
            pe.wait_ge(s_rows_lo, 2 * T + 4)
            pe.wait_ge(s_qt_done, G * C + G)

            def scores(t):
                pe.wait_ge(s_t3_ready, t + 1)
                for n in range(G):
                    last = product(PS[:, n, 0:GW], lambda i, c: QT[:, i, c, ds(t * P, P)],
                                   lambda i, c: XT[:, i, c, n * GW:(n + 1) * GW], C)
                last.then_inc(s_z_mm, 1)

            def turn(t):
                for i, ready, read in ((0, s_ph_ready, s_pt_hi), (1, s_pl_ready, s_pt_lo)):
                    pe.wait_ge(ready, t + 1)
                    if not isinstance(t, int) or t > 0:
                        pe.wait_ge(read, t)
                    for k in range(T):
                        at = 3072 + 2048 * i + k * P
                        last = nc.tensor.transpose(PS16[:, at:at + P], prob_hl[:, i, k * P:(k + 1) * P], ident[:, :])
                    last.then_inc(s_pt_mm, 1)

            def attend3(t):
                pe.wait_ge(s_pt_hi, t + 1)
                pe.wait_ge(s_pt_lo, t + 1)
                if not isinstance(t, int) or t > 0:
                    pe.wait_ge(s_o_ready, t)
                product(PS[:, 7, :], lambda i, k: prob_t[:, i, k, :], lambda i, k: VHL[:, i, k, :], T)\
                    .then_inc(s_o_mm, 1)

            pe.wait_ge(s_pad3, 2)
            scores(0)
            scores(1)
            turn(0)
            with pe.Fori(2, T) as t:
                scores(t)
                turn(t - 1)
                attend3(t - 2)
            attend3(T - 2)
            turn(T - 1)
            attend3(T - 1)



_INS = ["x", "adj", "L0_gnn_rel_pair_index", "L0_gnn_Wq", "L0_gnn_bq", "L0_gnn_Wk", "L0_gnn_bk", "L2_gnn_weight",
        "L2_gnn_bias", "L3_gnn_W_q", "L3_gnn_b_q", "L3_gnn_W_k", "L3_gnn_b_k", "L3_gnn_W_v", "L3_gnn_b_v"]


def kernel(**inputs):
    import numpy as _np
    import concourse.bacc as _bacc
    from concourse import mybir as _mybir
    from concourse.bass_utils import run_bass_kernel_spmd as _run

    nc = _bacc.Bacc("TRN2", target_bir_lowering=False, num_devices=1)
    arrays, args = {}, []
    for name in _INS:
        a = _np.ascontiguousarray(inputs[name])
        arrays[f"in_{name}"] = a
        args.append(nc.dram_tensor(f"in_{name}", a.shape, _mybir.dt.from_np(a.dtype), kind="ExternalInput").ap())
    args.append(nc.dram_tensor("out_0", (N, D), F32, kind="ExternalOutput").ap())
    build(nc, *args)
    r = _run(nc, [arrays], core_ids=[0])
    return r.results[0]["out_0"]
```

```python
from contextlib import ExitStack

import concourse.bass as bass
from concourse import mybir

ALU = mybir.AluOpType
ACT = mybir.ActivationFunctionType
F32 = mybir.dt.float32
F16 = mybir.dt.float16
BF16 = mybir.dt.bfloat16
I32 = mybir.dt.int32
U32 = mybir.dt.uint32
ds = bass.ds

P = 128
N = 1354
D = 512
T = -(-N // P)
NP = T * P
TAIL = N - (T - 1) * P
C = D // P
G = 3
GW = 452
NG = G * GW
HEADS = 8
E = 10000
EP, EC = 125, 80
OC = 16

SX = 256.0
SW0 = 64.0
SK = 16.0
SW = 1024.0
SP_ = 4096.0
SB = 16.0
EPS = 1e-5
DIAG = 1e-7
E_DIAG = 0.9999999
OFF = 1e30
FAR = 8.0e6
FILL = -10000.0
AHEAD = 3
SYM_POOL = 4
W1_AT_ONCE = 6
Z_SCALE = float(D) ** -0.5 / (SX * SW)



def build(nc, x_d, adj_d, rel_d, wq0_d, bq0_d, wk0_d, bk0_d, w2_d, b2_d, wq3_d, bq3_d, wk3_d, bk3_d,
          wv3_d, bv3_d, out_d):
    ctx = ExitStack()
    with ctx:
        def sb(name, shape, dt):
            return ctx.enter_context(nc.sbuf_tensor(name, shape, dt))

        def sem(name):
            return ctx.enter_context(nc.semaphore(name))

        A = sb("A", [P, T, NP], F16)
        AT = sb("AT", [P, T, NP], F16)
        X = sb("X", [P, T, D], F32)
        R1 = sb("R1", [P, T * NP], F16)
        R2 = sb("R2", [P, 2 * T * D], F16)
        R3 = sb("R3", [P, 2 * T * D], F16)
        R4 = sb("R4", [P, 2 * C * NP], F16)
        WA = sb("WA", [P, 2 * C * D], F16)
        WB = sb("WB", [P, 2 * C * D], F16)

        ident = sb("ident", [P, P], F16)
        identb = sb("identb", [P, P], BF16)
        iota = sb("iota", [P, NP], F16)
        before = sb("before", [P, P], F16)
        after = sb("after", [P, P], F16)
        ones = sb("ones", [P, P], F16)
        rel = sb("rel", [EP, 2 * EC], I32)
        subf = sb("subf", [EP, EC], F32)
        objf = sb("objf", [EP, EC], F32)
        bad = sb("bad", [EP, EC], F32)
        rel_ix = sb("rel_ix", [EP, EC], U32)
        hit = sb("hit", [EP, EC], F32)
        act16 = sb("act16", [EP, EC], F16)
        rank = sb("rank", [EP, EC], F16)
        pair = sb("pair", [EP, EC, 2], F16)
        tot16 = sb("tot16", [EC, P], F16)
        n_act = sb("n_act", [1, 1], I32)
        small = sb("small", [P, 256], F32)
        slot_ix = sb("slot_ix", [P, 1], U32)
        b_hl = sb("b_hl", [P, 2, 2 * C], F16)
        ident2 = sb("ident2", [P, P], F16)

        PS = ctx.enter_context(nc.psum_tensor("PS", [P, 8, 512], F32))
        PS16 = PS[:, :, :].rearrange("p b n -> p (b n)").bitcast(F16)

        n_cols = [0]

        def cols(n=1):
            n_cols[0] += n
            return small[:, n_cols[0] - n:n_cols[0]]

        bk0, bq0, bk3, bq3, c2 = (cols(C) for _ in range(5))
        mx, nb, zs, em, rz, g_tmp = (cols(HEADS) for _ in range(6))
        slot_row, slot_obj, slot_far, slot_low, rep, g_sum, row_id = (cols() for _ in range(7))
        beta, r_acc, r3, m3, nm3, z3 = (cols() for _ in range(6))
        row_n, col_n, c_a, c_b, nohas, dinv, dinv_half, dinv_s, mhalfs, rz_all = (cols(T) for _ in range(10))
        ln_st, ln_mv, ln_var, ln_rstd = cols(6), cols(2), cols(), cols()
        mv_all = cols(2 * T).rearrange("p (t two) -> p t two", two=2)
        var_all, rstd_all, rstd_s = (cols(T) for _ in range(3))

        def parts(region, at, *shape):
            n = 1
            for k in shape:
                n *= k
            v = region[:, at:at + n]
            if len(shape) == 2:
                return v.rearrange("p (a b) -> p a b", a=shape[0])
            if len(shape) == 3:
                return v.rearrange("p (a b c) -> p a b c", a=shape[0], b=shape[1])
            return v

        def words(region, at, *shape):
            n = 2
            for k in shape:
                n *= k
            v = region[:, 2 * at:2 * at + n].bitcast(F32)
            if len(shape) == 2:
                return v.rearrange("p (a b) -> p a b", a=shape[0])
            return v

        def flat(v):
            return v.rearrange("p a b -> p (a b)")

        KT = parts(R1, 0, 2, C, NG)
        kf = words(R1, 5424, G, GW)
        bmask = R1[:, 10848:10848 + NG].bitcast(BF16)
        wmask = parts(R1, 12204, NG)
        dmask = parts(R1, 13560, NP)
        SYM = parts(R1, 0, T, NP)
        XHL = R1[:, 0:4 * D].rearrange("p (s h n) -> p s h n", s=2, h=2)
        b2_row = words(R1, 2 * D, D)
        WVT = parts(R1, 2 * T * D, 2, C, D)
        score = words(R1, 0, NG)
        zero_fill = words(R1, NG, NG)
        prob_hl = parts(R1, 4 * NG, 2, NP)
        prob_t = R1[:, 4 * NG + 2 * NP:4 * NG + 6 * NP].rearrange("p (s h n) -> p s h n", s=2, h=2)
        UHL = parts(R2, 0, 2, T, D)
        wv_f = words(R2, 0, C, D)
        wv_hl = parts(R2, 4096, 2, C, D)
        SHL = parts(R2, 0, 2, T, D)
        a_row, bv_row = sb("a_row", [P, D], F32), sb("bv_row", [P, D], F32)
        out_t = words(R2, 0, D)
        wk0_f = words(R3, 0, C, D)
        w0_hl = parts(R3, 4096, 2, C, D)
        BASE = words(R3, 0, T, D)
        VHL = parts(R3, 0, 2, T, D)
        wq0_f = words(AT[:, :, :].rearrange("p a b -> p (a b)"), 0, C, D)
        w0q_hl = parts(AT[:, :, :].rearrange("p a b -> p (a b)"), 4096, 2, C, D)
        XT = parts(R4, 0, 2, C, NP)
        prob = [words(R4, NG * i, NG) for i in range(3)]
        fsum = words(R4, 3 * NG, NG)
        sub_b = parts(R4, 8 * NG, P)
        same = parts(R4, 8 * NG + P, P)
        obj_hot = parts(R4, 0, NG)
        adj_c = prob[1]
        qf0 = words(R4, 0, C, P)
        x_c = words(R4, 2 * NG, D)
        f_hl = parts(R4, 0, 2, NP)
        f_t = parts(R4, 2 * NP, 2, T, P)
        y_f = words(R4, 3 * NG, D)
        all_sub = [sub_b, same]
        all_obj = [parts(R4, 0, NG), parts(R4, NG, NG)]
        wq3_hl = parts(R4, 0, 2, C, D)
        wk3_hl = parts(R4, 4096, 2, C, D)
        w_stage = [words(R4, 4096, 2, D), words(WB, 1024, 2, D)]
        bk_b = parts(R4, 10240, 2, C, P)
        WKT = parts(WA, 0, 2, C, D)
        WQT = parts(WB, 0, 2, C, D)
        hot = [parts(WA, 2048 * i, OC, P) for i in range(2)]
        q_hl = parts(WA, 0, 2, HEADS, P)
        q_lanes = [(slice(64 * i, 64 * i + 64),
                    q_hl[64 * i:64 * i + 64].rearrange("p a (m two) n -> p a m two n", two=2)[:, :, :, i, :])
                   for i in range(2)]
        xc_hl = parts(WA, 2048, 2, D)
        xct = parts(WA, 3072, 2, C, P)
        y_hl = parts(WA, 3072, 2, D)
        put_hot = parts(WB, 0, NP)
        W2HL = parts(WA, 0, 2, C, D)
        GHL = parts(WB, 0, 2, C, D)
        staged = [wq3_hl, wk3_hl, W2HL]
        ATF = AT[:, :, :].rearrange("p a b -> p (a b)")
        QT = parts(ATF, 0, 2, C, NP)
        qf = words(R2, C * D, 2, GW)

        s_rel_in = sem("rel_in")
        s_x_in0 = sem("x_in0")
        s_x_in = sem("x_in")
        s_x_pad = sem("x_pad")
        s_wk0_in = sem("wk0_in")
        s_wq0_in = sem("wq0_in")
        s_b_in = sem("b_in")
        s_all_done = sem("all_done")
        s_wst_lo = sem("wst_lo")
        s_wst_in0 = sem("wst_in0")
        s_wst_in1 = sem("wst_in1")
        s_prod_mm = sem("prod_mm")
        s_wv_in = sem("wv_in")
        s_b3_in = sem("b3_in")
        s_o_norm = sem("o_norm")
        s_stored = sem("stored")
        s_a_pad = sem("a_pad")
        s_adj_in = sem("adj_in")
        s_blank = sem("blank")
        s_ident_ready = sem("ident_ready")
        s_const = sem("const")
        s_ix_ready = sem("ix_ready")
        s_hit_in = sem("hit_in")
        s_deg_ready = sem("deg_ready")
        s_dinv_ready = sem("dinv_ready")
        s_slot_fill = sem("slot_fill")
        s_gathered = sem("gathered")
        s_n_ready = sem("n_ready")
        s_slots_ready = sem("slots_ready")
        s_kp_mm = sem("kp_mm")
        s_ln_v = sem("ln_v")
        s_ln_rstd = sem("ln_rstd")
        s_r1_free = sem("r1_free")
        s_at_v = sem("at_v")
        s_at_a = sem("at_a")
        s_sym_sum = sem("sym_sum")
        s_sym_ready = sem("sym_ready")
        s_wst_hi = sem("wst_hi")
        s_x_hi = sem("x_hi")
        s_w0_hi = sem("w0_hi")
        s_xt_out = sem("xt_out")
        s_xt_mm = sem("xt_mm")
        s_kf_ready = sem("kf_ready")
        s_bias0 = sem("bias0")
        s_kt_done = sem("kt_done")
        s_at_mm = sem("at_mm")
        s_base_scaled = sem("base_scaled")
        s_closed_ready = sem("closed_ready")
        s_xc_hi = sem("xc_hi")
        s_xct_mm = sem("xct_mm")
        s_xct_out = sem("xct_out")
        s_q_mm = sem("q_mm")
        s_q_full = sem("q_full")
        s_nb_ready = sem("nb_ready")
        s_p_ready = sem("p_ready")
        s_em_ready = sem("em_ready")
        s_f_step = sem("f_step")
        s_f_hi = sem("f_hi")
        s_ft_mm = sem("ft_mm")
        s_ft_hi = sem("ft_hi")
        s_y_sum = sem("y_sum")
        s_y_hi = sem("y_hi")
        s_ln_x = sem("ln_x")
        s_u_hi = sem("u_hi")
        s_w1_hi = sem("w1_hi")
        s_wv_hi = sem("wv_hi")
        s_g_mm = sem("g_mm")
        s_g_hi = sem("g_hi")
        s_vec_mm = sem("vec_mm")
        s_vec_out = sem("vec_out")
        s_rows_mm = sem("rows_mm")
        s_rows_hi = sem("rows_hi")
        s_qf_ready = sem("qf_ready")
        s_qt_mm = sem("qt_mm")
        s_qt_done = sem("qt_done")
        s_nm3_ready = sem("nm3_ready")
        s_p3_ready = sem("p3_ready")
        s_pt_mm = sem("pt_mm")
        s_ph_ready = sem("ph_ready")
        s_o_mm = sem("o_mm")
        s_pt_hi = sem("pt_hi")
        s_w0_out = sem("w0_out")
        s_step = sem("step")
        s_x_lo = sem("x_lo")
        s_w0_lo = sem("w0_lo")
        s_w0_mm = sem("w0_mm")
        s_kh_done = sem("kh_done")
        s_sums_mm = sem("sums_mm")
        s_base_done = sem("base_done")
        s_dinv_s_ready = sem("dinv_s_ready")
        s_act_ready = sem("act_ready")
        s_tot_mm = sem("tot_mm")
        s_tot_ready = sem("tot_ready")
        s_rank_mm = sem("rank_mm")
        s_rank_ready = sem("rank_ready")
        s_d_ready = sem("d_ready")
        s_w_mm = sem("w_mm")
        s_w_step = sem("w_step")
        s_mask_ready = sem("mask_ready")
        s_xc_lo = sem("xc_lo")
        s_q_hi = sem("q_hi")
        s_q_lo = sem("q_lo")
        s_z_ready = sem("z_ready")
        s_rz_ready = sem("rz_ready")
        s_s_mm = sem("s_mm")
        s_t_ready = sem("t_ready")
        s_f_pad = sem("f_pad")
        s_g_step = sem("g_step")
        s_f_lo = sem("f_lo")
        s_ft_lo = sem("ft_lo")
        s_sym_v = sem("sym_v")
        s_put_mm = sem("put_mm")
        s_placed = sem("placed")
        s_ln_rs = sem("ln_rs")
        s_ln_s = sem("ln_s")
        s_ln_m = sem("ln_m")
        s_u_lo = sem("u_lo")
        s_all_step = sem("all_step")
        s_slot_step = sem("slot_step")
        s_hots_free = sem("hots_free")
        s_hots_sub = sem("hots_sub")
        s_hots_obj = sem("hots_obj")
        s_y_mm = sem("y_mm")
        s_all_res = sem("all_res")
        s_put_done = sem("put_done")
        s_slots_mm = sem("slots_mm")
        s_hot_ready = sem("hot_ready")
        s_sub_ready = sem("sub_ready")
        s_obj_ready = sem("obj_ready")
        s_sub_mm = sem("sub_mm")
        s_same_ready = sem("same_ready")
        s_rep_ready = sem("rep_ready")
        s_has_mm = sem("has_mm")
        s_has_ready = sem("has_ready")
        s_y_lo = sem("y_lo")
        s_ln_r = sem("ln_r")
        s_w1_lo = sem("w1_lo")
        s_bkb_ready = sem("bkb_ready")
        s_wv_lo = sem("wv_lo")
        s_g_lo = sem("g_lo")
        s_wvt_mm = sem("wvt_mm")
        s_wvt_out = sem("wvt_out")
        s_rows_lo = sem("rows_lo")
        s_x3_add = sem("x3_add")
        s_qh_done = sem("qh_done")
        s_pad3 = sem("pad3")
        s_t3_ready = sem("t3_ready")
        s_r_step = sem("r_step")
        s_r_ready = sem("r_ready")
        s_z_mm = sem("z_mm")
        s_nz_ready = sem("nz_ready")
        s_m3_ready = sem("m3_ready")
        s_pl_ready = sem("pl_ready")
        s_rz3_step = sem("rz3_step")
        s_rz3_ready = sem("rz3_ready")
        s_pt_lo = sem("pt_lo")
        s_o_ready = sem("o_ready")
        block = ctx.enter_context(nc.Block())

        def row(buf, t):
            return buf[:, ds(t, 1), :].rearrange("p a n -> p (a n)")

        def part_row(buf, i, t):
            return buf[:, i, ds(t, 1), :].rearrange("p a n -> p (a n)")

        def one(c, t):
            return c[:, ds(t, 1)]

        def x_row(i, slot):
            return XHL[:, slot, i, :]

        def turned(slot, i):
            return prob_t[:, ds(slot, 1), i, :].rearrange("p a n -> p (a n)")

        def w1_bank(t):
            return 2 + t if t < W1_AT_ONCE else t % 2


        PAIRS = ((0, 0), (0, 1), (1, 0))

        @block.sync
        def _(sp):
            sp.dma_start(rel[:, :], rel_d.rearrange("(p i) two -> p (i two)", p=EP)).then_inc(s_rel_in, 16)
            half = (T - 1) // 2
            sp.dma_start(X[:, 0:half, :], x_d[0:half * P].rearrange("(t p) d -> p t d", p=P)).then_inc(s_x_in0, 16)
            sp.dma_start(X[:, half:T - 1, :],
                         x_d[half * P:(T - 1) * P].rearrange("(t p) d -> p t d", p=P)).then_inc(s_x_in, 16)
            sp.wait_ge(s_x_pad, 1)
            sp.dma_start(X[0:TAIL, T - 1, :], x_d[(T - 1) * P:N]).then_inc(s_x_in, 16)
            sp.dma_start(wk0_f, wk0_d.rearrange("(m p) d -> p m d", p=P)).then_inc(s_wk0_in, 16)
            sp.dma_start(wq0_f, wq0_d.rearrange("(m p) d -> p m d", p=P)).then_inc(s_wq0_in, 16)
            for dst, src in ((bk0, bk0_d), (bq0, bq0_d), (bk3, bk3_d), (bq3, bq3_d)):
                sp.dma_start(dst, src.rearrange("(m p) -> p m", p=P),
                             allow_slow_non_contiguous=True).then_inc(s_b_in, 16)
            sp.wait_ge(s_all_done, 1)
            n = 0
            for src in (wq3_d, wk3_d, w2_d):
                for i in range(2):
                    if n >= 2:
                        sp.wait_ge(s_wst_lo, n - 1)
                    sp.dma_start(w_stage[i], src[i * 2 * P:(i + 1) * 2 * P].rearrange("(m p) d -> p m d", p=P))\
                        .then_inc((s_wst_in0, s_wst_in1)[i], 16)
                    n += 1
            sp.wait_ge(s_prod_mm, 2 * T)
            sp.dma_start(wv_f, wv3_d.rearrange("(m p) d -> p m d", p=P)).then_inc(s_wv_in, 16)
            for dst, src in ((b2_row, b2_d), (bv_row[:, :], bv3_d)):
                sp.dma_start(dst, src.rearrange("(o n) -> o n", o=1).to_broadcast([P, D])).then_inc(s_b3_in, 16)
            with sp.Fori(0, T - 1) as t:
                sp.wait_ge(s_o_norm, t + 1)
                sp.dma_start(out_d[ds(t * P, P)], row(X, t)).then_inc(s_stored, 16)
            sp.wait_ge(s_o_norm, T)
            sp.dma_start(out_d[(T - 1) * P:N], X[0:TAIL, T - 1, :]).then_inc(s_stored, 16)
            sp.wait_ge(s_stored, 16 * T)

        @block.gpsimd
        def _(pool):
            nc.gpsimd.memset(X[:, T - 1, :], 0.0).then_inc(s_x_pad, 1)
            nc.gpsimd.memset(A[:, T - 1, :], 0.0).then_inc(s_a_pad, 1)
            nc.gpsimd.memset(A[:, 0:T - 1, N:NP], 0.0).then_inc(s_a_pad, 1)
            pool.wait_ge(s_a_pad, 2)
            for a, b in ((0, 4), (4, 7), (7, T - 1)):
                pool.dma_start(A[:, a:b, 0:N], adj_d[a * P:b * P].rearrange("(t p) n -> p t n", p=P))\
                    .then_inc(s_adj_in, 16)
            pool.dma_start(A[0:TAIL, T - 1, 0:N], adj_d[(T - 1) * P:N]).then_inc(s_adj_in, 16)
            nc.gpsimd.memset(ident[:, :], 0.0).then_inc(s_blank, 1)
            nc.gpsimd.memset(ones[:, :], 1.0).then_inc(s_blank, 1)
            pool.wait_ge(s_blank, 2)
            nc.gpsimd.affine_select(out=ident[:, :], in_=ident[:, :], compare_op=ALU.not_equal, fill=1.0, base=0,
                                    pattern=[[-1, P]], channel_multiplier=1).then_inc(s_ident_ready, 1)
            nc.gpsimd.iota(iota[:, :], [[1, NP]], channel_multiplier=0,
                           allow_small_or_imprecise_dtypes=True).then_inc(s_const, 1)
            nc.gpsimd.affine_select(out=before[:, :], in_=ones[:, :], compare_op=ALU.is_gt, fill=0.0, base=0,
                                    pattern=[[1, P]], channel_multiplier=-1).then_inc(s_const, 1)
            nc.gpsimd.affine_select(out=after[:, :], in_=ones[:, :], compare_op=ALU.is_gt, fill=0.0, base=0,
                                    pattern=[[-1, P]], channel_multiplier=1).then_inc(s_const, 1)
            nc.gpsimd.iota(row_id, [[0, 1]], channel_multiplier=1,
                           allow_small_or_imprecise_dtypes=True).then_inc(s_const, 1)
            nc.gpsimd.memset(mhalfs, -0.5).then_inc(s_const, 1)
            pool.wait_ge(s_ident_ready, 1)
            nc.gpsimd.tensor_copy(identb[:, :], ident[:, :]).then_inc(s_const, 1)
            nc.gpsimd.tensor_tensor(ident2[:, :], ident[:, :], ident[:, :], ALU.add).then_inc(s_const, 1)
            pool.wait_ge(s_ix_ready, 1)
            for i in range(EC):
                nc.gpsimd.indirect_dma_start(
                    out=hit[:, i:i + 1], out_offset=None, in_=adj_d.rearrange("a (b o) -> (a b) o", o=1),
                    in_offset=bass.IndirectOffsetOnAxis(ap=rel_ix[:, i:i + 1], axis=0),
                    bounds_check=N * N - 1, oob_is_err=False).then_inc(s_hit_in, 16)
            pool.wait_ge(s_deg_ready, 1)
            pool.wait_ge(s_const, 7)
            nc.gpsimd.tensor_tensor(dinv, dinv, mhalfs, ALU.pow).then_inc(s_dinv_ready, 1)

            def blank_rows():
                nc.gpsimd.memset(adj_c, 0.0).then_inc(s_slot_fill, 1)
                nc.gpsimd.memset(x_c, 0.0).then_inc(s_slot_fill, 1)

            def gather_rows(r):
                pool.wait_ge(s_slot_fill, 3 * r + 2)
                pool.nop(nofuse=True)
                nc.gpsimd.indirect_dma_start(
                    out=x_c, out_offset=None, in_=x_d,
                    in_offset=bass.IndirectOffsetOnAxis(ap=slot_ix[:, 0:1], axis=0),
                    bounds_check=N - 1, oob_is_err=False).then_inc(s_gathered, 16)
                nc.gpsimd.indirect_dma_start(
                    out=adj_c[:, 0:N], out_offset=None, in_=adj_d,
                    in_offset=bass.IndirectOffsetOnAxis(ap=slot_ix[:, 0:1], axis=0),
                    bounds_check=N - 1, oob_is_err=False).then_inc(s_gathered, 16)
                nc.gpsimd.memset(WA[:, 0:2 * HEADS * P], 0.0).then_inc(s_slot_fill, 1)

            pool.wait_ge(s_n_ready, 1)
            many = pool.value_load(n_act[0:1, 0:1])
            with pool.If(many > P):
                with pool.Fori(0, T) as t:
                    pool.wait_ge(s_slots_ready, t + 1)
                    pool.nop(nofuse=True)
                    blank_rows()
                    gather_rows(t)
            with pool.Else():
                pool.wait_ge(s_kp_mm, G * C)
                blank_rows()
                pool.wait_ge(s_slots_ready, 1)
                gather_rows(0)

            def rstd(n):
                pool.wait_ge(s_ln_v, n + 1)
                nc.gpsimd.tensor_tensor(ln_rstd, ln_var, mhalfs[:, 0:1], ALU.pow).then_inc(s_ln_rstd, 1)

            pool.wait_ge(s_r1_free, 1)
            pool.wait_ge(s_at_v, 1 + (T + 1) // 2)
            pool.wait_ge(s_at_a, 1 + T // 2)
            for k in range(SYM_POOL):
                nc.gpsimd.tensor_tensor(SYM[:, k, :], A[:, k, :], AT[:, k, :], ALU.add).then_inc(s_sym_sum, 1)
                pool.wait_ge(s_sym_sum, k + 1)
                diag = SYM[:, k, k * P:(k + 1) * P]
                nc.gpsimd.tensor_tensor(diag, diag, ident2[:, :], ALU.add).then_inc(s_sym_ready, 1)
            for t in range(T):
                pool.wait_ge(s_ln_v, t + 1)
                nc.gpsimd.tensor_tensor(rstd_all[:, t:t + 1], var_all[:, t:t + 1], mhalfs[:, 0:1], ALU.pow)\
                    .then_inc(s_ln_rstd, 1)
            for n in range(6):
                half = slice(2 * (n % 2), 2 * (n % 2) + 2)
                pool.wait_ge(s_wst_hi, 2 * n + 2)
                nc.gpsimd.tensor_tensor(flat(staged[n // 2][:, 1, half, :]), flat(w_stage[n % 2]),
                                        flat(staged[n // 2][:, 0, half, :]), ALU.subtract).then_inc(s_wst_lo, 1)
            with pool.Fori(T, 4 * T) as n:
                rstd(n)

        @block.scalar
        def _(act):
            half = (T - 1) // 2

            def x_hi(t):
                nc.scalar.activation(part_row(UHL, 0, t), row(X, t), ACT.Copy, scale=SX).then_inc(s_x_hi, 1)

            act.wait_ge(s_x_in0, 16)
            x_hi(0)
            with act.Fori(1, half) as t:
                x_hi(t)
            act.wait_ge(s_x_in, 32)
            with act.Fori(half, T) as t:
                x_hi(t)
            act.wait_ge(s_wk0_in, 16)
            nc.scalar.activation(w0_hl[:, 0], wk0_f, ACT.Copy, scale=SW0).then_inc(s_w0_hi, 1)
            act.sem_inc(s_xt_out, 4)
            with act.Fori(0, T) as t:
                act.wait_ge(s_xt_mm, t + 1)
                nc.scalar.copy(XT[:, :, :, ds(t * P, P)],
                               PS16[:, ds((t % 4) * 1024, 1024)].rearrange("p (h c n) -> p h c n", h=2, c=C))\
                    .then_inc(s_xt_out, 1)
            act.wait_ge(s_wq0_in, 16)
            nc.scalar.activation(w0q_hl[:, 0], wq0_f, ACT.Copy, scale=SW0).then_inc(s_w0_hi, 1)
            act.sem_inc(s_kf_ready, G)
            act.wait_ge(s_bias0, 2)
            with act.Fori(0, C) as m:
                for n in range(G):
                    act.wait_ge(s_kp_mm, G * m + n + 1)
                    act.wait_ge(s_kt_done, G * m + n + 1)
                    act.nop(nofuse=True)
                    nc.scalar.activation(kf[:, n, :], PS[:, 2 + n, 0:GW], ACT.Identity, bias=one(bk0, m),
                                         scale=SK / (SX * SW0)).then_inc(s_kf_ready, 1)
            act.sem_inc(s_at_a, 1)
            with act.Fori(0, T // 2) as j:
                act.wait_ge(s_at_mm, 2 * j + 2)
                nc.scalar.copy(AT[:, :, ds(j * 2 * P + P, P)],
                               PS16[:, 4096:4096 + NP].rearrange("p (a n) -> p a n", n=P)).then_inc(s_at_a, 1)
            act.sem_inc(s_base_scaled, 2)
            act.wait_ge(s_closed_ready, 1)

            def scaled(t):
                act.wait_ge(s_prod_mm, t + 1)
                act.nop(nofuse=True)
                nc.scalar.activation(row(BASE, t), PS[:, ds(t % 2, 1), :].rearrange("p a n -> p (a n)"), ACT.Copy,
                                     scale=one(c_a, t)).then_inc(s_base_scaled, 1)

            with act.Fori(0, AHEAD) as t:
                scaled(t)

            def attend(r, between=False):
                act.wait_ge(s_gathered, 32 * r + 32)
                act.nop(nofuse=True)
                nc.scalar.activation(xc_hl[:, 0], x_c, ACT.Copy, scale=SX).then_inc(s_xc_hi, 1)
                if between:
                    scaled(T - 4)
                act.wait_ge(s_xct_mm, r + 1)
                nc.scalar.copy(xct, PS16[:, 7168:8192].rearrange("p (h c n) -> p h c n", h=2, c=C))\
                    .then_inc(s_xct_out, 1)
                if between:
                    scaled(T - 3)
                act.wait_ge(s_q_mm, r + 1)
                for m in range(C):
                    nc.scalar.activation(qf0[:, m, :], PS[:, 6, m * P:(m + 1) * P], ACT.Identity,
                                         bias=bq0[:, m:m + 1], scale=SK / (SX * SW0)).then_inc(s_q_full, 1)
                if between:
                    scaled(T - 2)
                for h in range(HEADS):
                    if between and h == 2:
                        scaled(T - 1)
                    act.wait_ge(s_nb_ready, HEADS * r + h + 1)
                    act.nop(nofuse=True)
                    nc.scalar.activation(prob[h % 3], prob[h % 3], ACT.Exp, bias=nb[:, h:h + 1],
                                         scale=1.0 / (SK * SK * 8.0), accum_out=zs[:, h:h + 1]).then_inc(s_p_ready, 1)
                    nc.scalar.activation(em[:, h:h + 1], nb[:, h:h + 1], ACT.Exp).then_inc(s_em_ready, 1)
                act.wait_ge(s_f_step, HEADS * r + HEADS)
                act.nop(nofuse=True)
                nc.scalar.activation(f_hl[:, 0, 0:NG], fsum, ACT.Copy, scale=SP_ / HEADS).then_inc(s_f_hi, 1)
                act.wait_ge(s_ft_mm, 2 * r + 1)
                nc.scalar.copy(f_t[:, 0], PS16[:, 2048:2048 + NP].rearrange("p (a n) -> p a n", n=P)).then_inc(s_ft_hi, 1)

            act.wait_ge(s_n_ready, 1)
            many = act.value_load(n_act[0:1, 0:1])
            with act.If(many > P):
                with act.Fori(AHEAD, T) as t:
                    scaled(t)
                with act.Fori(0, T) as t:
                    attend(t)
            with act.Else():
                for t in range(AHEAD, T - 4):
                    scaled(t)
                attend(0, between=True)
                act.wait_ge(s_y_sum, 3)
                nc.scalar.activation(y_hl[:, 0], y_f, ACT.Copy).then_inc(s_y_hi, 1)

            def u_hi(t):
                act.wait_ge(s_ln_x, t + 1)
                act.nop(nofuse=True)
                nc.scalar.activation(part_row(UHL, 0, t), row(X, t), ACT.Copy, scale=one(dinv_s, t)).then_inc(s_u_hi, 1)

            def stage_hi(n):
                half = slice(2 * (n % 2), 2 * (n % 2) + 2)
                act.wait_ge((s_wst_in0, s_wst_in1)[n % 2], 16 * (n // 2) + 16)
                act.nop(nofuse=True)
                nc.scalar.activation(staged[n // 2][:, 0, half, :], w_stage[n % 2], ACT.Copy, scale=SW)\
                    .then_inc(s_wst_hi, 1)
                nc.scalar.activation(w_stage[n % 2], w_stage[n % 2], ACT.Copy, scale=SW).then_inc(s_wst_hi, 1)

            def w1_hi(t):
                act.wait_ge(s_prod_mm, T + t + 1)
                act.nop(nofuse=True)
                nc.scalar.activation(VHL[:, 0, t, :], PS[:, w1_bank(t), :], ACT.Copy,
                                     scale=dinv_half[:, t:t + 1]).then_inc(s_w1_hi, 1)

            with act.Fori(0, 4) as t:
                u_hi(t)
            stage_hi(0)
            stage_hi(1)
            with act.Fori(4, T) as t:
                u_hi(t)
            for t in range(T):
                w1_hi(t)
                if 2 <= t < 6:
                    stage_hi(t)
            act.wait_ge(s_wv_in, 16)
            nc.scalar.activation(wv_hl[:, 0], wv_f, ACT.Copy, scale=SW).then_inc(s_wv_hi, 1)
            for d in range(C):
                act.wait_ge(s_g_mm, d + 1)
                nc.scalar.activation(GHL[:, 0, d, :], PS[:, 2 + d % 2, :], ACT.Copy, scale=1.0 / SW).then_inc(s_g_hi, 1)
            act.wait_ge(s_vec_mm, 1)
            nc.scalar.activation(a_row[:, :], PS[:, 4, :], ACT.Copy, scale=SX * SW / (SB * SW)).then_inc(s_vec_out, 1)
            nc.scalar.activation(c2, PS[:, 5, 0:C], ACT.Copy, scale=1.0 / SB).then_inc(s_vec_out, 1)
            nc.scalar.activation(beta, PS[:, 5, C:C + 1], ACT.Copy, scale=SX * SW / (SB * SB)).then_inc(s_vec_out, 1)
            act.sem_inc(s_xt_out, 2)

            def step(n, t, slot, turned=True, rows=True, end=True):
                if turned:
                    act.wait_ge(s_xt_mm, n * T + t - 1)
                    nc.scalar.copy(XT[:, :, :, ds((t - 2) * P, P)],
                                   PS16[:, 2048 + slot * 1024:3072 + slot * 1024]
                                   .rearrange("p (h c n) -> p h c n", h=2, c=C)).then_inc(s_xt_out, 1)
                if rows:
                    act.wait_ge(s_rows_mm, (n - 1) * T + t - 2)
                    act.nop(nofuse=True)
                    dst = SHL if n == 1 else VHL
                    nc.scalar.activation(part_row(dst, 0, t - 3), PS[:, 5 - slot, :], ACT.Copy, scale=1.0 / SX)\
                        .then_inc(s_rows_hi, 1)
                if end:
                    act.wait_ge(s_ln_x, n * T + t + 1)
                    act.nop(nofuse=True)
                    nc.scalar.activation(x_row(0, slot), row(X, t), ACT.Copy, scale=SX).then_inc(s_x_hi, 1)

            for n in (1, 2):
                if n == 2:
                    act.sem_inc(s_xt_out, 2)
                step(n, 0, 0, turned=False, rows=False)
                step(n, 1, 1, turned=False, rows=False)
                step(n, 2, 0, rows=False)
                with act.Fori(1, T // 2) as j:
                    step(n, 2 * j + 1, 1)
                    step(n, 2 * j + 2, 0)
                step(n, T, 1, end=False)
                step(n, T + 1, 0, end=False)
                step(n, T + 2, 1, turned=False, end=False)
            act.sem_inc(s_qf_ready, 2)

            def queries(n, m0, m1):
                with act.Fori(m0, m1) as m:
                    act.wait_ge(s_qt_mm, C * n + m + 1)
                    act.wait_ge(s_qt_done, C * n + m + 1)
                    act.nop(nofuse=True)
                    nc.scalar.activation(qf[:, ds(m % 2, 1), :].rearrange("p a n -> p (a n)"),
                                         PS[:, ds(6 + m % 2, 1), 0:GW].rearrange("p a n -> p (a n)"), ACT.Identity,
                                         bias=one(c2, m), scale=1.0 / SX).then_inc(s_qf_ready, 1)

            def soft(t):
                act.wait_ge(s_nm3_ready, t + 1)
                act.nop(nofuse=True)
                nc.scalar.activation(zero_fill[:, 0:N], score[:, 0:N], ACT.Exp, bias=nm3, scale=Z_SCALE,
                                     accum_out=z3).then_inc(s_p3_ready, 1)
                act.wait_ge(s_p3_ready, t + 1)
                if not isinstance(t, int) or t > 0:
                    act.wait_ge(s_pt_mm, 2 * t)
                    act.nop(nofuse=True)
                nc.scalar.activation(prob_hl[:, 0, 0:N], zero_fill[:, 0:N], ACT.Copy, scale=SP_).then_inc(s_ph_ready, 1)

            def turn(t):
                act.wait_ge(s_pt_mm, 2 * t + 1)
                if not isinstance(t, int) or t >= 2:
                    act.wait_ge(s_o_mm, t - 1)
                nc.scalar.copy(turned(t % 2, 0), PS16[:, 3072:3072 + NP]).then_inc(s_pt_hi, 1)

            queries(0, 0, C)
            queries(1, 0, 2)
            soft(0)
            queries(1, 2, C)
            turn(0)
            queries(2, 0, 2)
            soft(1)
            queries(2, 2, C)
            soft(2)
            turn(1)
            with act.Fori(3, T) as t:
                soft(t)
                turn(t - 1)
            turn(T - 1)

        @block.vector
        def _(dve):
            dve.sem_inc(s_w0_out, 2)
            dve.sem_inc(s_kt_done, G)
            dve.sem_inc(s_at_v, 1)
            dve.wait_ge(s_rel_in, 16)
            rel_v = rel[:, :].rearrange("p (i two) -> p two i", two=2)
            nc.vector.tensor_copy(subf[:, :], rel_v[:, 0]).then_inc(s_step, 1)
            nc.vector.tensor_copy(objf[:, :], rel_v[:, 1]).then_inc(s_step, 1)
            dve.wait_ge(s_step, 2)
            nc.vector.tensor_scalar(bad[:, :], subf[:, :], float(N), None, ALU.is_ge).then_inc(s_step, 1)
            nc.vector.tensor_tensor(hit[:, :], subf[:, :], objf[:, :], ALU.is_equal).then_inc(s_step, 1)
            nc.vector.tensor_scalar(pair[:, :, 0], subf[:, :], 1.0, None, ALU.add).then_inc(s_step, 1)
            nc.vector.tensor_scalar(pair[:, :, 1], objf[:, :], 1.0, None, ALU.add).then_inc(s_step, 1)
            dve.wait_ge(s_step, 6)
            nc.vector.scalar_tensor_tensor(out=bad[:, :], in0=objf[:, :], scalar=float(N), in1=bad[:, :],
                                           op0=ALU.is_ge, op1=ALU.add).then_inc(s_step, 1)
            dve.wait_ge(s_step, 7)
            nc.vector.tensor_tensor(bad[:, :], bad[:, :], hit[:, :], ALU.add).then_inc(s_step, 1)
            dve.wait_ge(s_step, 8)
            nc.vector.scalar_tensor_tensor(out=hit[:, :], in0=subf[:, :], scalar=float(N), in1=objf[:, :],
                                           op0=ALU.mult, op1=ALU.add).then_inc(s_step, 1)
            dve.wait_ge(s_step, 9)
            nc.vector.scalar_tensor_tensor(out=rel_ix[:, :], in0=bad[:, :], scalar=FAR, in1=hit[:, :],
                                           op0=ALU.mult, op1=ALU.add).then_inc(s_step, 1)
            dve.wait_ge(s_step, 10)
            nc.vector.memset(hit[:, :], 0.0).then_inc(s_ix_ready, 1)
            with dve.Fori(0, T) as t:
                dve.wait_ge(s_x_hi, t + 1)
                nc.vector.scalar_tensor_tensor(out=part_row(UHL, 1, t), in0=row(X, t), scalar=SX,
                                               in1=part_row(UHL, 0, t), op0=ALU.mult, op1=ALU.subtract)\
                    .then_inc(s_x_lo, 1)

            def w0_low(n, full, hl):
                dve.wait_ge(s_w0_hi, n + 1)
                nc.vector.scalar_tensor_tensor(out=flat(hl[:, 1]), in0=flat(full), scalar=SW0, in1=flat(hl[:, 0]),
                                               op0=ALU.mult, op1=ALU.subtract).then_inc(s_w0_lo, 1)

            w0_low(0, wk0_f, w0_hl)

            def weights_out(n, dst, m):
                dve.wait_ge(s_w0_mm, n + 1)
                nc.vector.tensor_copy(dst[:, :, :, m * P:(m + 1) * P],
                                      PS16[:, 4096 + (n % 2) * 1024:4096 + (n % 2) * 1024 + 1024]
                                      .rearrange("p (h c n) -> p h c n", h=2, c=C)).then_inc(s_w0_out, 1)

            for m in range(C):
                weights_out(m, WKT, m)
            dve.wait_ge(s_b_in, 64)
            nc.vector.tensor_scalar(bk0, bk0, SK, None, ALU.mult).then_inc(s_bias0, 1)
            nc.vector.tensor_scalar(bq0, bq0, SK, None, ALU.mult).then_inc(s_bias0, 1)
            w0_low(1, wq0_f, w0q_hl)
            with dve.Fori(0, C) as m:
                for n in range(G):
                    dve.wait_ge(s_kf_ready, G * m + n + 1 + G)
                    k_at = [KT[:, i, ds(m, 1), n * GW:(n + 1) * GW].rearrange("p a n -> p (a n)") for i in range(2)]
                    nc.vector.tensor_copy(k_at[0], kf[:, n, :]).then_inc(s_kh_done, 1)
                    dve.wait_ge(s_kh_done, G * m + n + 1)
                    nc.vector.tensor_tensor(k_at[1], kf[:, n, :], k_at[0], ALU.subtract).then_inc(s_kt_done, 1)
            for m in range(C):
                weights_out(C + m, WQT, m)
            with dve.Fori(0, (T + 1) // 2) as j:
                dve.wait_ge(s_at_mm, 2 * j + 1)
                nc.vector.tensor_copy(AT[:, :, ds(j * 2 * P, P)],
                                      PS16[:, 0:NP].rearrange("p (a n) -> p a n", n=P)).then_inc(s_at_v, 1)
            dve.wait_ge(s_sums_mm, 1)
            nc.vector.tensor_copy(row_n, PS[:, 2, 0:T]).then_inc(s_step, 1)
            nc.vector.tensor_copy(col_n, PS[:, 3, 0:T]).then_inc(s_step, 1)
            dve.wait_ge(s_step, 12)
            nc.vector.tensor_tensor(dinv, row_n, col_n, ALU.add).then_inc(s_step, 1)
            nc.vector.tensor_scalar(c_b, row_n, E_DIAG, DIAG, ALU.mult, ALU.add).then_inc(s_step, 1)
            dve.wait_ge(s_step, 14)
            nc.vector.tensor_scalar(dinv, dinv, 0.5, 1.0, ALU.mult, ALU.add).then_inc(s_deg_ready, 1)
            nc.vector.reciprocal(c_b, c_b).then_inc(s_step, 1)
            dve.wait_ge(s_step, 15)
            nc.vector.tensor_scalar(c_a, c_b, E_DIAG, None, ALU.mult).then_inc(s_step, 1)
            dve.wait_ge(s_step, 16)
            nc.vector.tensor_scalar(c_b, c_b, SX * DIAG, SX, ALU.mult, ALU.add).then_inc(s_closed_ready, 1)

            def residual(t):
                dve.wait_ge(s_base_scaled, t + 3)
                nc.vector.scalar_tensor_tensor(out=BASE[:, t, :], in0=X[:, t, :], scalar=c_b[:, t:t + 1],
                                               in1=BASE[:, t, :], op0=ALU.mult, op1=ALU.add).then_inc(s_base_done, 1)

            dve.wait_ge(s_closed_ready, 1)
            for t in range(AHEAD):
                residual(t)
            dve.wait_ge(s_dinv_ready, 1)
            nc.vector.tensor_scalar(dinv_half, dinv, 0.5, None, ALU.mult).then_inc(s_dinv_s_ready, 1)
            nc.vector.tensor_scalar(dinv_s, dinv, SX, None, ALU.mult).then_inc(s_dinv_s_ready, 1)
            dve.wait_ge(s_hit_in, 16 * EC)
            dve.wait_ge(s_const, 7)
            nc.vector.tensor_scalar(act16[:, :], hit[:, :], 1.0, None, ALU.is_equal).then_inc(s_act_ready, 1)
            dve.wait_ge(s_act_ready, 1)
            nc.vector.tensor_scalar(bad[:, :], act16[:, :], -20000.0, 20000.0, ALU.mult, ALU.add)\
                .then_inc(s_step, 1)
            dve.wait_ge(s_tot_mm, 1)
            nc.vector.tensor_copy(tot16[:, :], PS[0:EC, 1, 0:P]).then_inc(s_tot_ready, 1)
            dve.wait_ge(s_rank_mm, 1)
            nc.vector.tensor_copy(n_act[:, :], PS[0:1, 2, 0:1]).then_inc(s_n_ready, 1)
            dve.wait_ge(s_step, 17)
            nc.vector.tensor_tensor(rank[:, :], PS[0:EP, 0, 0:EC], bad[:, :], ALU.add).then_inc(s_rank_ready, 1)
            dve.wait_ge(s_rank_ready, 1)
            dve.wait_ge(s_n_ready, 1)
            many = dve.value_load(n_act[0:1, 0:1])

            def attend(r, between=False):
                nc.vector.tensor_scalar(dmask, iota[:, :], slot_row, None, ALU.is_equal).then_inc(s_d_ready, 1)
                dve.wait_ge(s_w_mm, r + 1)
                nc.vector.tensor_scalar(wmask.rearrange("p (g n) -> p g n", g=G), PS[:, 2:5, 0:GW], 1.0, 1.0,
                                        ALU.min, ALU.add).then_inc(s_w_step, 1)
                dve.wait_ge(s_w_step, r + 1)
                if between:
                    residual(T - 6)
                    residual(T - 5)
                dve.wait_ge(s_gathered, 32 * r + 32)
                nc.vector.tensor_tensor(wmask, wmask, adj_c, ALU.subtract).then_inc(s_mask_ready, 1)
                nc.vector.tensor_scalar(bmask, adj_c, -1.0, OFF, ALU.add, ALU.mult).then_inc(s_mask_ready, 1)
                dve.wait_ge(s_xc_hi, r + 1)
                nc.vector.scalar_tensor_tensor(out=xc_hl[:, 1], in0=x_c, scalar=SX, in1=xc_hl[:, 0], op0=ALU.mult,
                                               op1=ALU.subtract).then_inc(s_xc_lo, 1)
                if between:
                    residual(T - 4)
                    residual(T - 3)
                dve.wait_ge(s_q_full, C * r + C)
                dve.wait_ge(s_slot_fill, 3 * r + 3)
                for lanes, q_one in q_lanes:
                    nc.vector.tensor_copy(q_one[:, 0], qf0[lanes]).then_inc(s_q_hi, 1)
                dve.wait_ge(s_q_hi, 2 * r + 2)
                for lanes, q_one in q_lanes:
                    nc.vector.tensor_tensor(q_one[:, 1], qf0[lanes], q_one[:, 0], ALU.subtract).then_inc(s_q_lo, 1)
                dve.wait_ge(s_q_lo, 2 * r + 2)
                dve.wait_ge(s_mask_ready, 2 * r + 2)

                def add_head(h):
                    one_h = slice(h, h + 1)
                    dve.wait_ge(s_em_ready, HEADS * r + h + 1)
                    nc.vector.scalar_tensor_tensor(out=zs[:, one_h], in0=em[:, one_h], scalar=DIAG, in1=zs[:, one_h],
                                                   op0=ALU.mult, op1=ALU.add).then_inc(s_z_ready, 1)
                    dve.wait_ge(s_z_ready, HEADS * r + h + 1)
                    nc.vector.reciprocal(rz[:, one_h], zs[:, one_h]).then_inc(s_rz_ready, 1)
                    dve.wait_ge(s_rz_ready, HEADS * r + h + 1)
                    if h == 0:
                        nc.vector.tensor_scalar(fsum, prob[0], rz[:, one_h], None, ALU.mult).then_inc(s_f_step, 1)
                    else:
                        dve.wait_ge(s_f_step, HEADS * r + h)
                        nc.vector.scalar_tensor_tensor(out=fsum, in0=prob[h % 3], scalar=rz[:, one_h], in1=fsum,
                                                       op0=ALU.mult, op1=ALU.add).then_inc(s_f_step, 1)

                for h in range(HEADS):
                    b = 2 + G * (h % 2)
                    dve.wait_ge(s_s_mm, HEADS * r + h + 1)
                    if h >= 3:
                        dve.wait_ge(s_f_step, HEADS * r + h - 2)
                    dve.nop(nofuse=True)
                    nc.vector.tensor_tensor_reduce(
                        out=prob[h % 3].rearrange("p (g n) -> p g n", g=G), in0=PS[:, b:b + G, 0:GW],
                        in1=wmask.rearrange("p (g n) -> p g n", g=G), scale=1.0, scalar=-3.0e38, op0=ALU.mult,
                        op1=ALU.max, accum_out=mx[:, h:h + 1]).then_inc(s_t_ready, 1)
                    dve.wait_ge(s_t_ready, HEADS * r + h + 1)
                    nc.vector.tensor_scalar(nb[:, h:h + 1], mx[:, h:h + 1], -1.0 / (SK * SK * 8.0), -DIAG, ALU.mult,
                                            ALU.min).then_inc(s_nb_ready, 1)
                    if h >= 1:
                        add_head(h - 1)
                add_head(HEADS - 1)
                dve.wait_ge(s_f_step, HEADS * r + HEADS)
                nc.vector.memset(f_hl[:, :, NG:NP], 0.0).then_inc(s_f_pad, 1)
                nc.vector.tensor_tensor(g_tmp, em, rz, ALU.mult).then_inc(s_g_step, 1)
                dve.wait_ge(s_g_step, 3 * r + 1)
                nc.vector.reduce_sum(g_sum, g_tmp, mybir.AxisListType.X).then_inc(s_g_step, 1)
                dve.wait_ge(s_g_step, 3 * r + 2)
                nc.vector.tensor_scalar(g_sum, g_sum, DIAG / HEADS, 1.0, ALU.mult, ALU.add).then_inc(s_g_step, 1)
                dve.wait_ge(s_f_hi, r + 1)
                nc.vector.scalar_tensor_tensor(out=f_hl[:, 1, 0:NG], in0=fsum, scalar=SP_ / HEADS, in1=f_hl[:, 0, 0:NG],
                                               op0=ALU.mult, op1=ALU.subtract).then_inc(s_f_lo, 1)
                dve.wait_ge(s_ft_mm, 2 * r + 2)
                nc.vector.tensor_copy(f_t[:, 1], PS16[:, 4096:4096 + NP].rearrange("p (a n) -> p a n", n=P))\
                    .then_inc(s_ft_lo, 1)

            def symmetric():
                dve.wait_ge(s_r1_free, 1)
                dve.wait_ge(s_at_v, 1 + (T + 1) // 2)
                dve.wait_ge(s_at_a, 1 + T // 2)
                for k in range(SYM_POOL, T):
                    nc.vector.tensor_tensor(SYM[:, k, :], A[:, k, :], AT[:, k, :], ALU.add).then_inc(s_sym_v, 1)
                    dve.wait_ge(s_sym_v, 2 * (k - SYM_POOL) + 1)
                    diag = SYM[:, k, k * P:(k + 1) * P]
                    nc.vector.tensor_tensor(diag, diag, ident2[:, :], ALU.add).then_inc(s_sym_v, 1)

            def layer0_end(put):
                for t in range(T + 2):
                    if put and t < T:
                        dve.wait_ge(s_put_mm, t + 1)
                        nc.vector.scalar_tensor_tensor(out=BASE[:, t, :], in0=BASE[:, t, :], scalar=nohas[:, t:t + 1],
                                                       in1=PS[:, t % 2, :], op0=ALU.mult, op1=ALU.add)\
                            .then_inc(s_placed, 1)
                    if 1 <= t <= T:
                        dve.wait_ge(s_ln_rstd, t)
                        nc.vector.tensor_scalar(rstd_s[:, t - 1:t], rstd_all[:, t - 1:t], 1.0 / SX, None, ALU.mult)\
                            .then_inc(s_ln_rs, 1)
                    if t < T:
                        if put:
                            dve.wait_ge(s_placed, t + 1)
                            dve.nop(nofuse=True)
                        nc.vector.bn_stats(ln_st, BASE[:, t, :]).then_inc(s_ln_s, 1)
                    if 1 <= t <= T:
                        dve.wait_ge(s_ln_rs, t)
                        nc.vector.tensor_scalar(X[:, t - 1, :], BASE[:, t - 1, :], mv_all[:, t - 1, 0:1],
                                                rstd_s[:, t - 1:t], ALU.subtract, ALU.mult).then_inc(s_ln_x, 1)
                    if t < T:
                        dve.wait_ge(s_ln_s, t + 1)
                        dve.nop(nofuse=True)
                        nc.vector.bn_aggr(mv_all[:, t, :], ln_st).then_inc(s_ln_m, 1)
                    if t >= 2:
                        dve.wait_ge(s_u_hi, t - 1)
                        nc.vector.scalar_tensor_tensor(out=UHL[:, 1, t - 2, :], in0=X[:, t - 2, :],
                                                       scalar=dinv_s[:, t - 2:t - 1], in1=UHL[:, 0, t - 2, :],
                                                       op0=ALU.mult, op1=ALU.subtract).then_inc(s_u_lo, 1)
                    if t < T:
                        dve.wait_ge(s_ln_m, t + 1)
                        nc.vector.tensor_scalar(var_all[:, t:t + 1], mv_all[:, t, 1:2], 1.0 / (SX * SX), EPS,
                                                ALU.mult, ALU.add).then_inc(s_ln_v, 1)

            with dve.If(many > P):
                nc.vector.tensor_scalar(bad[:, :], act16[:, :], 5000.0, -5000.0, ALU.mult, ALU.add)\
                    .then_inc(s_all_step, 1)
                nc.vector.tensor_copy(slot_row, row_id).then_inc(s_all_step, 1)
                dve.wait_ge(s_all_step, 2)
                nc.vector.tensor_tensor(subf[:, :], subf[:, :], bad[:, :], ALU.add).then_inc(s_all_step, 1)
                dve.wait_ge(s_all_step, 3)
                for t in range(AHEAD, T):
                    residual(t)
                dve.wait_ge(s_base_done, T)
                with dve.Fori(0, T) as t:
                    nc.vector.tensor_scalar(slot_far, slot_row, 0.0, FAR, ALU.is_lt, ALU.mult)\
                        .then_inc(s_slot_step, 1)
                    dve.wait_ge(s_slot_step, t + 1)
                    nc.vector.tensor_tensor(slot_ix[:, :], slot_far, slot_row, ALU.add).then_inc(s_slots_ready, 1)
                    with dve.Fori(0, EC // 2) as j:
                        for i in range(2):
                            dve.wait_ge(s_hots_free, t * EC + j * 2 + i + 1)
                            nc.vector.tensor_scalar(all_sub[i][0:EP, :], iota[0:EP, 0:P], one(subf, j * 2 + i), None,
                                                    ALU.is_equal).then_inc(s_hots_sub, 1)
                            nc.vector.tensor_scalar(all_obj[i][0:EP, :], iota[0:EP, 0:NG], one(objf, j * 2 + i), None,
                                                    ALU.is_equal).then_inc(s_hots_obj, 1)
                    attend(t)
                    dve.wait_ge(s_y_mm, t + 1)
                    dve.wait_ge(s_g_step, 3 * t + 3)
                    nc.vector.tensor_scalar(row(BASE, t), row(X, t), g_sum, SX, ALU.mult, ALU.mult).then_inc(s_all_res, 1)
                    dve.wait_ge(s_all_res, t + 1)
                    nc.vector.scalar_tensor_tensor(out=row(BASE, t), in0=PS[:, 0, :], scalar=1.0 / SP_,
                                                   in1=row(BASE, t), op0=ALU.mult, op1=ALU.add)\
                        .then_inc(s_put_done, 1)
                    nc.vector.tensor_scalar(slot_row, slot_row, float(P), None, ALU.add).then_inc(s_all_step, 1)
                    nc.vector.tensor_scalar(subf[:, :], subf[:, :], float(-P), None, ALU.add).then_inc(s_all_step, 1)
                    dve.wait_ge(s_all_step, 2 * t + 5)
                    dve.wait_ge(s_put_done, t + 1)
                nc.vector.memset(ln_mv, 0.0).then_inc(s_r1_free, 1)
                dve.wait_ge(s_r1_free, 1)
                nc.vector.memset(ln_mv, 0.0).then_inc(s_all_done, 1)
                symmetric()
                dve.wait_ge(s_dinv_s_ready, 2)
                layer0_end(put=False)
            with dve.Else():
                for k in range(EC // OC):
                    if k >= 2:
                        dve.wait_ge(s_slots_mm, k - 1)
                    nc.vector.tensor_tensor(
                        hot[k % 2][0:EP], rank[:, k * OC:(k + 1) * OC].unsqueeze(2).to_broadcast([EP, OC, P]),
                        iota[0:EP, 0:P].unsqueeze(1).to_broadcast([EP, OC, P]), ALU.is_equal).then_inc(s_hot_ready, 1)
                dve.wait_ge(s_slots_mm, EC // OC)
                nc.vector.tensor_scalar(slot_row, PS[:, 5, 0:1], -1.0, None, ALU.add).then_inc(s_slot_step, 1)
                nc.vector.tensor_scalar(slot_obj, PS[:, 5, 1:2], -1.0, None, ALU.add).then_inc(s_slot_step, 1)
                dve.wait_ge(s_slot_step, 2)
                nc.vector.tensor_scalar(slot_far, slot_row, 0.0, FAR, ALU.is_lt, ALU.mult).then_inc(s_slot_step, 1)
                nc.vector.tensor_scalar(sub_b, ones[:, :], slot_row, None, ALU.mult).then_inc(s_sub_ready, 1)
                for t in range(AHEAD, T - 6):
                    residual(t)
                nc.vector.tensor_scalar(obj_hot, iota[:, 0:NG], slot_obj, None, ALU.is_equal).then_inc(s_obj_ready, 1)
                nc.vector.tensor_scalar(slot_low, slot_row, 0.0, None, ALU.is_ge).then_inc(s_slot_step, 1)
                dve.wait_ge(s_slot_step, 4)
                nc.vector.tensor_tensor(slot_ix[:, :], slot_far, slot_row, ALU.add).then_inc(s_slots_ready, 1)
                dve.wait_ge(s_sub_mm, 1)
                nc.vector.tensor_scalar(same, PS[:, 6, 0:P], slot_row, slot_low, ALU.is_equal, ALU.mult)\
                    .then_inc(s_same_ready, 1)
                dve.wait_ge(s_same_ready, 1)
                nc.vector.tensor_tensor_reduce(out=sub_b, in0=same, in1=after[:, :], scale=1.0, scalar=0.0,
                                               op0=ALU.mult, op1=ALU.add, accum_out=rep).then_inc(s_slot_step, 1)
                dve.wait_ge(s_slot_step, 5)
                nc.vector.tensor_scalar(rep, rep, 0.0, slot_low, ALU.is_equal, ALU.mult).then_inc(s_rep_ready, 1)
                attend(0, between=True)
                dve.wait_ge(s_rep_ready, 1)
                dve.wait_ge(s_d_ready, 1)
                nc.vector.tensor_scalar(put_hot, dmask, rep, None, ALU.mult).then_inc(s_r1_free, 1)
                dve.wait_ge(s_g_step, 3)
                dve.wait_ge(s_f_lo, 1)
                nc.vector.tensor_scalar(y_f, xc_hl[:, 0], g_sum, None, ALU.mult).then_inc(s_y_sum, 1)
                dve.wait_ge(s_y_sum, 1)
                nc.vector.scalar_tensor_tensor(out=y_f, in0=xc_hl[:, 1], scalar=g_sum, in1=y_f, op0=ALU.mult,
                                               op1=ALU.add).then_inc(s_y_sum, 1)
                residual(T - 2)
                residual(T - 1)
                symmetric()
                dve.wait_ge(s_has_mm, 1)
                nc.vector.tensor_scalar(nohas, PS[:, 1, 0:T], -1.0, 1.0, ALU.mult, ALU.add).then_inc(s_has_ready, 1)
                dve.wait_ge(s_y_mm, 1)
                dve.wait_ge(s_y_sum, 2)
                nc.vector.scalar_tensor_tensor(out=y_f, in0=PS[:, 0, :], scalar=1.0 / SP_, in1=y_f, op0=ALU.mult,
                                               op1=ALU.add).then_inc(s_y_sum, 1)
                dve.wait_ge(s_y_hi, 1)
                nc.vector.tensor_tensor(y_hl[:, 1], y_f, y_hl[:, 0], ALU.subtract).then_inc(s_y_lo, 1)
                dve.wait_ge(s_y_lo, 1)
                nc.vector.memset(ln_mv, 0.0).then_inc(s_all_done, 1)
                dve.wait_ge(s_has_ready, 1)
                dve.wait_ge(s_base_done, T)
                dve.wait_ge(s_dinv_s_ready, 2)
                layer0_end(put=True)

            def norm(n, x_t):
                dve.wait_ge(s_ln_r, n + 1)
                dve.nop(nofuse=True)
                nc.vector.bn_stats(ln_st, x_t).then_inc(s_ln_s, 1)
                dve.wait_ge(s_ln_s, n + 1)
                dve.nop(nofuse=True)
                nc.vector.bn_aggr(ln_mv, ln_st).then_inc(s_ln_m, 1)
                dve.wait_ge(s_ln_m, n + 1)
                nc.vector.tensor_scalar(ln_var, ln_mv[:, 1:2], EPS, None, ALU.add).then_inc(s_ln_v, 1)
                dve.wait_ge(s_ln_rstd, n + 1)
                return nc.vector.tensor_scalar(x_t, x_t, ln_mv[:, 0:1], ln_rstd, ALU.subtract, ALU.mult)

            def w1_lo(t):
                dve.wait_ge(s_w1_hi, t + 1)
                nc.vector.scalar_tensor_tensor(
                    out=VHL[:, 1, t, :], in0=PS[:, w1_bank(t), :], scalar=dinv_half[:, t:t + 1], in1=VHL[:, 0, t, :],
                    op0=ALU.mult, op1=ALU.subtract).then_inc(s_w1_lo, 1)

            for t in range(T):
                w1_lo(t)
            nc.vector.tensor_scalar(b_hl[:, 0, 0:C], bk3, SB, None, ALU.mult).then_inc(s_step, 1)
            nc.vector.tensor_scalar(b_hl[:, 0, C:2 * C], bq3, SB, None, ALU.mult).then_inc(s_step, 1)
            dve.wait_ge(s_step, 19)
            nc.vector.scalar_tensor_tensor(out=b_hl[:, 1, 0:C], in0=bk3, scalar=SB, in1=b_hl[:, 0, 0:C], op0=ALU.mult,
                                           op1=ALU.subtract).then_inc(s_step, 1)
            nc.vector.scalar_tensor_tensor(out=b_hl[:, 1, C:2 * C], in0=bq3, scalar=SB, in1=b_hl[:, 0, C:2 * C],
                                           op0=ALU.mult, op1=ALU.subtract).then_inc(s_step, 1)
            dve.wait_ge(s_step, 21)
            for i in range(2):
                for m in range(C):
                    nc.vector.tensor_scalar(bk_b[:, i, m, :], ones[:, :], b_hl[:, i, m:m + 1], None, ALU.mult)\
                        .then_inc(s_bkb_ready, 1)
            dve.wait_ge(s_wv_hi, 1)
            nc.vector.scalar_tensor_tensor(out=flat(wv_hl[:, 1]), in0=flat(wv_f), scalar=SW, in1=flat(wv_hl[:, 0]),
                                           op0=ALU.mult, op1=ALU.subtract).then_inc(s_wv_lo, 1)
            for d in range(C):
                dve.wait_ge(s_g_hi, d + 1)
                nc.vector.scalar_tensor_tensor(out=GHL[:, 1, d, :], in0=PS[:, 2 + d % 2, :], scalar=1.0 / SW,
                                               in1=GHL[:, 0, d, :], op0=ALU.mult, op1=ALU.subtract)\
                    .then_inc(s_g_lo, 1)
            for m in range(C):
                dve.wait_ge(s_wvt_mm, m + 1)
                nc.vector.tensor_copy(WVT[:, :, :, m * P:(m + 1) * P],
                                      PS16[:, 6144 + (m % 2) * 1024:6144 + (m % 2) * 1024 + 1024]
                                      .rearrange("p (h c n) -> p h c n", h=2, c=C)).then_inc(s_wvt_out, 1)

            def add_rows(t, before, scale):
                dve.wait_ge(s_prod_mm, before + t + 1)
                return nc.vector.scalar_tensor_tensor(
                    out=row(X, t), in0=PS[:, ds(t % 2, 1), :].rearrange("p a n -> p (a n)"), scalar=scale,
                    in1=row(X, t), op0=ALU.mult, op1=ALU.add)

            def x_low(n, t, slot):
                dve.wait_ge(s_x_hi, n * T + t + 1)
                nc.vector.scalar_tensor_tensor(out=x_row(1, slot), in0=row(X, t), scalar=SX, in1=x_row(0, slot),
                                               op0=ALU.mult, op1=ALU.subtract).then_inc(s_x_lo, 1)

            def rows_low(n, t, slot):
                dst = SHL if n == 1 else VHL
                dve.wait_ge(s_rows_hi, (n - 1) * T + t + 1)
                nc.vector.scalar_tensor_tensor(out=part_row(dst, 1, t), in0=PS[:, 4 + slot, :], scalar=1.0 / SX,
                                               in1=part_row(dst, 0, t), op0=ALU.mult, op1=ALU.subtract)\
                    .then_inc(s_rows_lo, 1)

            dve.wait_ge(s_ln_x, T)
            dve.sem_inc(s_ln_r, T)

            def step(n, t, slot, rows=True):
                if n == 2:
                    dve.wait_ge(s_ln_x, T + t + 1)
                    nc.vector.tensor_tensor(row(X, t), row(X, t), b2_row, ALU.add).then_inc(s_x3_add, 1)
                    dve.wait_ge(s_x3_add, t + 1)
                add_rows(t, (n + 1) * T, 1.0 / SX if n == 1 else 1.0 / SW).then_inc(s_ln_r, 1)
                norm(n * T + t, row(X, t)).then_inc(s_ln_x, 1)
                x_low(n, t, slot)
                if rows:
                    rows_low(n, t - 3, 1 - slot)

            dve.wait_ge(s_b3_in, 32)
            dve.sem_inc(s_rows_lo, 2)
            for n in (1, 2):
                step(n, 0, 0, rows=False)
                step(n, 1, 1, rows=False)
                step(n, 2, 0, rows=False)
                with dve.Fori(1, T // 2) as j:
                    step(n, 2 * j + 1, 1)
                    step(n, 2 * j + 2, 0)
                for t in range(T - 3, T):
                    rows_low(n, t, t % 2)
            dve.sem_inc(s_qt_done, 2)

            def queries(n, m0, m1):
                with dve.Fori(m0, m1) as m:
                    dve.wait_ge(s_qf_ready, C * n + m + 3)
                    full = qf[:, ds(m % 2, 1), :].rearrange("p a n -> p (a n)")
                    q_at = [QT[:, i, ds(m, 1), n * GW:(n + 1) * GW].rearrange("p a n -> p (a n)") for i in range(2)]
                    nc.vector.tensor_copy(q_at[0], full).then_inc(s_qh_done, 1)
                    dve.wait_ge(s_qh_done, C * n + m + 1)
                    nc.vector.tensor_tensor(q_at[1], full, q_at[0], ALU.subtract).then_inc(s_qt_done, 1)

            dve.wait_ge(s_vec_out, 3)
            nc.vector.memset(QT[:, :, :, NG:NP], 0.0).then_inc(s_pad3, 1)
            nc.vector.memset(prob_hl[:, :, N:NP], 0.0).then_inc(s_pad3, 1)
            dve.sem_inc(s_t3_ready, 1)

            def scores(t):
                dve.wait_ge(s_ln_x, 2 * T + t + 1)
                nc.vector.scalar_tensor_tensor(out=out_t, in0=row(X, t), scalar=1.0, in1=a_row[:, :], op0=ALU.mult,
                                               op1=ALU.mult, accum_out=r_acc).then_inc(s_r_step, 1)
                dve.wait_ge(s_r_step, t + 1)
                nc.vector.tensor_tensor(r3, r_acc, beta, ALU.add).then_inc(s_r_ready, 1)
                dve.wait_ge(s_r_ready, t + 1)
                dve.wait_ge(s_z_mm, t + 1)
                nc.vector.scalar_tensor_tensor(
                    out=score.rearrange("p (g n) -> p g n", g=G), in0=PS[:, 0:G, 0:GW], scalar=r3,
                    in1=A[:, ds(t, 1), 0:NG].rearrange("p a (g n) -> p (a g) n", g=G), op0=ALU.add, op1=ALU.mult)\
                    .then_inc(s_t3_ready, 1)
                dve.wait_ge(s_t3_ready, t + 2)
                nc.vector.tensor_scalar(zero_fill[:, 0:N], score[:, 0:N], 0.0, FILL / Z_SCALE, ALU.is_equal, ALU.mult)\
                    .then_inc(s_nz_ready, 1)
                dve.wait_ge(s_nz_ready, t + 1)
                dve.nop(nofuse=True)
                nc.vector.tensor_tensor_reduce(out=score[:, 0:N], in0=score[:, 0:N], in1=zero_fill[:, 0:N], scale=1.0,
                                               scalar=-3.0e38, op0=ALU.add, op1=ALU.max, accum_out=m3)\
                    .then_inc(s_m3_ready, 1)
                dve.wait_ge(s_m3_ready, t + 1)
                nc.vector.tensor_scalar(nm3, m3, -Z_SCALE, None, ALU.mult).then_inc(s_nm3_ready, 1)

            def prob_low(t):
                dve.wait_ge(s_ph_ready, t + 1)
                nc.vector.scalar_tensor_tensor(out=prob_hl[:, 1, 0:N], in0=zero_fill[:, 0:N], scalar=SP_,
                                               in1=prob_hl[:, 0, 0:N], op0=ALU.mult, op1=ALU.subtract)\
                    .then_inc(s_pl_ready, 1)
                nc.vector.reciprocal(one(rz_all, t), z3).then_inc(s_rz3_step, 1)
                dve.wait_ge(s_rz3_step, t + 1)
                nc.vector.tensor_scalar(one(rz_all, t), one(rz_all, t), 1.0 / (SP_ * SW), None, ALU.mult)\
                    .then_inc(s_rz3_ready, 1)

            def turn(t):
                dve.wait_ge(s_pt_mm, 2 * t + 2)
                nc.vector.tensor_copy(turned(t % 2, 1), PS16[:, 5120:5120 + NP]).then_inc(s_pt_lo, 1)

            def finish(t):
                dve.wait_ge(s_o_mm, t + 1)
                dve.wait_ge(s_rz3_ready, t + 1)
                nc.vector.scalar_tensor_tensor(out=out_t, in0=PS[:, 7, :], scalar=one(rz_all, t), in1=bv_row[:, :],
                                               op0=ALU.mult, op1=ALU.add).then_inc(s_o_ready, 1)
                dve.wait_ge(s_o_ready, t + 1)
                nc.vector.scalar_tensor_tensor(out=row(X, t), in0=out_t, scalar=0.0, in1=row(X, t), op0=ALU.max,
                                               op1=ALU.add).then_inc(s_ln_r, 1)
                norm(3 * T + t, row(X, t)).then_inc(s_o_norm, 1)

            queries(0, 0, C)
            scores(0)
            queries(1, 0, 2)
            prob_low(0)
            queries(1, 2, C)
            turn(0)
            scores(1)
            queries(2, 0, 2)
            prob_low(1)
            queries(2, 2, C)
            with dve.Fori(2, T) as t:
                scores(t)
                turn(t - 1)
                prob_low(t)
                finish(t - 2)
            turn(T - 1)
            finish(T - 2)
            finish(T - 1)

        @block.tensor
        def _(pe):
            def turn_rows(t, at, hl):
                for i in range(2):
                    for c in range(C):
                        last = nc.tensor.transpose(PS16[:, at + (i * C + c) * P:at + (i * C + c + 1) * P],
                                                   hl[:, i, t, c * P:(c + 1) * P], ident[:, :])
                return last

            def turn_weight(hl, m, at):
                for i in range(2):
                    for c in range(C):
                        last = nc.tensor.transpose(PS16[:, at + (i * C + c) * P:at + (i * C + c + 1) * P],
                                                   hl[:, i, m, c * P:(c + 1) * P], ident[:, :])
                return last

            def turn_tile(slot):
                for i in range(2):
                    for c in range(C):
                        at = 2048 + slot * 1024 + (i * C + c) * P
                        last = nc.tensor.transpose(PS16[:, at:at + P], x_row(i, slot)[:, c * P:(c + 1) * P],
                                                   ident[:, :])
                return last

            def product(out, lhs, rhs, n):
                for k in range(n):
                    for j, (a, b) in enumerate(PAIRS):
                        last = nc.tensor.matmul(out, lhs(a, k), rhs(b, k), start=(k == 0 and j == 0),
                                                stop=(k == n - 1 and j == len(PAIRS) - 1))
                return last

            def graph_product(out, mat, t, rhs):
                for k in range(T):
                    for i in range(2):
                        last = nc.tensor.matmul(out, mat[:, k, ds(t * P, P)], rhs[:, i, k, :],
                                                start=(k == 0 and i == 0), stop=(k == T - 1 and i == 1))
                return last

            def bank(t, first=0):
                return PS[:, ds(first + t % 2, 1), :].rearrange("p a n -> p (a n)")

            pe.wait_ge(s_ident_ready, 1)
            for t in range(T):
                pe.wait_ge(s_x_lo, t + 1)
                pe.wait_ge(s_xt_out, t + 1)
                turn_rows(t, (t % 4) * 1024, UHL).then_inc(s_xt_mm, 1)
            pe.wait_ge(s_w0_lo, 1)
            for m in range(C):
                pe.wait_ge(s_w0_out, m + 1)
                turn_weight(w0_hl, m, 4096 + (m % 2) * 1024).then_inc(s_w0_mm, 1)
            pe.wait_ge(s_w0_out, 2 + C)
            pe.wait_ge(s_xt_out, 4 + T)
            with pe.Fori(0, C) as m:
                for n in range(G):
                    pe.wait_ge(s_kf_ready, G * m + n + 1)
                    product(PS[:, 2 + n, 0:GW], lambda i, c: WKT[:, i, c, ds(m * P, P)],
                            lambda i, c: XT[:, i, c, n * GW:(n + 1) * GW], C).then_inc(s_kp_mm, 1)
            pe.wait_ge(s_w0_lo, 2)
            pe.wait_ge(s_kf_ready, G * C + G)
            for m in range(C):
                pe.wait_ge(s_w0_out, C + m + 1)
                turn_weight(w0q_hl, m, 4096 + (m % 2) * 1024).then_inc(s_w0_mm, 1)
            pe.wait_ge(s_w0_out, 2 + 2 * C)
            pe.wait_ge(s_adj_in, 64)

            def turn_adj(t, at):
                for k in range(T):
                    last = nc.tensor.transpose(PS16[:, at + k * P:at + (k + 1) * P],
                                               A[:, t, k * P:(k + 1) * P], ident[:, :])
                last.then_inc(s_at_mm, 1)

            for j in range(T // 2):
                pe.wait_ge(s_at_v, j + 1)
                turn_adj(j * 2, 0)
                pe.wait_ge(s_at_a, j + 1)
                turn_adj(j * 2 + 1, 4096)
            pe.wait_ge(s_at_v, T // 2 + 1)
            turn_adj(T - 1, 0)
            pe.wait_ge(s_at_v, 1 + (T + 1) // 2)
            pe.wait_ge(s_at_a, 1 + T // 2)
            for b, mat in ((2, AT), (3, A)):
                for t in range(T):
                    for k in range(T):
                        last = nc.tensor.matmul(PS[:, b, t:t + 1], mat[:, k, t * P:(t + 1) * P], ones[:, 0:1],
                                                start=(k == 0), stop=(k == T - 1))
            last.then_inc(s_sums_mm, 1)
            def adj_x(t):
                pe.wait_ge(s_base_scaled, t + 1)
                graph_product(bank(t), AT, t, UHL).then_inc(s_prod_mm, 1)

            with pe.Fori(0, AHEAD) as t:
                adj_x(t)
            pe.wait_ge(s_const, 7)
            pe.wait_ge(s_act_ready, 1)
            pe.wait_ge(s_base_scaled, 2 + AHEAD)
            nc.tensor.matmul(PS[0:EC, 1, 0:P], act16[:, :], ones[0:EP, :], start=True, stop=True).then_inc(s_tot_mm, 1)
            nc.tensor.matmul(PS[0:EP, 0, 0:EC], before[0:EP, 0:EP], act16[:, :], start=True, stop=False)
            pe.wait_ge(s_tot_ready, 1)
            nc.tensor.matmul(PS[0:EP, 0, 0:EC], tot16[:, 0:EP], before[0:EC, 0:EC], start=False, stop=True)
            nc.tensor.matmul(PS[:, 2, 0:1], tot16[:, :], ones[0:EC, 0:1], start=True, stop=True).then_inc(s_rank_mm, 1)
            pe.wait_ge(s_n_ready, 1)
            many = pe.value_load(n_act[0:1, 0:1])

            def attend(r, between=False):
                pe.wait_ge(s_xc_lo, r + 1)
                for i in range(2):
                    for c in range(C):
                        last = nc.tensor.transpose(PS16[:, 7168 + (i * C + c) * P:7168 + (i * C + c + 1) * P],
                                                   xc_hl[:, i, c * P:(c + 1) * P], ident[:, :])
                last.then_inc(s_xct_mm, 1)
                if between:
                    adj_x(T - 3)
                pe.wait_ge(s_xct_out, r + 1)
                for m in range(C):
                    last = product(PS[:, 6, m * P:(m + 1) * P], lambda i, c: WQT[:, i, c, m * P:(m + 1) * P],
                                   lambda i, c: xct[:, i, c, :], C)
                last.then_inc(s_q_mm, 1)
                if between:
                    adj_x(T - 2)
                pe.wait_ge(s_q_lo, 2 * r + 2)
                pe.wait_ge(s_mask_ready, 2 * r + 2)
                for h in range(HEADS):
                    if between and h == 2:
                        adj_x(T - 1)
                    if h >= 2:
                        pe.wait_ge(s_t_ready, HEADS * r + h - 1)
                    for n in range(G):
                        out, cols = PS[:, 2 + G * (h % 2) + n, 0:GW], slice(n * GW, (n + 1) * GW)
                        nc.tensor.matmul(out, identb[:, :], bmask[:, cols], start=True, stop=False)
                        for j, (a, b) in enumerate(PAIRS):
                            last = nc.tensor.matmul(out, q_hl[:, a, h, :], KT[:, b, h // 2, cols],
                                                    start=False, stop=(j == len(PAIRS) - 1))
                    last.then_inc(s_s_mm, 1)
                for i, ready in enumerate((s_f_hi, s_f_lo)):
                    pe.wait_ge(s_f_pad, r + 1)
                    pe.wait_ge(ready, r + 1)
                    for k in range(T):
                        at = 2048 * (i + 1) + k * P
                        last = nc.tensor.transpose(PS16[:, at:at + P], f_hl[:, i, k * P:(k + 1) * P], ident[:, :])
                    last.then_inc(s_ft_mm, 1)
                if between:
                    pe.wait_ge(s_r1_free, 1)
                    for t in range(T):
                        last = nc.tensor.matmul(PS[:, 1, t:t + 1], put_hot[:, t * P:(t + 1) * P], ones[:, 0:1],
                                                start=True, stop=True)
                    last.then_inc(s_has_mm, 1)
                pe.wait_ge(s_ft_hi, r + 1)
                for a, b in PAIRS:
                    if a == 1:
                        pe.wait_ge(s_ft_lo, r + 1)
                    for k in range(T):
                        last = nc.tensor.matmul(PS[:, 0, :], f_t[:, a, k, :], UHL[:, b, k, :],
                                                start=((a, b) == PAIRS[0] and k == 0),
                                                stop=((a, b) == PAIRS[-1] and k == T - 1))
                last.then_inc(s_y_mm, 1)

            def layer1_start(put):
                for k in range(-4, T):
                    if put and k + 4 < T:
                        if k >= -2:
                            pe.wait_ge(s_placed, k + 3)
                        for i in range(2):
                            last = nc.tensor.matmul(PS[:, k % 2, :], put_hot[:, (k + 4) * P:(k + 5) * P],
                                                    y_hl[:, i, :], start=(i == 0), stop=(i == 1))
                        last.then_inc(s_put_mm, 1)
                    if k < 0:
                        continue
                    if k < SYM_POOL:
                        pe.wait_ge(s_sym_ready, k + 1)
                    else:
                        pe.wait_ge(s_sym_v, 2 * (k - SYM_POOL) + 2)
                    pe.wait_ge(s_u_lo, k + 1)
                    for t in range(W1_AT_ONCE):
                        for i in range(2):
                            last = nc.tensor.matmul(PS[:, w1_bank(t), :], SYM[:, k, t * P:(t + 1) * P],
                                                    UHL[:, i, k, :], start=(k == 0 and i == 0),
                                                    stop=(k == T - 1 and i == 1))
                        if k == T - 1:
                            last.then_inc(s_prod_mm, 1)

            with pe.If(many > P):
                pe.wait_ge(s_rank_ready, 1)
                with pe.Fori(AHEAD, T) as t:
                    adj_x(t)
                pe.sem_inc(s_hots_free, 2)

                def relations(t, j, first=False, end=False):
                    for i in range(2):
                        pe.wait_ge(s_hots_obj, t * EC + j * 2 + i + 1)
                        for n in range(G):
                            last = nc.tensor.matmul(PS[:, 2 + n, 0:GW], all_sub[i][0:EP, :],
                                                    all_obj[i][0:EP, n * GW:(n + 1) * GW],
                                                    start=(first and i == 0), stop=(end and i == 1))
                        last.then_inc(s_hots_free, 1)
                    if end:
                        return last

                with pe.Fori(0, T) as t:
                    relations(t, 0, first=True)
                    with pe.Fori(1, EC // 2 - 1) as j:
                        relations(t, j)
                    relations(t, EC // 2 - 1, end=True)
                    pe.wait_ge(s_hots_free, (t + 1) * EC + 2)
                    nc.tensor.matmul(PS[:, 5, 0:1], ident[:, :], ones[:, 0:1], start=True, stop=True)\
                        .then_inc(s_w_mm, 1)
                    attend(t)
                layer1_start(put=False)
            with pe.Else():
                for k in range(EC // OC):
                    if k % 2 == 0 and k // 2 < T - AHEAD - 6:
                        adj_x(AHEAD + k // 2)
                    pe.wait_ge(s_hot_ready, k + 1)
                    for i in range(OC):
                        e = k * OC + i
                        last = nc.tensor.matmul(PS[:, 5, 0:2], hot[k % 2][0:EP, i, :], pair[:, e, :], start=(e == 0),
                                                stop=(e == EC - 1))
                    last.then_inc(s_slots_mm, 1)
                pe.wait_ge(s_sub_ready, 1)
                nc.tensor.matmul(PS[:, 6, 0:P], sub_b, ident[:, :], start=True, stop=True).then_inc(s_sub_mm, 1)
                adj_x(T - 6)
                pe.wait_ge(s_obj_ready, 1)
                pe.wait_ge(s_same_ready, 1)
                for n in range(G):
                    last = nc.tensor.matmul(PS[:, 2 + n, 0:GW], same, obj_hot[:, n * GW:(n + 1) * GW], start=True,
                                            stop=True)
                last.then_inc(s_w_mm, 1)
                adj_x(T - 5)
                adj_x(T - 4)
                attend(0, between=True)
                pe.wait_ge(s_has_ready, 1)
                pe.wait_ge(s_y_lo, 1)
                layer1_start(put=True)

            for t in range(W1_AT_ONCE, T):
                if t >= W1_AT_ONCE + 2:
                    pe.wait_ge(s_w1_lo, t - 1)
                graph_product(PS[:, w1_bank(t), :], SYM, t, UHL).then_inc(s_prod_mm, 1)
            pe.wait_ge(s_wst_lo, 6)
            pe.wait_ge(s_w1_lo, W1_AT_ONCE)
            for d in range(C):
                if d >= 2:
                    pe.wait_ge(s_g_lo, d - 1)
                product(PS[:, 2 + d % 2, :], lambda i, c: wq3_hl[:, i, c, d * P:(d + 1) * P],
                        lambda i, c: wk3_hl[:, i, c, :], C).then_inc(s_g_mm, 1)
            pe.wait_ge(s_bkb_ready, 2 * C)
            product(PS[:, 4, :], lambda i, c: bk_b[:, i, c, :], lambda i, c: wq3_hl[:, i, c, :], C)
            for m in range(C):
                product(PS[:, 5, m:m + 1], lambda i, c: wk3_hl[:, i, c, m * P:(m + 1) * P],
                        lambda i, c: b_hl[:, i, C + c:C + c + 1], C)
            product(PS[:, 5, C:C + 1], lambda i, c: bk_b[:, i, c, :], lambda i, c: b_hl[:, i, C + c:C + c + 1], C)\
                .then_inc(s_vec_mm, 1)
            pe.wait_ge(s_wv_lo, 1)
            for m in range(C):
                if m >= 2:
                    pe.wait_ge(s_wvt_out, m - 1)
                turn_weight(wv_hl, m, 6144 + (m % 2) * 1024).then_inc(s_wvt_mm, 1)
            pe.wait_ge(s_w1_lo, T)
            pe.wait_ge(s_g_lo, C)
            pe.wait_ge(s_vec_out, 3)
            pe.wait_ge(s_wvt_out, C)

            def adj_product(n, t, slot, late=False):
                pe.wait_ge(s_ln_r, n * T + t - 1)
                rhs = VHL if n == 1 else SHL
                for k in range(T):
                    if late and k == T - 1:
                        pe.wait_ge(s_rows_lo, 2 + T)
                    for i in range(2):
                        last = nc.tensor.matmul(PS[:, slot, :], AT[:, k, ds(t * P, P)], rhs[:, i, k, :],
                                                start=(k == 0 and i == 0), stop=(k == T - 1 and i == 1))
                last.then_inc(s_prod_mm, 1)

            def turn_step(n, t, slot):
                pe.wait_ge(s_x_lo, n * T + t + 1)
                pe.wait_ge(s_xt_out, n * (T + 2) + 2 + t + 1)
                turn_tile(slot).then_inc(s_xt_mm, 1)

            def rows_step(n, t, slot):
                pe.wait_ge(s_xt_out, n * (T + 2) + 4 + t + 1)
                pe.wait_ge(s_rows_lo, (n - 1) * T + t + 1)
                weight = W2HL if n == 1 else WVT
                product(PS[:, 4 + slot, :], lambda i, c: XT[:, i, c, ds(t * P, P)], lambda i, c: weight[:, i, c, :], C)\
                    .then_inc(s_rows_mm, 1)

            for n in (1, 2):
                if n == 2:
                    pe.wait_ge(s_rows_lo, 1 + T)
                adj_product(n, 0, 0, late=(n == 2))
                adj_product(n, 1, 1)
                adj_product(n, 2, 0)
                turn_step(n, 0, 0)
                with pe.Fori(1, T // 2) as j:
                    adj_product(n, 2 * j + 1, 1)
                    turn_step(n, 2 * j - 1, 1)
                    rows_step(n, 2 * j - 2, 0)
                    adj_product(n, 2 * j + 2, 0)
                    turn_step(n, 2 * j, 0)
                    rows_step(n, 2 * j - 1, 1)
                turn_step(n, T - 2, 1)
                rows_step(n, T - 3, 0)
                rows_step(n, T - 2, 1)
                turn_step(n, T - 1, 0)
                rows_step(n, T - 1, 0)

            def queries(n):
                with pe.Fori(0, C) as m:
                    pe.wait_ge(s_qf_ready, C * n + m + 1)
                    product(PS[:, ds(6 + m % 2, 1), 0:GW].rearrange("p a n -> p (a n)"),
                            lambda i, c: GHL[:, i, c, ds(m * P, P)],
                            lambda i, c: XT[:, i, c, n * GW:(n + 1) * GW], C).then_inc(s_qt_mm, 1)

            def scores(t):
                pe.wait_ge(s_t3_ready, t + 1)
                for n in range(G):
                    last = product(PS[:, n, 0:GW], lambda i, c: QT[:, i, c, ds(t * P, P)],
                                   lambda i, c: XT[:, i, c, n * GW:(n + 1) * GW], C)
                last.then_inc(s_z_mm, 1)

            def turn(t):
                for i, ready, read in ((0, s_ph_ready, s_pt_hi), (1, s_pl_ready, s_pt_lo)):
                    pe.wait_ge(ready, t + 1)
                    if not isinstance(t, int) or t > 0:
                        pe.wait_ge(read, t)
                    for k in range(T):
                        at = 3072 + 2048 * i + k * P
                        last = nc.tensor.transpose(PS16[:, at:at + P], prob_hl[:, i, k * P:(k + 1) * P], ident[:, :])
                    last.then_inc(s_pt_mm, 1)

            def attend3(t):
                pe.wait_ge(s_pt_hi, t + 1)
                pe.wait_ge(s_pt_lo, t + 1)
                if not isinstance(t, int) or t > 0:
                    pe.wait_ge(s_o_ready, t)
                product(PS[:, 7, :], lambda i, k: turned(t % 2, i)[:, k * P:(k + 1) * P],
                        lambda i, k: VHL[:, i, k, :], T).then_inc(s_o_mm, 1)

            queries(0)
            pe.wait_ge(s_pad3, 2)
            pe.wait_ge(s_qt_done, 2 + C)
            scores(0)
            queries(1)
            pe.wait_ge(s_qf_ready, 2 + 2 * C)
            turn(0)
            scores(1)
            pe.wait_ge(s_pt_lo, 1)
            queries(2)
            pe.wait_ge(s_qf_ready, 2 + 3 * C)
            pe.wait_ge(s_qt_done, 2 + 3 * C)
            pe.wait_ge(s_rows_lo, 2 * T + 2)
            with pe.Fori(2, T) as t:
                scores(t)
                turn(t - 1)
                attend3(t - 2)
            attend3(T - 2)
            turn(T - 1)
            attend3(T - 1)



_INS = ["x", "adj", "L0_gnn_rel_pair_index", "L0_gnn_Wq", "L0_gnn_bq", "L0_gnn_Wk", "L0_gnn_bk", "L2_gnn_weight",
        "L2_gnn_bias", "L3_gnn_W_q", "L3_gnn_b_q", "L3_gnn_W_k", "L3_gnn_b_k", "L3_gnn_W_v", "L3_gnn_b_v"]


def kernel(**inputs):
    import numpy as _np
    import concourse.bacc as _bacc
    from concourse import mybir as _mybir
    from concourse.bass_utils import run_bass_kernel_spmd as _run

    nc = _bacc.Bacc("TRN2", target_bir_lowering=False, num_devices=1)
    arrays, args = {}, []
    for name in _INS:
        a = _np.ascontiguousarray(inputs[name])
        arrays[f"in_{name}"] = a
        args.append(nc.dram_tensor(f"in_{name}", a.shape, _mybir.dt.from_np(a.dtype), kind="ExternalInput").ap())
    args.append(nc.dram_tensor("out_0", (N, D), F32, kind="ExternalOutput").ap())
    build(nc, *args)
    r = _run(nc, [arrays], core_ids=[0])
    return r.results[0]["out_0"]
```

```python
from contextlib import ExitStack

import concourse.bass as bass
from concourse import mybir

ALU = mybir.AluOpType
ACT = mybir.ActivationFunctionType
F32 = mybir.dt.float32
F16 = mybir.dt.float16
BF16 = mybir.dt.bfloat16
I32 = mybir.dt.int32
U32 = mybir.dt.uint32
ds = bass.ds

P = 128
N = 1354
D = 512
T = -(-N // P)
NP = T * P
TAIL = N - (T - 1) * P
C = D // P
G = 3
GW = 452
NG = G * GW
HEADS = 8
E = 10000
EP, EC = 125, 80
OC = 16

SX = 256.0
SW0 = 64.0
SK = 16.0
SW = 1024.0
SP_ = 4096.0
SB = 16.0
EPS = 1e-5
DIAG = 1e-7
E_DIAG = 0.9999999
OFF = 1e30
FAR = 8.0e6
FILL = -10000.0
ADJ_FIRST = 7
XG = -(-T // C)
AHEAD = 5
SYM_FIRST = 7
EARLY = 4 * OC
W1_AT_ONCE = 6
Z_SCALE = float(D) ** -0.5 / (SX * SW)



def build(nc, x_d, adj_d, rel_d, wq0_d, bq0_d, wk0_d, bk0_d, w2_d, b2_d, wq3_d, bq3_d, wk3_d, bk3_d,
          wv3_d, bv3_d, out_d):
    ctx = ExitStack()
    with ctx:
        def sb(name, shape, dt):
            return ctx.enter_context(nc.sbuf_tensor(name, shape, dt))

        def sem(name):
            return ctx.enter_context(nc.semaphore(name))

        A = sb("A", [P, T, NP], F16)
        AT = sb("AT", [P, T, NP], F16)
        X = sb("X", [P, T, D], F32)
        R1 = sb("R1", [P, T * NP], F16)
        R2 = sb("R2", [P, 2 * T * D], F16)
        R3 = sb("R3", [P, 2 * T * D], F16)
        R4 = sb("R4", [P, 2 * C * NP], F16)
        WA = sb("WA", [P, 2 * C * D], F16)
        WB = sb("WB", [P, 2 * C * D], F16)

        ident = sb("ident", [P, P], F16)
        iota = sb("iota", [P, NP], F16)
        before = sb("before", [P, P], F16)
        after = sb("after", [P, P], F16)
        ones = sb("ones", [P, P], F16)
        rel = sb("rel", [EP, 2 * EC], I32)
        subf = sb("subf", [EP, EC], F32)
        objf = sb("objf", [EP, EC], F32)
        bad = sb("bad", [EP, EC], F32)
        rel_ix = sb("rel_ix", [EP, EC], U32)
        hit = sb("hit", [EP, EC], F32)
        act16 = sb("act16", [EP, EC], F16)
        rank = sb("rank", [EP, EC], F32)
        pair = sb("pair", [EP, EC, 2], F16)
        tot16 = sb("tot16", [P, P], F16)
        row_n16 = sb("row_n16", [P, T], F16)[:, :]
        n_act = sb("n_act", [1, 1], I32)
        small = sb("small", [P, 360], F32)
        slot_ix = sb("slot_ix", [P, 1], U32)
        b_hl = sb("b_hl", [P, 2, 2 * C], F16)
        obj_ix = sb("obj_ix", [P, 1], U32)
        w_hl = sb("w_hl", [P, 4], F16)
        d_hl = sb("d_hl", [P, 2 * HEADS], F16)
        identf = sb("identf", [P, P], F32)

        PS = ctx.enter_context(nc.psum_tensor("PS", [P, 8, 512], F32))
        PS16 = PS[:, :, :].rearrange("p b n -> p (b n)").bitcast(F16)

        n_cols = [0]

        def cols(n=1):
            n_cols[0] += n
            return small[:, n_cols[0] - n:n_cols[0]]

        bk0, bq0, bk3, bq3, c2 = (cols(C) for _ in range(5))
        mx, nb, zs, em, rz, g_tmp = (cols(HEADS) for _ in range(6))
        slot_row, slot_obj, slot_far, slot_low, rep, g_sum, row_id = (cols() for _ in range(7))
        beta, r_acc, r3, m3, nm3, z3 = (cols() for _ in range(6))
        row_n, col_n, c_a, c_b, nohas, dinv, dinv_half, dinv_s, mhalfs, rz_all = (cols(T) for _ in range(10))
        ln_st, ln_mv, ln_var, ln_rstd = cols(6), cols(2), cols(), cols()
        att, zs2, args, p_em = cols(HEADS), cols(2 * HEADS), cols(2 * HEADS), cols(2 * HEADS)
        em_d = cols(2 * HEADS).rearrange("p (a h) -> p a h", a=2)
        weights, first, row_sum, obj_weight = cols(2), cols(), cols(), cols()
        has = cols(3 * T).rearrange("p (t n) -> p t n", n=3)
        mv_all = cols(2 * T).rearrange("p (t two) -> p t two", two=2)
        var_all, rstd_all = cols(T), cols(T)

        def parts(region, at, *shape):
            n = 1
            for k in shape:
                n *= k
            v = region[:, at:at + n]
            if len(shape) == 2:
                return v.rearrange("p (a b) -> p a b", a=shape[0])
            if len(shape) == 3:
                return v.rearrange("p (a b c) -> p a b c", a=shape[0], b=shape[1])
            return v

        def words(region, at, *shape):
            n = 2
            for k in shape:
                n *= k
            v = region[:, 2 * at:2 * at + n].bitcast(F32)
            if len(shape) == 2:
                return v.rearrange("p (a b) -> p a b", a=shape[0])
            return v

        def flat(v):
            return v.rearrange("p a b -> p (a b)")

        KT = parts(R1, 0, 2, C, NG)
        kf = words(R1, 5424, G, GW)
        bmask = R1[:, 10848:10848 + NG].bitcast(BF16)
        wmask = parts(R1, 12204, NG)
        identb = parts(R1, 13560, P).bitcast(BF16)
        SYM = parts(R1, 0, T, NP)
        XHL = R1[:, 0:4 * D].rearrange("p (s h n) -> p s h n", s=2, h=2)
        b2_row = words(R1, 2 * D, D)
        WVT = parts(R1, 2 * T * D, 2, C, D)
        score = words(R1, 0, NG)
        zero_fill = words(R1, NG, NG)
        prob_hl = parts(R1, 4 * NG, 2, NP)
        prob_t = R1[:, 4 * NG + 2 * NP:4 * NG + 6 * NP].rearrange("p (s h n) -> p s h n", s=2, h=2)
        UHL = parts(R2, 0, 2, T, D)
        wv_f = words(R2, 0, C, D)
        wv_hl = parts(R2, 4096, 2, C, D)
        SHL = parts(R2, 0, 2, T, D)
        a_row, bv_row = sb("a_row", [P, D], F32), sb("bv_row", [P, D], F32)
        out_t = words(R2, 0, D)
        wk0_f = words(R3, 0, C, D)
        w0_hl = parts(R3, 4096, 2, C, D)
        BASE = words(R3, 0, T, D)
        bq0_row, bk0_row = bv_row[:, :], BASE[:, T - 1, :]
        spare = nc.dram_tensor("spare", (P, 2 * C * D), F16, kind="Internal").ap()
        VHL = parts(R3, 0, 2, T, D)
        wq0_f = words(AT[:, :, :].rearrange("p a b -> p (a b)"), 0, C, D)
        w0q_hl = parts(AT[:, :, :].rearrange("p a b -> p (a b)"), 4096, 2, C, D)
        XT = parts(R4, 0, 2, C, NP)
        prob = [words(R4, NG * i, NG) for i in range(3)]
        fsum = words(R4, 3 * NG, NG)
        sub_b = parts(R4, 8 * NG, P)
        all_same = parts(R4, 8 * NG + P, P)
        adj_c = prob[1]
        qf0 = words(R4, 0, C, P)
        x_c = words(R4, 2 * NG, D)
        f_hl = parts(R4, 0, 2, NP)
        f_t = parts(R4, 2 * NP, 2, T, P)
        all_sub = [sub_b, all_same]
        all_obj = [parts(R4, 0, NG), parts(R4, NG, NG)]
        hot = [parts(R4, 6144 + 2048 * i, OC, P) for i in range(2)]
        hot_down = parts(R4, 8192, T, P)
        pair_x = words(R4, 2048, 2, D)
        pair_hl = parts(R4, 6144, 2, 2, D)
        pair_t = parts(R4, 8192, 2, 2 * C * P)
        pair_q, pair_k = words(R4, 3072, D), words(R4, 3584, D)
        att_b = words(R4, 4096, HEADS, P)
        att_row = words(R4, 3072, HEADS, P)
        other_row = words(R4, 5120, P)
        same, same_pair = parts(R4, 10496, P), parts(R4, 10624, P)
        row_b, obj_b = before[:, :], tot16[:, :]
        unused = parts(R4, 4096, 5, NP)
        g_bank = (6, 7, 2, 3)
        wq3_hl = parts(R1, 0, 2, C, D)
        wk3_hl = parts(R1, 4096, 2, C, D)
        bk_b = parts(R1, 12288, 2, C, P)
        WKT = parts(WA, 0, 2, C, D)
        WQT = parts(WB, 0, 2, C, D)
        q_hl = parts(WA, 0, 2, HEADS, P)
        q_lanes = [(slice(64 * i, 64 * i + 64),
                    q_hl[64 * i:64 * i + 64].rearrange("p a (m two) n -> p a m two n", two=2)[:, :, :, i, :])
                   for i in range(2)]
        xc_hl = parts(WA, 2048, 2, D)
        xct = parts(WA, 3072, 2, C, P)
        row_hot = parts(WA, 0, NP)
        put_hl = parts(WA, NP, 2, D)
        put_hot = parts(WB, 0, NP)
        W2HL = parts(WA, 0, 2, C, D)
        GHL = parts(R4, 0, 2, C, D)
        GW3 = parts(WB, 0, 2, C, D)

        def w_stage(n):
            return words(R1, 4096 + 1024 * (n % 2), 2, D) if n < 4 else words(R4, 2048 + 1024 * (n % 2), 2, D)

        def staged(n, i):
            return (wq3_hl, wk3_hl, W2HL)[n // 2][:, i, 2 * (n % 2):2 * (n % 2) + 2, :]

        ATF = AT[:, :, :].rearrange("p a b -> p (a b)")
        QT = parts(ATF, 0, 2, C, NP)
        qf = words(R2, C * D, 2, GW)

        s_rel_in = sem("rel_in")
        s_wk0_in = sem("wk0_in")
        s_wq0_in = sem("wq0_in")
        s_wst_in0 = sem("wst_in0")
        s_wst_in1 = sem("wst_in1")
        s_b_in = sem("b_in")
        s_wst_lo = sem("wst_lo")
        s_x_in0 = sem("x_in0")
        s_x_in = sem("x_in")
        s_blank = sem("blank")
        s_all_done = sem("all_done")
        s_g_lo = sem("g_lo")
        s_moved = sem("moved")
        s_prod_mm = sem("prod_mm")
        s_b3_in = sem("b3_in")
        s_o_norm = sem("o_norm")
        s_stored = sem("stored")
        s_adj_in0 = sem("adj_in0")
        s_adj_in1 = sem("adj_in1")
        s_ident_ready = sem("ident_ready")
        s_const = sem("const")
        s_ix_ready = sem("ix_ready")
        s_hit_in0 = sem("hit_in0")
        s_hit_in1 = sem("hit_in1")
        s_deg_ready = sem("deg_ready")
        s_dinv_ready = sem("dinv_ready")
        s_gathered = sem("gathered")
        s_ln_v = sem("ln_v")
        s_ln_rstd = sem("ln_rstd")
        s_n_ready = sem("n_ready")
        s_saved = sem("saved")
        s_slots_ready = sem("slots_ready")
        s_slot_fill = sem("slot_fill")
        s_put_done = sem("put_done")
        s_placed = sem("placed")
        s_closed = sem("closed")
        s_summed = sem("summed")
        s_wst_hi = sem("wst_hi")
        s_w0_hi = sem("w0_hi")
        s_at_a = sem("at_a")
        s_at_mm = sem("at_mm")
        s_g_mm = sem("g_mm")
        s_g_hi = sem("g_hi")
        s_x_hi = sem("x_hi")
        s_vec_mm = sem("vec_mm")
        s_vec_out = sem("vec_out")
        s_base_out = sem("base_out")
        s_rows_summed = sem("rows_summed")
        s_xc_hi = sem("xc_hi")
        s_xct_mm = sem("xct_mm")
        s_xct_out = sem("xct_out")
        s_q_mm = sem("q_mm")
        s_q_full = sem("q_full")
        s_nb_ready = sem("nb_ready")
        s_p_ready = sem("p_ready")
        s_em_ready = sem("em_ready")
        s_f_step = sem("f_step")
        s_f_hi = sem("f_hi")
        s_ft_mm = sem("ft_mm")
        s_ft_hi = sem("ft_hi")
        s_ln_x = sem("ln_x")
        s_u_hi = sem("u_hi")
        s_xt_out = sem("xt_out")
        s_xt_mm = sem("xt_mm")
        s_kf_ready = sem("kf_ready")
        s_bias0 = sem("bias0")
        s_kp_mm = sem("kp_mm")
        s_kt_done = sem("kt_done")
        s_arg_ready = sem("arg_ready")
        s_weight_ready = sem("weight_ready")
        s_y_hi = sem("y_hi")
        s_has_ready = sem("has_ready")
        s_w1_hi = sem("w1_hi")
        s_wv_hi = sem("wv_hi")
        s_qf_ready = sem("qf_ready")
        s_qt_mm = sem("qt_mm")
        s_qt_done = sem("qt_done")
        s_rows_mm = sem("rows_mm")
        s_rows_hi = sem("rows_hi")
        s_nm3_ready = sem("nm3_ready")
        s_p3_ready = sem("p3_ready")
        s_pt_mm = sem("pt_mm")
        s_ph_ready = sem("ph_ready")
        s_o_mm = sem("o_mm")
        s_pt_hi = sem("pt_hi")
        s_w0_out = sem("w0_out")
        s_at_v = sem("at_v")
        s_step = sem("step")
        s_w0_lo = sem("w0_lo")
        s_w0_mm = sem("w0_mm")
        s_bkb_ready = sem("bkb_ready")
        s_x_lo = sem("x_lo")
        s_sym_sum = sem("sym_sum")
        s_sym_ready = sem("sym_ready")
        s_act_ready = sem("act_ready")
        s_tot_mm = sem("tot_mm")
        s_tot_ready = sem("tot_ready")
        s_rank_mm = sem("rank_mm")
        s_rank_ready = sem("rank_ready")
        s_slots_mm = sem("slots_mm")
        s_hot_ready = sem("hot_ready")
        s_dinv_s_ready = sem("dinv_s_ready")
        s_w_mm = sem("w_mm")
        s_w_step = sem("w_step")
        s_mask_ready = sem("mask_ready")
        s_xc_lo = sem("xc_lo")
        s_q_hi = sem("q_hi")
        s_q_lo = sem("q_lo")
        s_z_ready = sem("z_ready")
        s_s_mm = sem("s_mm")
        s_t_ready = sem("t_ready")
        s_f_pad = sem("f_pad")
        s_g_step = sem("g_step")
        s_f_lo = sem("f_lo")
        s_ft_lo = sem("ft_lo")
        s_put_mm = sem("put_mm")
        s_ln_s = sem("ln_s")
        s_ln_m = sem("ln_m")
        s_u_lo = sem("u_lo")
        s_kh_done = sem("kh_done")
        s_all_step = sem("all_step")
        s_slot_step = sem("slot_step")
        s_hots_free = sem("hots_free")
        s_hots_made = sem("hots_made")
        s_y_mm = sem("y_mm")
        s_all_res = sem("all_res")
        s_sub_ready = sem("sub_ready")
        s_sub_mm = sem("sub_mm")
        s_same_ready = sem("same_ready")
        s_row_ready = sem("row_ready")
        s_row_mm = sem("row_mm")
        s_xct_lo = sem("xct_lo")
        s_pair_step = sem("pair_step")
        s_attb_ready = sem("attb_ready")
        s_put_ready = sem("put_ready")
        s_att_mm = sem("att_mm")
        s_d_ready = sem("d_ready")
        s_sum_mm = sem("sum_mm")
        s_y_lo = sem("y_lo")
        s_has_mm = sem("has_mm")
        s_ln_r = sem("ln_r")
        s_w1_lo = sem("w1_lo")
        s_wv_lo = sem("wv_lo")
        s_wvt_mm = sem("wvt_mm")
        s_wvt_out = sem("wvt_out")
        s_rows_lo = sem("rows_lo")
        s_x3_add = sem("x3_add")
        s_qh_done = sem("qh_done")
        s_pad3 = sem("pad3")
        s_t3_ready = sem("t3_ready")
        s_r_step = sem("r_step")
        s_z_mm = sem("z_mm")
        s_m3_ready = sem("m3_ready")
        s_pl_ready = sem("pl_ready")
        s_rz3_ready = sem("rz3_ready")
        s_pt_lo = sem("pt_lo")
        s_o_ready = sem("o_ready")
        block = ctx.enter_context(nc.Block())

        def row(buf, t):
            return buf[:, ds(t, 1), :].rearrange("p a n -> p (a n)")

        def part_row(buf, i, t):
            return buf[:, i, ds(t, 1), :].rearrange("p a n -> p (a n)")

        def one(c, t):
            return c[:, ds(t, 1)]

        def x_row(i, slot):
            return XHL[:, slot, i, :]

        def turned(slot, i):
            return prob_t[:, ds(slot, 1), i, :].rearrange("p a n -> p (a n)")

        def at_bank(t):
            return 4096 * (t % 2) + 2048 * (t // 2 % 2)

        def w1_bank(t):
            return 2 + t if t < W1_AT_ONCE else t % 2


        PAIRS = ((0, 0), (0, 1), (1, 0))

        @block.sync
        def _(sp):
            sp.dma_start(rel[:, :], rel_d.rearrange("(p i) two -> p (i two)", p=EP)).then_inc(s_rel_in, 16)
            sp.dma_start(wk0_f, wk0_d.rearrange("(m p) d -> p m d", p=P)).then_inc(s_wk0_in, 16)
            sp.dma_start(wq0_f, wq0_d.rearrange("(m p) d -> p m d", p=P)).then_inc(s_wq0_in, 16)
            def stage(n, src):
                i = n % 2
                sp.dma_start(w_stage(n), src[i * 2 * P:(i + 1) * 2 * P].rearrange("(m p) d -> p m d", p=P))\
                    .then_inc((s_wst_in0, s_wst_in1)[i], 16)

            stage(0, wq3_d)
            stage(1, wq3_d)
            for dst, src in ((bk0, bk0_d), (bq0, bq0_d), (bk3, bk3_d), (bq3, bq3_d)):
                sp.dma_start(dst, src.rearrange("(m p) -> p m", p=P),
                             allow_slow_non_contiguous=True).then_inc(s_b_in, 16)
            for dst, src in ((bq0_row, bq0_d), (bk0_row, bk0_d)):
                sp.dma_start(dst, src.rearrange("(o n) -> o n", o=1).to_broadcast([P, D])).then_inc(s_b_in, 16)
            for n in (2, 3):
                sp.wait_ge(s_wst_lo, n - 1)
                stage(n, wk3_d)
            half = (T - 1) // 2
            sp.dma_start(X[:, 0:half, :], x_d[0:half * P].rearrange("(t p) d -> p t d", p=P)).then_inc(s_x_in0, 16)
            sp.dma_start(X[:, half:T - 1, :],
                         x_d[half * P:(T - 1) * P].rearrange("(t p) d -> p t d", p=P)).then_inc(s_x_in, 16)
            sp.wait_ge(s_blank, 1)
            sp.dma_start(X[0:TAIL, T - 1, :], x_d[(T - 1) * P:N]).then_inc(s_x_in, 16)
            sp.wait_ge(s_all_done, 1)
            sp.wait_ge(s_g_lo, C)
            sp.dma_start(WB[:, :], R4[:, 0:2 * C * D]).then_inc(s_moved, 16)
            stage(4, w2_d)
            stage(5, w2_d)
            sp.wait_ge(s_moved, 16)
            sp.wait_ge(s_prod_mm, 2 * T)
            sp.dma_start(wv_f, wv3_d.rearrange("(m p) d -> p m d", p=P)).then_inc(s_moved, 16)
            for dst, src in ((b2_row, b2_d), (bv_row[:, :], bv3_d)):
                sp.dma_start(dst, src.rearrange("(o n) -> o n", o=1).to_broadcast([P, D])).then_inc(s_b3_in, 16)
            with sp.Fori(0, T - 1) as t:
                sp.wait_ge(s_o_norm, t + 1)
                sp.dma_start(out_d[ds(t * P, P)], row(X, t)).then_inc(s_stored, 16)
            sp.wait_ge(s_o_norm, T)
            sp.dma_start(out_d[(T - 1) * P:N], X[0:TAIL, T - 1, :]).then_inc(s_stored, 16)
            sp.wait_ge(s_stored, 16 * T)

        @block.gpsimd
        def _(pool):
            nc.gpsimd.memset(X[:, T - 1, :], 0.0).then_inc(s_blank, 1)
            nc.gpsimd.memset(A[:, T - 1, :], 0.0).then_inc(s_blank, 1)
            nc.gpsimd.memset(A[:, 0:T - 1, N:NP], 0.0).then_inc(s_blank, 1)
            pool.wait_ge(s_blank, 3)
            for a, b in ((0, 4), (4, ADJ_FIRST), (ADJ_FIRST, T - 1)):
                pool.dma_start(A[:, a:b, 0:N], adj_d[a * P:b * P].rearrange("(t p) n -> p t n", p=P))\
                    .then_inc(s_adj_in0 if b <= ADJ_FIRST else s_adj_in1, 16)
            pool.dma_start(A[0:TAIL, T - 1, 0:N], adj_d[(T - 1) * P:N]).then_inc(s_adj_in1, 16)
            nc.gpsimd.memset(ident[:, :], 0.0).then_inc(s_blank, 1)
            nc.gpsimd.memset(ones[:, :], 1.0).then_inc(s_blank, 1)
            pool.wait_ge(s_blank, 5)
            nc.gpsimd.affine_select(out=ident[:, :], in_=ident[:, :], compare_op=ALU.not_equal, fill=1.0, base=0,
                                    pattern=[[-1, P]], channel_multiplier=1).then_inc(s_ident_ready, 1)
            nc.gpsimd.iota(iota[:, 0:P], [[1, P]], channel_multiplier=0,
                           allow_small_or_imprecise_dtypes=True).then_inc(s_const, 1)
            nc.gpsimd.affine_select(out=before[:, :], in_=ones[:, :], compare_op=ALU.is_gt, fill=0.0, base=0,
                                    pattern=[[1, P]], channel_multiplier=-1).then_inc(s_const, 1)
            nc.gpsimd.affine_select(out=after[:, :], in_=ones[:, :], compare_op=ALU.is_gt, fill=0.0, base=0,
                                    pattern=[[-1, P]], channel_multiplier=1).then_inc(s_const, 1)
            nc.gpsimd.iota(row_id, [[0, 1]], channel_multiplier=1,
                           allow_small_or_imprecise_dtypes=True).then_inc(s_const, 1)
            nc.gpsimd.memset(mhalfs, -0.5).then_inc(s_const, 1)
            pool.wait_ge(s_ix_ready, 1)
            for i in range(EC):
                nc.gpsimd.indirect_dma_start(
                    out=hit[:, i:i + 1], out_offset=None, in_=adj_d.rearrange("a (b o) -> (a b) o", o=1),
                    in_offset=bass.IndirectOffsetOnAxis(ap=rel_ix[:, i:i + 1], axis=0),
                    bounds_check=N * N - 1, oob_is_err=False).then_inc(s_hit_in0 if i < EARLY else s_hit_in1, 16)
            pool.wait_ge(s_deg_ready, 1)
            pool.wait_ge(s_const, 5)
            nc.gpsimd.tensor_tensor(dinv, dinv, mhalfs, ALU.pow).then_inc(s_dinv_ready, 1)

            def fetch(dst, src, ix):
                nc.gpsimd.indirect_dma_start(
                    out=dst, out_offset=None, in_=src, in_offset=bass.IndirectOffsetOnAxis(ap=ix[:, 0:1], axis=0),
                    bounds_check=N - 1, oob_is_err=False).then_inc(s_gathered, 16)

            def rstd0(t):
                pool.wait_ge(s_ln_v, t + 1)
                nc.gpsimd.tensor_tensor(rstd_all[:, t:t + 1], var_all[:, t:t + 1], mhalfs[:, 0:1], ALU.pow)\
                    .then_inc(s_ln_rstd, 1)

            pool.wait_ge(s_n_ready, 1)
            many = pool.value_load(n_act[0:1, 0:1])
            with pool.If(many > P):
                pool.dma_start(spare, R4[:, 0:2 * C * D]).then_inc(s_saved, 16)
                with pool.Fori(0, T) as t:
                    pool.wait_ge(s_slots_ready, t + 1)
                    pool.nop(nofuse=True)
                    nc.gpsimd.memset(adj_c, 0.0).then_inc(s_slot_fill, 1)
                    nc.gpsimd.memset(x_c, 0.0).then_inc(s_slot_fill, 1)
                    pool.wait_ge(s_slot_fill, 3 * t + 2)
                    pool.nop(nofuse=True)
                    fetch(x_c, x_d, slot_ix)
                    fetch(adj_c[:, 0:N], adj_d, slot_ix)
                    nc.gpsimd.memset(WA[:, 0:2 * HEADS * P], 0.0).then_inc(s_slot_fill, 1)
                pool.wait_ge(s_put_done, T)
                pool.wait_ge(s_saved, 16)
                pool.dma_start(R4[:, 0:2 * C * D], spare).then_inc(s_saved, 16)
                for t in range(T):
                    rstd0(t)
            with pool.Else():
                nc.gpsimd.memset(pair_x[:, :, :], 0.0).then_inc(s_slot_fill, 1)
                pool.wait_ge(s_slot_fill, 1)
                pool.wait_ge(s_slots_ready, 2)
                fetch(pair_x[:, 0, :], x_d, slot_ix)
                fetch(pair_x[:, 1, :], x_d, obj_ix)
                for t in range(T + 1):
                    if t < T:
                        pool.wait_ge(s_placed, t + 1)
                        pool.wait_ge(s_closed, t + 1)
                        nc.gpsimd.tensor_tensor(BASE[:, t, :], BASE[:, t, :], X[:, t, :], ALU.add).then_inc(s_summed, 1)
                    if t >= 1:
                        rstd0(t - 1)

            def rstd(n):
                pool.wait_ge(s_ln_v, n + 1)
                nc.gpsimd.tensor_tensor(ln_rstd, ln_var, mhalfs[:, 0:1], ALU.pow).then_inc(s_ln_rstd, 1)

            for n in (4, 5):
                pool.wait_ge(s_wst_hi, 2 * n - 2)
                nc.gpsimd.tensor_tensor(flat(staged(n, 1)), flat(w_stage(n)), flat(staged(n, 0)), ALU.subtract)\
                    .then_inc(s_wst_lo, 1)
            with pool.Fori(T, 4 * T) as n:
                rstd(n)

        @block.scalar
        def _(act):
            act.wait_ge(s_wk0_in, 16)
            nc.scalar.activation(w0_hl[:, 0], wk0_f, ACT.Copy, scale=SW0).then_inc(s_w0_hi, 1)
            act.wait_ge(s_wq0_in, 16)
            nc.scalar.activation(w0q_hl[:, 0], wq0_f, ACT.Copy, scale=SW0).then_inc(s_w0_hi, 1)
            def stage_hi(n):
                act.wait_ge((s_wst_in0, s_wst_in1)[n % 2], 16 * (n // 2) + 16)
                act.nop(nofuse=True)
                nc.scalar.activation(staged(n, 0), w_stage(n), ACT.Copy, scale=SW).then_inc(s_wst_hi, 1)

            stage_hi(0)
            stage_hi(1)
            act.sem_inc(s_at_a, 2)

            def at_out(j):
                act.wait_ge(s_at_mm, 2 * j + 2)
                nc.scalar.copy(AT[:, :, ds(j * 2 * P + P, P)],
                               PS16[:, ds(4096 + 2048 * (j % 2), NP)].rearrange("p (a n) -> p a n", n=P)).then_inc(s_at_a, 1)

            with act.Fori(0, T // 2 - 3) as j:
                at_out(j)
            stage_hi(2)
            at_out(T // 2 - 3)
            stage_hi(3)
            at_out(T // 2 - 2)
            at_out(T // 2 - 1)
            for d in range(C):
                act.wait_ge(s_g_mm, d + 1)
                nc.scalar.activation(GHL[:, 0, d, :], PS[:, g_bank[d], :], ACT.Copy, scale=1.0 / SW).then_inc(s_g_hi, 1)
                for t in range(d * XG, min(d * XG + XG, T)):
                    act.wait_ge(s_x_in0 if t < (T - 1) // 2 else s_x_in, 16 if t < (T - 1) // 2 else 32)
                    nc.scalar.activation(UHL[:, 0, t, :], X[:, t, :], ACT.Copy, scale=SX).then_inc(s_x_hi, 1)
            act.wait_ge(s_vec_mm, 1)
            nc.scalar.activation(a_row[:, :], PS[:, 4, :], ACT.Copy, scale=SX * SW / (SB * SW)).then_inc(s_vec_out, 1)
            nc.scalar.activation(c2, PS[:, 5, 0:C], ACT.Copy, scale=1.0 / SB).then_inc(s_vec_out, 1)
            nc.scalar.activation(beta, PS[:, 5, C:C + 1], ACT.Copy, scale=SX * SW / (SB * SB)).then_inc(s_vec_out, 1)
            act.sem_inc(s_base_out, 2)

            def row_sums(t):
                if t >= 5:
                    act.wait_ge(s_rows_summed, t - 4)
                nc.scalar.activation(unused[:, t % 5, :], A[:, t, :], ACT.Copy, accum_out=row_n[:, t:t + 1]).then_inc(s_rows_summed, 1)

            def base_out(t):
                act.wait_ge(s_prod_mm, t + 1)
                nc.scalar.copy(row(BASE, t), PS[:, ds(t % 2, 1), :].rearrange("p a n -> p (a n)")).then_inc(s_base_out, 1)

            row_sums(0)
            for t in range(T // 2):
                row_sums(2 * t + 1)
                row_sums(2 * t + 2)
                base_out(t)
            with act.Fori(T // 2, AHEAD + 4) as t:
                base_out(t)

            def attend(r):
                act.wait_ge(s_gathered, 32 * r + 32)
                act.nop(nofuse=True)
                nc.scalar.activation(xc_hl[:, 0], x_c, ACT.Copy, scale=SX).then_inc(s_xc_hi, 1)
                act.wait_ge(s_xct_mm, r + 1)
                nc.scalar.copy(xct, PS16[:, 7168:8192].rearrange("p (h c n) -> p h c n", h=2, c=C))\
                    .then_inc(s_xct_out, 1)
                act.wait_ge(s_q_mm, r + 1)
                for m in range(C):
                    nc.scalar.activation(qf0[:, m, :], PS[:, 6, m * P:(m + 1) * P], ACT.Identity,
                                         bias=bq0[:, m:m + 1], scale=SK / (SX * SW0)).then_inc(s_q_full, 1)
                for h in range(HEADS):
                    act.wait_ge(s_nb_ready, HEADS * r + h + 1)
                    act.nop(nofuse=True)
                    nc.scalar.activation(prob[h % 3], prob[h % 3], ACT.Exp, bias=nb[:, h:h + 1],
                                         scale=1.0 / (SK * SK * 8.0), accum_out=zs[:, h:h + 1]).then_inc(s_p_ready, 1)
                    nc.scalar.activation(em[:, h:h + 1], nb[:, h:h + 1], ACT.Exp).then_inc(s_em_ready, 1)
                act.wait_ge(s_f_step, HEADS * r + HEADS)
                act.nop(nofuse=True)
                nc.scalar.activation(f_hl[:, 0, 0:NG], fsum, ACT.Copy, scale=SP_ / HEADS).then_inc(s_f_hi, 1)
                act.wait_ge(s_ft_mm, 2 * r + 1)
                nc.scalar.copy(f_t[:, 0], PS16[:, 2048:2048 + NP].rearrange("p (a n) -> p a n", n=P)).then_inc(s_ft_hi, 1)

            def u_hi(t):
                act.wait_ge(s_ln_x, t + 1)
                act.nop(nofuse=True)
                nc.scalar.activation(UHL[:, 0, t, :], X[:, t, :], ACT.Copy, scale=dinv_s[:, t:t + 1]).then_inc(s_u_hi, 1)

            act.wait_ge(s_n_ready, 1)
            many = act.value_load(n_act[0:1, 0:1])
            with act.If(many > P):
                with act.Fori(AHEAD + 4, T) as t:
                    base_out(t)
                act.wait_ge(s_saved, 16)
                act.sem_inc(s_xt_out, 4)
                with act.Fori(0, T) as t:
                    act.wait_ge(s_xt_mm, t + 1)
                    nc.scalar.copy(XT[:, :, :, ds(t * P, P)],
                                   PS16[:, ds((t % 4) * 1024, 1024)].rearrange("p (h c n) -> p h c n", h=2, c=C))\
                        .then_inc(s_xt_out, 1)
                act.sem_inc(s_kf_ready, G)
                act.wait_ge(s_bias0, 2)
                with act.Fori(0, C) as m:
                    for n in range(G):
                        act.wait_ge(s_kp_mm, G * m + n + 1)
                        act.wait_ge(s_kt_done, G * m + n + 1)
                        act.nop(nofuse=True)
                        nc.scalar.activation(kf[:, n, :], PS[:, 2 + n, 0:GW], ACT.Identity, bias=one(bk0, m),
                                             scale=SK / (SX * SW0)).then_inc(s_kf_ready, 1)
                with act.Fori(0, T) as t:
                    attend(t)
                for t in range(T):
                    u_hi(t)
            with act.Else():
                act.sem_inc(s_xt_out, T + 4)
                act.wait_ge(s_gathered, 32)
                nc.scalar.activation(flat(pair_hl[:, 0]), flat(pair_x), ACT.Copy, scale=SX).then_inc(s_xc_hi, 1)
                act.wait_ge(s_xct_mm, 1)
                nc.scalar.copy(pair_t[:, 0], PS16[:, 6144:7168]).then_inc(s_xct_out, 1)
                base_out(T - 2)
                act.wait_ge(s_arg_ready, 2)
                nc.scalar.activation(p_em, args, ACT.Exp).then_inc(s_p_ready, 1)
                base_out(T - 1)
                act.wait_ge(s_weight_ready, 1)
                nc.scalar.activation(put_hl[:, 0], pair_x[:, 1, :], ACT.Copy, scale=obj_weight).then_inc(s_y_hi, 1)

                def closed(t):
                    nc.scalar.activation(BASE[:, t, :], BASE[:, t, :], ACT.Copy, scale=c_a[:, t:t + 1])\
                        .then_inc(s_closed, 1)

                act.wait_ge(s_has_ready, 1)
                for t in range(3):
                    closed(t)
                for t in range(T):
                    if t + 3 < T:
                        closed(t + 3)
                    u_hi(t)

            def w1_hi(t):
                act.wait_ge(s_prod_mm, T + t + 1)
                act.nop(nofuse=True)
                nc.scalar.activation(VHL[:, 0, t, :], PS[:, w1_bank(t), :], ACT.Copy,
                                     scale=dinv_half[:, t:t + 1]).then_inc(s_w1_hi, 1)

            for t in range(T):
                w1_hi(t)
                if t in (6, 7):
                    stage_hi(t - 2)
                    nc.scalar.activation(w_stage(t - 2), w_stage(t - 2), ACT.Copy, scale=SW).then_inc(s_wst_hi, 1)
            act.wait_ge(s_moved, 32)
            nc.scalar.activation(wv_hl[:, 0], wv_f, ACT.Copy, scale=SW).then_inc(s_wv_hi, 1)
            act.sem_inc(s_qf_ready, 2)

            def queries(n, m0, m1):
                with act.Fori(m0, m1) as m:
                    act.wait_ge(s_qt_mm, C * n + m + 1)
                    act.wait_ge(s_qt_done, C * n + m + 1)
                    act.nop(nofuse=True)
                    nc.scalar.activation(qf[:, ds(m % 2, 1), :].rearrange("p a n -> p (a n)"),
                                         PS[:, ds(6 + m % 2, 1), 0:GW].rearrange("p a n -> p (a n)"), ACT.Identity,
                                         bias=one(c2, m), scale=1.0 / SX).then_inc(s_qf_ready, 1)

            act.wait_ge(s_moved, 16)
            act.sem_inc(s_xt_out, 2)

            def step(n, t, slot, turned=True, rows=True, end=True):
                if turned:
                    act.wait_ge(s_xt_mm, n * T + t - 1)
                    nc.scalar.copy(XT[:, :, :, ds((t - 2) * P, P)],
                                   PS16[:, 2048 + slot * 1024:3072 + slot * 1024]
                                   .rearrange("p (h c n) -> p h c n", h=2, c=C)).then_inc(s_xt_out, 1)
                if rows:
                    act.wait_ge(s_rows_mm, (n - 1) * T + t - 2)
                    act.nop(nofuse=True)
                    dst = SHL if n == 1 else VHL
                    nc.scalar.activation(part_row(dst, 0, t - 3), PS[:, 5 - slot, :], ACT.Copy, scale=1.0 / SX)\
                        .then_inc(s_rows_hi, 1)
                if end:
                    act.wait_ge(s_ln_x, n * T + t + 1)
                    act.nop(nofuse=True)
                    nc.scalar.activation(x_row(0, slot), row(X, t), ACT.Copy, scale=SX).then_inc(s_x_hi, 1)

            for n in (1, 2):
                if n == 2:
                    act.sem_inc(s_xt_out, 2)
                step(n, 0, 0, turned=False, rows=False)
                step(n, 1, 1, turned=False, rows=False)
                step(n, 2, 0, rows=False)
                with act.Fori(1, T // 2) as j:
                    step(n, 2 * j + 1, 1)
                    step(n, 2 * j + 2, 0)
                step(n, T, 1, end=False)
                step(n, T + 1, 0, end=False)
                if n == 2:
                    queries(0, 0, C)
                step(n, T + 2, 1, turned=False, end=False)
            def soft(t):
                act.wait_ge(s_nm3_ready, t + 1)
                act.nop(nofuse=True)
                nc.scalar.activation(zero_fill[:, 0:N], score[:, 0:N], ACT.Exp, bias=nm3, scale=Z_SCALE,
                                     accum_out=z3).then_inc(s_p3_ready, 1)
                act.wait_ge(s_p3_ready, t + 1)
                if not isinstance(t, int) or t > 0:
                    act.wait_ge(s_pt_mm, 2 * t)
                    act.nop(nofuse=True)
                nc.scalar.activation(prob_hl[:, 0, 0:N], zero_fill[:, 0:N], ACT.Copy, scale=SP_).then_inc(s_ph_ready, 1)

            def turn(t):
                act.wait_ge(s_pt_mm, 2 * t + 1)
                if not isinstance(t, int) or t >= 2:
                    act.wait_ge(s_o_mm, t - 1)
                nc.scalar.copy(turned(t % 2, 0), PS16[:, 3072:3072 + NP]).then_inc(s_pt_hi, 1)

            queries(1, 0, 2)
            soft(0)
            queries(1, 2, C)
            turn(0)
            queries(2, 0, 2)
            soft(1)
            queries(2, 2, C)
            soft(2)
            turn(1)
            with act.Fori(3, T) as t:
                soft(t)
                turn(t - 1)
            turn(T - 1)

        @block.vector
        def _(dve):
            dve.sem_inc(s_w0_out, 2)
            dve.sem_inc(s_at_v, 2)
            dve.wait_ge(s_rel_in, 16)
            rel_v = rel[:, :].rearrange("p (i two) -> p two i", two=2)
            nc.vector.tensor_copy(subf[:, :], rel_v[:, 0]).then_inc(s_step, 1)
            nc.vector.tensor_copy(objf[:, :], rel_v[:, 1]).then_inc(s_step, 1)
            dve.wait_ge(s_step, 2)
            nc.vector.tensor_scalar(bad[:, :], subf[:, :], float(N), None, ALU.is_ge).then_inc(s_step, 1)
            nc.vector.tensor_tensor(hit[:, :], subf[:, :], objf[:, :], ALU.is_equal).then_inc(s_step, 1)
            nc.vector.tensor_scalar(pair[:, :, 0], subf[:, :], 1.0, None, ALU.add).then_inc(s_step, 1)
            nc.vector.tensor_scalar(pair[:, :, 1], objf[:, :], 1.0, None, ALU.add).then_inc(s_step, 1)
            dve.wait_ge(s_step, 6)
            nc.vector.scalar_tensor_tensor(out=bad[:, :], in0=objf[:, :], scalar=float(N), in1=bad[:, :],
                                           op0=ALU.is_ge, op1=ALU.add).then_inc(s_step, 1)
            dve.wait_ge(s_step, 7)
            nc.vector.tensor_tensor(bad[:, :], bad[:, :], hit[:, :], ALU.add).then_inc(s_step, 1)
            dve.wait_ge(s_step, 8)
            nc.vector.scalar_tensor_tensor(out=hit[:, :], in0=subf[:, :], scalar=float(N), in1=objf[:, :],
                                           op0=ALU.mult, op1=ALU.add).then_inc(s_step, 1)
            dve.wait_ge(s_step, 9)
            nc.vector.scalar_tensor_tensor(out=rel_ix[:, :], in0=bad[:, :], scalar=FAR, in1=hit[:, :],
                                           op0=ALU.mult, op1=ALU.add).then_inc(s_step, 1)
            dve.wait_ge(s_step, 10)
            nc.vector.memset(hit[:, :], 0.0).then_inc(s_ix_ready, 1)
            def w0_low(n, full, hl):
                dve.wait_ge(s_w0_hi, n + 1)
                nc.vector.scalar_tensor_tensor(out=flat(hl[:, 1]), in0=flat(full), scalar=SW0, in1=flat(hl[:, 0]),
                                               op0=ALU.mult, op1=ALU.subtract).then_inc(s_w0_lo, 1)

            w0_low(0, wk0_f, w0_hl)

            def weights_out(n, dst, m):
                dve.wait_ge(s_w0_mm, n + 1)
                nc.vector.tensor_copy(dst[:, :, :, m * P:(m + 1) * P],
                                      PS16[:, 4096 + (n % 2) * 1024:4096 + (n % 2) * 1024 + 1024]
                                      .rearrange("p (h c n) -> p h c n", h=2, c=C)).then_inc(s_w0_out, 1)

            for m in range(C):
                weights_out(m, WKT, m)
            w0_low(1, wq0_f, w0q_hl)
            for m in range(C):
                weights_out(C + m, WQT, m)
            def stage_lo(n):
                dve.wait_ge(s_wst_hi, n + 1)
                nc.vector.scalar_tensor_tensor(out=flat(staged(n, 1)), in0=flat(w_stage(n)), scalar=SW,
                                               in1=flat(staged(n, 0)), op0=ALU.mult, op1=ALU.subtract)\
                    .then_inc(s_wst_lo, 1)

            stage_lo(0)
            stage_lo(1)
            def at_out(j):
                dve.wait_ge(s_at_mm, 2 * j + 1)
                nc.vector.tensor_copy(AT[:, :, ds(j * 2 * P, P)],
                                      PS16[:, ds(2048 * (j % 2), NP)].rearrange("p (a n) -> p a n", n=P)).then_inc(s_at_v, 1)

            with dve.Fori(0, T // 2 - 1) as j:
                at_out(j)
            stage_lo(2)
            stage_lo(3)
            at_out(T // 2 - 1)
            at_out(T // 2)
            dve.wait_ge(s_b_in, 96)
            dve.wait_ge(s_const, 5)
            nc.vector.tensor_scalar(b_hl[:, 0, 0:C], bk3, SB, None, ALU.mult).then_inc(s_step, 1)
            nc.vector.tensor_scalar(b_hl[:, 0, C:2 * C], bq3, SB, None, ALU.mult).then_inc(s_step, 1)
            dve.wait_ge(s_step, 12)
            nc.vector.scalar_tensor_tensor(out=b_hl[:, 1, 0:C], in0=bk3, scalar=SB, in1=b_hl[:, 0, 0:C], op0=ALU.mult,
                                           op1=ALU.subtract).then_inc(s_step, 1)
            nc.vector.scalar_tensor_tensor(out=b_hl[:, 1, C:2 * C], in0=bq3, scalar=SB, in1=b_hl[:, 0, C:2 * C],
                                           op0=ALU.mult, op1=ALU.subtract).then_inc(s_step, 1)
            dve.wait_ge(s_step, 14)
            for i in range(2):
                for m in range(C):
                    nc.vector.tensor_scalar(bk_b[:, i, m, :], ones[:, :], b_hl[:, i, m:m + 1], None, ALU.mult)\
                        .then_inc(s_bkb_ready, 1)
            for d in range(C):
                dve.wait_ge(s_g_hi, d + 1)
                nc.vector.scalar_tensor_tensor(out=GHL[:, 1, d, :], in0=PS[:, g_bank[d], :], scalar=1.0 / SW,
                                               in1=GHL[:, 0, d, :], op0=ALU.mult, op1=ALU.subtract)\
                    .then_inc(s_g_lo, 1)
                for t in range(d * XG, min(d * XG + XG, T)):
                    dve.wait_ge(s_x_hi, t + 1)
                    nc.vector.scalar_tensor_tensor(out=UHL[:, 1, t, :], in0=X[:, t, :], scalar=SX, in1=UHL[:, 0, t, :],
                                                   op0=ALU.mult, op1=ALU.subtract).then_inc(s_x_lo, 1)
            dve.wait_ge(s_at_v, 2 + (T + 1) // 2)
            dve.wait_ge(s_at_a, 2 + T // 2)
            dve.wait_ge(s_vec_mm, 1)

            def symmetric(before, tiles, sums=None):
                for k in tiles:
                    if sums is None:
                        op = nc.vector.tensor_tensor(SYM[:, k, :], A[:, k, :], AT[:, k, :], ALU.add)
                    else:
                        op = nc.vector.scalar_tensor_tensor(out=SYM[:, k, :], in0=A[:, k, :], scalar=1.0,
                                                            in1=AT[:, k, :], op0=ALU.mult, op1=ALU.add,
                                                            accum_out=sums[:, k:k + 1])
                    op.then_inc(s_sym_sum, 1)
                    dve.wait_ge(s_sym_sum, before + k + 1)
                    diag = SYM[:, k, k * P:(k + 1) * P]
                    nc.vector.scalar_tensor_tensor(out=diag, in0=ident[:, :], scalar=2.0, in1=diag, op0=ALU.mult,
                                                   op1=ALU.add).then_inc(s_sym_ready, 1)

            symmetric(0, range(0, SYM_FIRST), sums=dinv)
            dve.wait_ge(s_const, 5)
            w = P
            while w < NP:
                more = min(w, NP - w)
                nc.vector.tensor_scalar(iota[:, w:w + more], iota[:, 0:more], float(w), None, ALU.add)\
                    .then_inc(s_const, 1)
                w += more
                dve.wait_ge(s_const, {2 * P: 6, 4 * P: 7, 8 * P: 8, NP: 9}[w])
            nc.vector.tensor_copy(identf[:, :], ident[:, :]).then_inc(s_const, 1)
            def rank_columns(i, c0, c1):
                dve.wait_ge((s_hit_in0, s_hit_in1)[i], 16 * (c1 - c0))
                nc.vector.tensor_scalar(act16[:, c0:c1], hit[:, c0:c1], 1.0, None, ALU.is_equal).then_inc(s_act_ready, 1)
                dve.wait_ge(s_act_ready, i + 1)
                nc.vector.tensor_scalar(bad[:, c0:c1], act16[:, c0:c1], -20000.0, 20000.0, ALU.mult, ALU.add)\
                    .then_inc(s_step, 1)
                dve.wait_ge(s_tot_mm, i + 1)
                nc.vector.tensor_copy(tot16[0:c1, :], PS[0:c1, 4, 0:P]).then_inc(s_tot_ready, 1)
                dve.wait_ge(s_rank_mm, i + 1)
                if i == 1:
                    nc.vector.tensor_copy(n_act[:, :], PS[0:1, 7, 0:1]).then_inc(s_n_ready, 1)
                dve.wait_ge(s_step, (15, 19)[i])
                nc.vector.tensor_tensor(rank[:, c0:c1], PS[0:EP, 6, c0:c1], bad[:, c0:c1], ALU.add)\
                    .then_inc(s_rank_ready, 1)
                dve.wait_ge(s_rank_ready, i + 1)

            def one_hots(k):
                if k >= 2:
                    dve.wait_ge(s_slots_mm, k - 1)
                for i in range(OC):
                    last = nc.vector.tensor_scalar(hot[k % 2][0:EP, i, :], iota[0:EP, 0:P],
                                                   rank[:, k * OC + i:k * OC + i + 1], None, ALU.is_equal)
                last.then_inc(s_hot_ready, 1)

            rank_columns(0, 0, EARLY)
            symmetric(0, range(SYM_FIRST, SYM_FIRST + 1), sums=dinv)
            dve.wait_ge(s_rows_summed, T)
            for k in range(EARLY // OC):
                one_hots(k)
            symmetric(0, range(SYM_FIRST + 1, T), sums=dinv)
            nc.vector.tensor_scalar(dinv, dinv, 0.5, 1.0, ALU.mult, ALU.add).then_inc(s_deg_ready, 1)
            nc.vector.tensor_scalar(c_b, row_n, E_DIAG, DIAG, ALU.mult, ALU.add).then_inc(s_step, 1)
            dve.wait_ge(s_step, 16)
            nc.vector.reciprocal(c_b, c_b).then_inc(s_step, 1)
            dve.wait_ge(s_step, 17)
            nc.vector.tensor_scalar(c_a, c_b, E_DIAG, None, ALU.mult).then_inc(s_step, 1)
            rank_columns(1, EARLY, EC)
            dve.wait_ge(s_n_ready, 1)
            many = dve.value_load(n_act[0:1, 0:1])

            def scale_dinv():
                dve.wait_ge(s_dinv_ready, 1)
                nc.vector.tensor_scalar(dinv_half, dinv, 0.5, None, ALU.mult).then_inc(s_dinv_s_ready, 1)
                nc.vector.tensor_scalar(dinv_s, dinv, SX, None, ALU.mult).then_inc(s_dinv_s_ready, 1)
                dve.wait_ge(s_dinv_s_ready, 2)

            def attend(r):
                dve.wait_ge(s_w_mm, r + 1)
                nc.vector.tensor_scalar(wmask.rearrange("p (g n) -> p g n", g=G), PS[:, 2:5, 0:GW], 1.0, 1.0,
                                        ALU.min, ALU.add).then_inc(s_w_step, 1)
                dve.wait_ge(s_w_step, r + 1)
                dve.wait_ge(s_gathered, 32 * r + 32)
                nc.vector.tensor_tensor(wmask, wmask, adj_c, ALU.subtract).then_inc(s_mask_ready, 1)
                nc.vector.tensor_scalar(bmask, adj_c, -1.0, OFF, ALU.add, ALU.mult).then_inc(s_mask_ready, 1)
                dve.wait_ge(s_xc_hi, r + 1)
                nc.vector.scalar_tensor_tensor(out=xc_hl[:, 1], in0=x_c, scalar=SX, in1=xc_hl[:, 0], op0=ALU.mult,
                                               op1=ALU.subtract).then_inc(s_xc_lo, 1)
                dve.wait_ge(s_q_full, C * r + C)
                dve.wait_ge(s_slot_fill, 3 * r + 3)
                for lanes, q_one in q_lanes:
                    nc.vector.tensor_copy(q_one[:, 0], qf0[lanes]).then_inc(s_q_hi, 1)
                dve.wait_ge(s_q_hi, 2 * r + 2)
                for lanes, q_one in q_lanes:
                    nc.vector.tensor_tensor(q_one[:, 1], qf0[lanes], q_one[:, 0], ALU.subtract).then_inc(s_q_lo, 1)
                dve.wait_ge(s_q_lo, 2 * r + 2)
                dve.wait_ge(s_mask_ready, 2 * r + 2)

                def add_head(h):
                    one_h = slice(h, h + 1)
                    dve.wait_ge(s_em_ready, HEADS * r + h + 1)
                    nc.vector.scalar_tensor_tensor(out=zs[:, one_h], in0=em[:, one_h], scalar=DIAG, in1=zs[:, one_h],
                                                   op0=ALU.mult, op1=ALU.add).then_inc(s_z_ready, 1)
                    dve.wait_ge(s_z_ready, 2 * HEADS * r + 2 * h + 1)
                    nc.vector.reciprocal(rz[:, one_h], zs[:, one_h]).then_inc(s_z_ready, 1)
                    dve.wait_ge(s_z_ready, 2 * HEADS * r + 2 * h + 2)
                    if h == 0:
                        nc.vector.tensor_scalar(fsum, prob[0], rz[:, one_h], None, ALU.mult).then_inc(s_f_step, 1)
                    else:
                        dve.wait_ge(s_f_step, HEADS * r + h)
                        nc.vector.scalar_tensor_tensor(out=fsum, in0=prob[h % 3], scalar=rz[:, one_h], in1=fsum,
                                                       op0=ALU.mult, op1=ALU.add).then_inc(s_f_step, 1)

                for h in range(HEADS):
                    b = 2 + G * (h % 2)
                    dve.wait_ge(s_s_mm, HEADS * r + h + 1)
                    if h >= 3:
                        dve.wait_ge(s_f_step, HEADS * r + h - 2)
                    dve.nop(nofuse=True)
                    nc.vector.tensor_tensor_reduce(
                        out=prob[h % 3].rearrange("p (g n) -> p g n", g=G), in0=PS[:, b:b + G, 0:GW],
                        in1=wmask.rearrange("p (g n) -> p g n", g=G), scale=1.0, scalar=-3.0e38, op0=ALU.mult,
                        op1=ALU.max, accum_out=mx[:, h:h + 1]).then_inc(s_t_ready, 1)
                    dve.wait_ge(s_t_ready, HEADS * r + h + 1)
                    nc.vector.tensor_scalar(nb[:, h:h + 1], mx[:, h:h + 1], -1.0 / (SK * SK * 8.0), -DIAG, ALU.mult,
                                            ALU.min).then_inc(s_nb_ready, 1)
                    if h >= 1:
                        add_head(h - 1)
                add_head(HEADS - 1)
                dve.wait_ge(s_f_step, HEADS * r + HEADS)
                nc.vector.memset(f_hl[:, :, NG:NP], 0.0).then_inc(s_f_pad, 1)
                nc.vector.tensor_tensor(g_tmp, em, rz, ALU.mult).then_inc(s_g_step, 1)
                dve.wait_ge(s_g_step, 3 * r + 1)
                nc.vector.reduce_sum(g_sum, g_tmp, mybir.AxisListType.X).then_inc(s_g_step, 1)
                dve.wait_ge(s_g_step, 3 * r + 2)
                nc.vector.tensor_scalar(g_sum, g_sum, DIAG / HEADS, 1.0, ALU.mult, ALU.add).then_inc(s_g_step, 1)
                dve.wait_ge(s_f_hi, r + 1)
                nc.vector.scalar_tensor_tensor(out=f_hl[:, 1, 0:NG], in0=fsum, scalar=SP_ / HEADS, in1=f_hl[:, 0, 0:NG],
                                               op0=ALU.mult, op1=ALU.subtract).then_inc(s_f_lo, 1)
                dve.wait_ge(s_ft_mm, 2 * r + 2)
                nc.vector.tensor_copy(f_t[:, 1], PS16[:, 4096:4096 + NP].rearrange("p (a n) -> p a n", n=P))\
                    .then_inc(s_ft_lo, 1)

            def layer0_end(put):
                lag = 1 if put else 0
                for t in range(T + 2 + lag):
                    n = t - lag
                    if put and t < T:
                        dve.wait_ge(s_put_mm, t + 1)
                        nc.vector.scalar_tensor_tensor(out=X[:, t, :], in0=X[:, t, :], scalar=c_b[:, t:t + 1],
                                                       in1=PS[:, t % 2, :], op0=ALU.mult, op1=ALU.add)\
                            .then_inc(s_placed, 1)
                    if 0 <= n < T:
                        if put:
                            dve.wait_ge(s_summed, n + 1)
                            dve.nop(nofuse=True)
                        nc.vector.bn_stats(ln_st, BASE[:, n, :]).then_inc(s_ln_s, 1)
                    if 1 <= n <= T:
                        dve.wait_ge(s_ln_rstd, n)
                        nc.vector.tensor_scalar(X[:, n - 1, :], BASE[:, n - 1, :], mv_all[:, n - 1, 0:1],
                                                rstd_all[:, n - 1:n], ALU.subtract, ALU.mult).then_inc(s_ln_x, 1)
                    if 0 <= n < T:
                        dve.wait_ge(s_ln_s, n + 1)
                        dve.nop(nofuse=True)
                        nc.vector.bn_aggr(mv_all[:, n, :], ln_st).then_inc(s_ln_m, 1)
                    if n >= 2:
                        dve.wait_ge(s_u_hi, n - 1)
                        nc.vector.scalar_tensor_tensor(out=UHL[:, 1, n - 2, :], in0=X[:, n - 2, :],
                                                       scalar=dinv_s[:, n - 2:n - 1], in1=UHL[:, 0, n - 2, :],
                                                       op0=ALU.mult, op1=ALU.subtract).then_inc(s_u_lo, 1)
                    if 0 <= n < T:
                        dve.wait_ge(s_ln_m, n + 1)
                        nc.vector.tensor_scalar(var_all[:, n:n + 1], mv_all[:, n, 1:2], EPS * SX * SX, None, ALU.add).then_inc(s_ln_v, 1)

            with dve.If(many > P):
                dve.wait_ge(s_b_in, 96)
                nc.vector.tensor_scalar(bk0, bk0, SK, None, ALU.mult).then_inc(s_bias0, 1)
                nc.vector.tensor_scalar(bq0, bq0, SK, None, ALU.mult).then_inc(s_bias0, 1)
                nc.vector.tensor_copy(identb, ident[:, :]).then_inc(s_kh_done, 1)
                dve.sem_inc(s_kt_done, G)
                with dve.Fori(0, C) as m:
                    for n in range(G):
                        dve.wait_ge(s_kf_ready, G * m + n + 1 + G)
                        k_at = [KT[:, i, ds(m, 1), n * GW:(n + 1) * GW].rearrange("p a n -> p (a n)") for i in range(2)]
                        nc.vector.tensor_copy(k_at[0], kf[:, n, :]).then_inc(s_kh_done, 1)
                        dve.wait_ge(s_kh_done, G * m + n + 2)
                        nc.vector.tensor_tensor(k_at[1], kf[:, n, :], k_at[0], ALU.subtract).then_inc(s_kt_done, 1)
                nc.vector.tensor_scalar(bad[:, :], act16[:, :], 5000.0, -5000.0, ALU.mult, ALU.add)\
                    .then_inc(s_all_step, 1)
                nc.vector.tensor_copy(slot_row, row_id).then_inc(s_all_step, 1)
                dve.wait_ge(s_all_step, 2)
                nc.vector.tensor_tensor(subf[:, :], subf[:, :], bad[:, :], ALU.add).then_inc(s_all_step, 1)
                dve.wait_ge(s_all_step, 3)
                dve.wait_ge(s_base_out, 2 + T)
                dve.wait_ge(s_kp_mm, G * C)
                with dve.Fori(0, T) as t:
                    nc.vector.tensor_scalar(slot_far, slot_row, 0.0, FAR, ALU.is_lt, ALU.mult)\
                        .then_inc(s_slot_step, 1)
                    dve.wait_ge(s_slot_step, t + 1)
                    nc.vector.tensor_tensor(slot_ix[:, :], slot_far, slot_row, ALU.add).then_inc(s_slots_ready, 1)
                    with dve.Fori(0, EC // 2) as j:
                        for i in range(2):
                            dve.wait_ge(s_hots_free, t * EC + j * 2 + i + 1)
                            nc.vector.tensor_scalar(all_sub[i][0:EP, :], iota[0:EP, 0:P], one(subf, j * 2 + i), None,
                                                    ALU.is_equal).then_inc(s_hots_made, 1)
                            nc.vector.tensor_scalar(all_obj[i][0:EP, :], iota[0:EP, 0:NG], one(objf, j * 2 + i), None,
                                                    ALU.is_equal).then_inc(s_hots_made, 1)
                    attend(t)
                    dve.wait_ge(s_y_mm, t + 1)
                    dve.wait_ge(s_g_step, 3 * t + 3)
                    nc.vector.tensor_scalar(row(BASE, t), row(X, t), g_sum, SX, ALU.mult, ALU.mult).then_inc(s_all_res, 1)
                    dve.wait_ge(s_all_res, t + 1)
                    nc.vector.scalar_tensor_tensor(out=row(BASE, t), in0=PS[:, 0, :], scalar=1.0 / SP_,
                                                   in1=row(BASE, t), op0=ALU.mult, op1=ALU.add)\
                        .then_inc(s_put_done, 1)
                    nc.vector.tensor_scalar(slot_row, slot_row, float(P), None, ALU.add).then_inc(s_all_step, 1)
                    nc.vector.tensor_scalar(subf[:, :], subf[:, :], float(-P), None, ALU.add).then_inc(s_all_step, 1)
                    dve.wait_ge(s_all_step, 2 * t + 5)
                    dve.wait_ge(s_put_done, t + 1)
                dve.wait_ge(s_saved, 32)
                nc.vector.memset(ln_mv, 0.0).then_inc(s_all_done, 1)
                symmetric(T, range(T))
                scale_dinv()
                layer0_end(put=False)
            with dve.Else():
                for k in range(EARLY // OC, EC // OC):
                    one_hots(k)
                dve.wait_ge(s_slots_mm, EC // OC)
                nc.vector.tensor_scalar(slot_row, PS[:, 5, 0:1], -1.0, None, ALU.add).then_inc(s_slot_step, 1)
                nc.vector.tensor_scalar(slot_obj, PS[:, 5, 1:2], -1.0, None, ALU.add).then_inc(s_slot_step, 1)
                dve.wait_ge(s_slot_step, 2)
                nc.vector.tensor_scalar(slot_far, slot_row, 0.0, FAR, ALU.is_lt, ALU.mult).then_inc(s_slot_step, 1)
                nc.vector.tensor_scalar(slot_low, slot_row, 0.0, None, ALU.is_ge).then_inc(s_slot_step, 1)
                nc.vector.tensor_scalar(row_b, ones[:, :], slot_row, None, ALU.mult).then_inc(s_sub_ready, 1)
                nc.vector.tensor_scalar(obj_b, ones[:, :], slot_obj, None, ALU.mult).then_inc(s_sub_ready, 1)
                dve.wait_ge(s_slot_step, 4)
                nc.vector.tensor_tensor(slot_ix[:, :], slot_far, slot_row, ALU.add).then_inc(s_slots_ready, 1)
                nc.vector.tensor_tensor(obj_ix[:, :], slot_far, slot_obj, ALU.add).then_inc(s_slots_ready, 1)
                scale_dinv()
                dve.wait_ge(s_sub_mm, 1)
                nc.vector.tensor_scalar(same, PS[:, 6, 0:P], slot_row, slot_low, ALU.is_equal, ALU.mult)\
                    .then_inc(s_same_ready, 1)
                dve.wait_ge(s_same_ready, 1)
                nc.vector.scalar_tensor_tensor(out=same_pair, in0=PS[:, 6, P:2 * P], scalar=slot_obj, in1=same,
                                               op0=ALU.is_equal, op1=ALU.mult).then_inc(s_same_ready, 1)
                nc.vector.tensor_tensor_reduce(out=row_b, in0=same, in1=after[:, :], scale=1.0, scalar=0.0,
                                               op0=ALU.mult, op1=ALU.add, accum_out=rep).then_inc(s_slot_step, 1)
                nc.vector.tensor_copy(row_n16, row_n).then_inc(s_row_ready, 1)
                for t in range(T):
                    nc.vector.tensor_scalar(hot_down[:, t, :], PS[:, 6, 0:P], float(-t * P), row_id, ALU.add,
                                            ALU.is_equal).then_inc(s_row_ready, 1)
                dve.wait_ge(s_same_ready, 2)
                nc.vector.tensor_tensor_reduce(out=obj_b, in0=same_pair, in1=after[:, :], scale=1.0, scalar=0.0,
                                               op0=ALU.mult, op1=ALU.add, accum_out=first).then_inc(s_slot_step, 1)
                dve.wait_ge(s_slot_step, 6)
                nc.vector.tensor_scalar(rep, rep, 0.0, slot_low, ALU.is_equal, ALU.mult).then_inc(s_slot_step, 1)
                nc.vector.tensor_scalar(first, first, 0.0, slot_low, ALU.is_equal, ALU.mult).then_inc(s_slot_step, 1)
                dve.wait_ge(s_row_mm, 1)
                nc.vector.tensor_scalar(row_sum, PS[:, 4, 0:1], 1.0, DIAG, ALU.max, ALU.add).then_inc(s_slot_step, 1)
                dve.wait_ge(s_xc_hi, 1)
                nc.vector.scalar_tensor_tensor(out=flat(pair_hl[:, 1]), in0=flat(pair_x), scalar=SX,
                                               in1=flat(pair_hl[:, 0]), op0=ALU.mult, op1=ALU.subtract)\
                    .then_inc(s_xc_lo, 1)
                dve.wait_ge(s_xct_mm, 2)
                nc.vector.tensor_copy(pair_t[:, 1], PS16[:, 7168:8192]).then_inc(s_xct_lo, 1)
                dve.wait_ge(s_b_in, 96)
                dve.wait_ge(s_q_mm, 1)
                nc.vector.scalar_tensor_tensor(out=pair_q, in0=PS[:, 2, :], scalar=1.0 / (SX * SW0), in1=bq0_row,
                                               op0=ALU.mult, op1=ALU.add).then_inc(s_pair_step, 1)
                dve.wait_ge(s_q_mm, 2)
                nc.vector.scalar_tensor_tensor(out=pair_k, in0=PS[:, 3, :], scalar=1.0 / (SX * SW0), in1=bk0_row,
                                               op0=ALU.mult, op1=ALU.add).then_inc(s_pair_step, 1)
                dve.wait_ge(s_pair_step, 2)
                nc.vector.tensor_tensor(pair_q, pair_q, pair_k, ALU.mult).then_inc(s_pair_step, 1)
                dve.wait_ge(s_pair_step, 3)
                nc.vector.reduce_sum(att, pair_q.rearrange("p (h n) -> p h n", h=HEADS), mybir.AxisListType.X)\
                    .then_inc(s_pair_step, 1)
                dve.wait_ge(s_pair_step, 4)
                nc.vector.tensor_scalar(att, att, 0.125, None, ALU.mult).then_inc(s_pair_step, 1)
                dve.wait_ge(s_pair_step, 5)
                nc.vector.tensor_copy(att_b, att.unsqueeze(2).to_broadcast([P, HEADS, P])).then_inc(s_attb_ready, 1)
                nc.vector.tensor_scalar(row_hot, iota[:, :], slot_row, None, ALU.is_equal).then_inc(s_slot_step, 1)
                dve.wait_ge(s_slot_step, 10)
                nc.vector.tensor_scalar(put_hot, row_hot, rep, None, ALU.mult).then_inc(s_put_ready, 1)
                nc.vector.tensor_scalar(other_row, same, -1.0, OFF, ALU.add, ALU.mult).then_inc(s_attb_ready, 1)
                dve.wait_ge(s_attb_ready, 2)
                dve.wait_ge(s_att_mm, 1)
                nc.vector.tensor_tensor(att_row, PS[:, 4:6, :].rearrange("p b (h n) -> p (b h) n", n=P),
                                        other_row.unsqueeze(1).to_broadcast([P, HEADS, P]), ALU.add)\
                    .then_inc(s_pair_step, 1)
                dve.wait_ge(s_pair_step, 6)
                nc.vector.reduce_max(mx, att_row, mybir.AxisListType.X).then_inc(s_pair_step, 1)
                dve.wait_ge(s_pair_step, 7)
                nc.vector.tensor_scalar(args[:, HEADS:2 * HEADS], mx, DIAG, -1.0, ALU.max, ALU.mult)\
                    .then_inc(s_arg_ready, 1)
                dve.wait_ge(s_arg_ready, 1)
                nc.vector.tensor_tensor(args[:, 0:HEADS], att, args[:, HEADS:2 * HEADS], ALU.add)\
                    .then_inc(s_arg_ready, 1)
                dve.wait_ge(s_p_ready, 1)
                nc.vector.tensor_tensor(em_d[:, 1, :], p_em[:, 0:HEADS], p_em[:, HEADS:2 * HEADS], ALU.subtract)\
                    .then_inc(s_pair_step, 1)
                nc.vector.tensor_copy(em_d[:, 0, :], p_em[:, HEADS:2 * HEADS]).then_inc(s_pair_step, 1)
                dve.wait_ge(s_pair_step, 9)
                nc.vector.tensor_scalar(em_d[:, 1, :], em_d[:, 1, :], first, None, ALU.mult).then_inc(s_pair_step, 1)
                dve.wait_ge(s_pair_step, 10)
                nc.vector.tensor_scalar(d_hl[:, 0:HEADS], em_d[:, 1, :], SP_, None, ALU.mult).then_inc(s_pair_step, 1)
                dve.wait_ge(s_pair_step, 11)
                nc.vector.scalar_tensor_tensor(out=d_hl[:, HEADS:2 * HEADS], in0=em_d[:, 1, :], scalar=SP_,
                                               in1=d_hl[:, 0:HEADS], op0=ALU.mult, op1=ALU.subtract)\
                    .then_inc(s_d_ready, 1)
                dve.wait_ge(s_sum_mm, 1)
                nc.vector.tensor_copy(zs2, PS[:, 6, 0:2 * HEADS]).then_inc(s_pair_step, 1)
                dve.wait_ge(s_pair_step, 12)
                nc.vector.tensor_tensor(zs, zs2[:, 0:HEADS], zs2[:, HEADS:2 * HEADS], ALU.add).then_inc(s_pair_step, 1)
                dve.wait_ge(s_pair_step, 13)
                nc.vector.tensor_scalar(zs, zs, 1.0 / SP_, None, ALU.mult).then_inc(s_pair_step, 1)
                dve.wait_ge(s_pair_step, 14)
                nc.vector.scalar_tensor_tensor(out=zs, in0=em_d[:, 0, :], scalar=row_sum, in1=zs, op0=ALU.mult,
                                               op1=ALU.add).then_inc(s_pair_step, 1)
                dve.wait_ge(s_pair_step, 15)
                nc.vector.reciprocal(rz, zs).then_inc(s_pair_step, 1)
                dve.wait_ge(s_pair_step, 16)
                nc.vector.tensor_tensor(em_d, em_d, rz.unsqueeze(1).to_broadcast([P, 2, HEADS]), ALU.mult)\
                    .then_inc(s_pair_step, 1)
                dve.wait_ge(s_pair_step, 17)
                nc.vector.reduce_sum(weights, em_d, mybir.AxisListType.X).then_inc(s_pair_step, 1)
                dve.wait_ge(s_pair_step, 18)
                nc.vector.tensor_scalar(obj_weight, weights[:, 1:2], SX / HEADS, None, ALU.mult)\
                    .then_inc(s_weight_ready, 1)
                nc.vector.tensor_scalar(w_hl[:, 0:1], weights[:, 0:1], SP_ / HEADS, None, ALU.mult)\
                    .then_inc(s_pair_step, 1)
                nc.vector.memset(w_hl[:, 2:3], 1.0).then_inc(s_pair_step, 1)
                dve.wait_ge(s_pair_step, 20)
                nc.vector.scalar_tensor_tensor(out=w_hl[:, 1:2], in0=weights[:, 0:1], scalar=SP_ / HEADS,
                                               in1=w_hl[:, 0:1], op0=ALU.mult, op1=ALU.subtract)\
                    .then_inc(s_put_ready, 1)
                dve.wait_ge(s_y_hi, 1)
                nc.vector.scalar_tensor_tensor(out=put_hl[:, 1], in0=pair_x[:, 1, :], scalar=obj_weight,
                                               in1=put_hl[:, 0], op0=ALU.mult, op1=ALU.subtract).then_inc(s_y_lo, 1)
                dve.wait_ge(s_has_mm, 1)
                nc.vector.tensor_copy(has, PS[:, 7, 0:3 * T].rearrange("p (t n) -> p t n", n=3)).then_inc(s_pair_step, 1)
                dve.wait_ge(s_pair_step, 21)
                nc.vector.tensor_scalar(nohas, has[:, :, 2], -1.0, 1.0, ALU.mult, ALU.add).then_inc(s_pair_step, 1)
                nc.vector.tensor_tensor(has[:, :, 0], has[:, :, 0], has[:, :, 1], ALU.add).then_inc(s_pair_step, 1)
                dve.wait_ge(s_pair_step, 23)
                nc.vector.tensor_tensor(c_a, c_a, nohas, ALU.mult).then_inc(s_pair_step, 1)
                nc.vector.tensor_scalar(has[:, :, 0], has[:, :, 0], 1.0 / SP_, None, ALU.mult).then_inc(s_pair_step, 1)
                dve.wait_ge(s_pair_step, 25)
                nc.vector.tensor_tensor(c_a, c_a, has[:, :, 0], ALU.add).then_inc(s_has_ready, 1)
                dve.wait_ge(s_has_ready, 1)
                nc.vector.tensor_scalar(c_b, c_a, SX * DIAG, SX, ALU.mult, ALU.add).then_inc(s_pair_step, 1)
                dve.wait_ge(s_pair_step, 26)
                nc.vector.memset(ln_mv, 0.0).then_inc(s_all_done, 1)
                dve.wait_ge(s_y_lo, 1)
                layer0_end(put=True)

            def norm(n, x_t):
                dve.wait_ge(s_ln_r, n + 1)
                dve.nop(nofuse=True)
                nc.vector.bn_stats(ln_st, x_t).then_inc(s_ln_s, 1)
                dve.wait_ge(s_ln_s, n + 1)
                dve.nop(nofuse=True)
                nc.vector.bn_aggr(ln_mv, ln_st).then_inc(s_ln_m, 1)
                dve.wait_ge(s_ln_m, n + 1)
                nc.vector.tensor_scalar(ln_var, ln_mv[:, 1:2], EPS, None, ALU.add).then_inc(s_ln_v, 1)
                dve.wait_ge(s_ln_rstd, n + 1)
                return nc.vector.tensor_scalar(x_t, x_t, ln_mv[:, 0:1], ln_rstd, ALU.subtract, ALU.mult)

            def w1_lo(t):
                dve.wait_ge(s_w1_hi, t + 1)
                nc.vector.scalar_tensor_tensor(
                    out=VHL[:, 1, t, :], in0=PS[:, w1_bank(t), :], scalar=dinv_half[:, t:t + 1], in1=VHL[:, 0, t, :],
                    op0=ALU.mult, op1=ALU.subtract).then_inc(s_w1_lo, 1)

            for t in range(T):
                w1_lo(t)
            dve.wait_ge(s_ln_x, T)
            dve.sem_inc(s_ln_r, T)
            dve.wait_ge(s_wv_hi, 1)
            nc.vector.scalar_tensor_tensor(out=flat(wv_hl[:, 1]), in0=flat(wv_f), scalar=SW, in1=flat(wv_hl[:, 0]),
                                           op0=ALU.mult, op1=ALU.subtract).then_inc(s_wv_lo, 1)
            for m in range(C):
                dve.wait_ge(s_wvt_mm, m + 1)
                nc.vector.tensor_copy(WVT[:, :, :, m * P:(m + 1) * P],
                                      PS16[:, 6144 + (m % 2) * 1024:6144 + (m % 2) * 1024 + 1024]
                                      .rearrange("p (h c n) -> p h c n", h=2, c=C)).then_inc(s_wvt_out, 1)

            def add_rows(t, before, scale):
                dve.wait_ge(s_prod_mm, before + t + 1)
                return nc.vector.scalar_tensor_tensor(
                    out=row(X, t), in0=PS[:, ds(t % 2, 1), :].rearrange("p a n -> p (a n)"), scalar=scale,
                    in1=row(X, t), op0=ALU.mult, op1=ALU.add)

            def x_low(n, t, slot):
                dve.wait_ge(s_x_hi, n * T + t + 1)
                nc.vector.scalar_tensor_tensor(out=x_row(1, slot), in0=row(X, t), scalar=SX, in1=x_row(0, slot),
                                               op0=ALU.mult, op1=ALU.subtract).then_inc(s_x_lo, 1)

            def rows_low(n, t, slot):
                dst = SHL if n == 1 else VHL
                dve.wait_ge(s_rows_hi, (n - 1) * T + t + 1)
                nc.vector.scalar_tensor_tensor(out=part_row(dst, 1, t), in0=PS[:, 4 + slot, :], scalar=1.0 / SX,
                                               in1=part_row(dst, 0, t), op0=ALU.mult, op1=ALU.subtract)\
                    .then_inc(s_rows_lo, 1)


            def step(n, t, slot, rows=True):
                if n == 2:
                    dve.wait_ge(s_ln_x, T + t + 1)
                    nc.vector.tensor_tensor(row(X, t), row(X, t), b2_row, ALU.add).then_inc(s_x3_add, 1)
                    dve.wait_ge(s_x3_add, t + 1)
                add_rows(t, (n + 1) * T, 1.0 / SX if n == 1 else 1.0 / SW).then_inc(s_ln_r, 1)
                norm(n * T + t, row(X, t)).then_inc(s_ln_x, 1)
                x_low(n, t, slot)
                if rows:
                    rows_low(n, t - 3, 1 - slot)

            dve.sem_inc(s_qt_done, 2)

            def queries(n, m0, m1):
                with dve.Fori(m0, m1) as m:
                    dve.wait_ge(s_qf_ready, C * n + m + 3)
                    full = qf[:, ds(m % 2, 1), :].rearrange("p a n -> p (a n)")
                    q_at = [QT[:, i, ds(m, 1), n * GW:(n + 1) * GW].rearrange("p a n -> p (a n)") for i in range(2)]
                    nc.vector.tensor_copy(q_at[0], full).then_inc(s_qh_done, 1)
                    dve.wait_ge(s_qh_done, C * n + m + 1)
                    nc.vector.tensor_tensor(q_at[1], full, q_at[0], ALU.subtract).then_inc(s_qt_done, 1)

            dve.wait_ge(s_b3_in, 32)
            dve.sem_inc(s_rows_lo, 2)
            for n in (1, 2):
                step(n, 0, 0, rows=False)
                step(n, 1, 1, rows=False)
                step(n, 2, 0, rows=False)
                with dve.Fori(1, T // 2) as j:
                    step(n, 2 * j + 1, 1)
                    step(n, 2 * j + 2, 0)
                rows_low(n, T - 3, 0)
                rows_low(n, T - 2, 1)
                if n == 2:
                    queries(0, 0, C)
                rows_low(n, T - 1, 0)
            dve.wait_ge(s_vec_out, 3)
            nc.vector.memset(QT[:, :, :, NG:NP], 0.0).then_inc(s_pad3, 1)
            nc.vector.memset(prob_hl[:, :, N:NP], 0.0).then_inc(s_pad3, 1)
            dve.sem_inc(s_t3_ready, 1)

            def scores(t):
                dve.wait_ge(s_ln_x, 2 * T + t + 1)
                nc.vector.scalar_tensor_tensor(out=out_t, in0=row(X, t), scalar=1.0, in1=a_row[:, :], op0=ALU.mult,
                                               op1=ALU.mult, accum_out=r_acc).then_inc(s_r_step, 1)
                dve.wait_ge(s_r_step, 2 * t + 1)
                nc.vector.tensor_tensor(r3, r_acc, beta, ALU.add).then_inc(s_r_step, 1)
                dve.wait_ge(s_r_step, 2 * t + 2)
                dve.wait_ge(s_z_mm, t + 1)
                nc.vector.scalar_tensor_tensor(
                    out=score.rearrange("p (g n) -> p g n", g=G), in0=PS[:, 0:G, 0:GW], scalar=r3,
                    in1=A[:, ds(t, 1), 0:NG].rearrange("p a (g n) -> p (a g) n", g=G), op0=ALU.add, op1=ALU.mult)\
                    .then_inc(s_t3_ready, 1)
                dve.wait_ge(s_t3_ready, t + 2)
                nc.vector.tensor_scalar(zero_fill[:, 0:N], score[:, 0:N], 0.0, FILL / Z_SCALE, ALU.is_equal, ALU.mult)\
                    .then_inc(s_m3_ready, 1)
                dve.wait_ge(s_m3_ready, 2 * t + 1)
                dve.nop(nofuse=True)
                nc.vector.tensor_tensor_reduce(out=score[:, 0:N], in0=score[:, 0:N], in1=zero_fill[:, 0:N], scale=1.0,
                                               scalar=-3.0e38, op0=ALU.add, op1=ALU.max, accum_out=m3)\
                    .then_inc(s_m3_ready, 1)
                dve.wait_ge(s_m3_ready, 2 * t + 2)
                nc.vector.tensor_scalar(nm3, m3, -Z_SCALE, None, ALU.mult).then_inc(s_nm3_ready, 1)

            def prob_low(t):
                dve.wait_ge(s_ph_ready, t + 1)
                nc.vector.scalar_tensor_tensor(out=prob_hl[:, 1, 0:N], in0=zero_fill[:, 0:N], scalar=SP_,
                                               in1=prob_hl[:, 0, 0:N], op0=ALU.mult, op1=ALU.subtract)\
                    .then_inc(s_pl_ready, 1)
                nc.vector.reciprocal(one(rz_all, t), z3).then_inc(s_rz3_ready, 1)
                dve.wait_ge(s_rz3_ready, 2 * t + 1)
                nc.vector.tensor_scalar(one(rz_all, t), one(rz_all, t), 1.0 / (SP_ * SW), None, ALU.mult)\
                    .then_inc(s_rz3_ready, 1)

            def turn(t):
                dve.wait_ge(s_pt_mm, 2 * t + 2)
                nc.vector.tensor_copy(turned(t % 2, 1), PS16[:, 5120:5120 + NP]).then_inc(s_pt_lo, 1)

            def finish(t, out=7):
                dve.wait_ge(s_o_mm, t + 1)
                dve.wait_ge(s_rz3_ready, 2 * t + 2)
                nc.vector.scalar_tensor_tensor(out=out_t, in0=PS[:, out, :], scalar=one(rz_all, t), in1=bv_row[:, :],
                                               op0=ALU.mult, op1=ALU.add).then_inc(s_o_ready, 1)
                dve.wait_ge(s_o_ready, t + 1)
                nc.vector.scalar_tensor_tensor(out=row(X, t), in0=out_t, scalar=0.0, in1=row(X, t), op0=ALU.max,
                                               op1=ALU.add).then_inc(s_ln_r, 1)
                norm(3 * T + t, row(X, t)).then_inc(s_o_norm, 1)

            scores(0)
            queries(1, 0, 2)
            prob_low(0)
            queries(1, 2, C)
            turn(0)
            scores(1)
            queries(2, 0, 2)
            prob_low(1)
            queries(2, 2, C)
            with dve.Fori(2, T) as t:
                scores(t)
                turn(t - 1)
                prob_low(t)
                finish(t - 2)
            turn(T - 1)
            finish(T - 2)
            finish(T - 1, out=0)

        @block.tensor
        def _(pe):
            def turn_rows(t, at, hl):
                for i in range(2):
                    for c in range(C):
                        last = nc.tensor.transpose(PS16[:, at + (i * C + c) * P:at + (i * C + c + 1) * P],
                                                   hl[:, i, t, c * P:(c + 1) * P], ident[:, :])
                return last

            def turn_weight(hl, m, at):
                for i in range(2):
                    for c in range(C):
                        last = nc.tensor.transpose(PS16[:, at + (i * C + c) * P:at + (i * C + c + 1) * P],
                                                   hl[:, i, m, c * P:(c + 1) * P], ident[:, :])
                return last

            def turn_tile(slot):
                for i in range(2):
                    for c in range(C):
                        at = 2048 + slot * 1024 + (i * C + c) * P
                        last = nc.tensor.transpose(PS16[:, at:at + P], x_row(i, slot)[:, c * P:(c + 1) * P],
                                                   ident[:, :])
                return last

            def product(out, lhs, rhs, n):
                for k in range(n):
                    for j, (a, b) in enumerate(PAIRS):
                        last = nc.tensor.matmul(out, lhs(a, k), rhs(b, k), start=(k == 0 and j == 0),
                                                stop=(k == n - 1 and j == len(PAIRS) - 1))
                return last

            def graph_product(out, mat, t, rhs):
                for k in range(T):
                    for i in range(2):
                        last = nc.tensor.matmul(out, mat[:, k, ds(t * P, P)], rhs[:, i, k, :],
                                                start=(k == 0 and i == 0), stop=(k == T - 1 and i == 1))
                return last

            def bank(t, first=0):
                return PS[:, ds(first + t % 2, 1), :].rearrange("p a n -> p (a n)")

            pe.wait_ge(s_ident_ready, 1)
            pe.wait_ge(s_w0_lo, 1)
            for m in range(C):
                pe.wait_ge(s_w0_out, m + 1)
                turn_weight(w0_hl, m, 4096 + (m % 2) * 1024).then_inc(s_w0_mm, 1)
            pe.wait_ge(s_w0_out, 2 + C)
            pe.wait_ge(s_w0_lo, 2)
            for m in range(C):
                pe.wait_ge(s_w0_out, C + m + 1)
                turn_weight(w0q_hl, m, 4096 + (m % 2) * 1024).then_inc(s_w0_mm, 1)
            pe.wait_ge(s_w0_out, 2 + 2 * C)
            pe.wait_ge(s_adj_in0, 32)
            for t in range(T):
                if t == ADJ_FIRST:
                    pe.wait_ge(s_adj_in1, 32)
                pe.wait_ge((s_at_v, s_at_a)[t % 2], t // 2 + 1)
                for k in range(T):
                    last = nc.tensor.transpose(PS16[:, at_bank(t) + k * P:at_bank(t) + (k + 1) * P],
                                               A[:, t, k * P:(k + 1) * P], ident[:, :])
                last.then_inc(s_at_mm, 1)
            pe.wait_ge(s_wst_lo, 4)
            pe.wait_ge(s_at_a, 1 + T // 2)
            for d in range(C):
                if d == 2:
                    pe.wait_ge(s_at_v, 2 + (T + 1) // 2)
                    pe.wait_ge(s_at_a, 2 + T // 2)
                product(PS[:, g_bank[d], :], lambda i, c: wq3_hl[:, i, c, d * P:(d + 1) * P],
                        lambda i, c: wk3_hl[:, i, c, :], C).then_inc(s_g_mm, 1)
            pe.wait_ge(s_bkb_ready, 2 * C)
            product(PS[:, 4, :], lambda i, c: bk_b[:, i, c, :], lambda i, c: wq3_hl[:, i, c, :], C)
            for m in range(C):
                product(PS[:, 5, m:m + 1], lambda i, c: wk3_hl[:, i, c, m * P:(m + 1) * P],
                        lambda i, c: b_hl[:, i, C + c:C + c + 1], C)
            product(PS[:, 5, C:C + 1], lambda i, c: bk_b[:, i, c, :], lambda i, c: b_hl[:, i, C + c:C + c + 1], C)\
                .then_inc(s_vec_mm, 1)
            def adj_x(t):
                pe.wait_ge(s_base_out, t + 1)
                graph_product(bank(t), AT, t, UHL).then_inc(s_prod_mm, 1)

            def rank_columns(i, c0, c1):
                pe.wait_ge(s_act_ready, i + 1)
                if i == 1:
                    pe.wait_ge(s_rank_ready, 1)
                nc.tensor.matmul(PS[0:c1, 4, 0:P], act16[:, 0:c1], ones[0:EP, :], start=True, stop=True)\
                    .then_inc(s_tot_mm, 1)
                nc.tensor.matmul(PS[0:EP, 6, c0:c1], before[0:EP, 0:EP], act16[:, c0:c1], start=True, stop=False)
                pe.wait_ge(s_tot_ready, i + 1)
                last = nc.tensor.matmul(PS[0:EP, 6, c0:c1], tot16[0:c1, 0:EP], before[0:c1, c0:c1], start=False,
                                        stop=True)
                if i == 1:
                    last = nc.tensor.matmul(PS[:, 7, 0:1], tot16[0:EC, :], ones[0:EC, 0:1], start=True, stop=True)
                last.then_inc(s_rank_mm, 1)

            def take_slots(k):
                pe.wait_ge(s_hot_ready, k + 1)
                for i in range(OC):
                    e = k * OC + i
                    last = nc.tensor.matmul(PS[:, 5, 0:2], hot[k % 2][0:EP, i, :], pair[:, e, :], start=(e == 0),
                                            stop=(e == EC - 1))
                last.then_inc(s_slots_mm, 1)

            pe.wait_ge(s_x_lo, T)
            with pe.Fori(0, AHEAD) as t:
                adj_x(t)
            pe.wait_ge(s_const, 5)
            pe.wait_ge(s_vec_out, 3)
            rank_columns(0, 0, EARLY)
            adj_x(AHEAD)
            take_slots(0)
            take_slots(1)
            adj_x(AHEAD + 1)
            take_slots(2)
            take_slots(3)
            adj_x(AHEAD + 2)
            rank_columns(1, EARLY, EC)
            adj_x(AHEAD + 3)
            pe.wait_ge(s_n_ready, 1)
            many = pe.value_load(n_act[0:1, 0:1])

            def attend(r):
                pe.wait_ge(s_xc_lo, r + 1)
                for i in range(2):
                    for c in range(C):
                        last = nc.tensor.transpose(PS16[:, 7168 + (i * C + c) * P:7168 + (i * C + c + 1) * P],
                                                   xc_hl[:, i, c * P:(c + 1) * P], ident[:, :])
                last.then_inc(s_xct_mm, 1)
                pe.wait_ge(s_xct_out, r + 1)
                for m in range(C):
                    last = product(PS[:, 6, m * P:(m + 1) * P], lambda i, c: WQT[:, i, c, m * P:(m + 1) * P],
                                   lambda i, c: xct[:, i, c, :], C)
                last.then_inc(s_q_mm, 1)
                pe.wait_ge(s_q_lo, 2 * r + 2)
                pe.wait_ge(s_mask_ready, 2 * r + 2)
                for h in range(HEADS):
                    if h >= 2:
                        pe.wait_ge(s_t_ready, HEADS * r + h - 1)
                    for n in range(G):
                        out, cols = PS[:, 2 + G * (h % 2) + n, 0:GW], slice(n * GW, (n + 1) * GW)
                        nc.tensor.matmul(out, identb, bmask[:, cols], start=True, stop=False)
                        for j, (a, b) in enumerate(PAIRS):
                            last = nc.tensor.matmul(out, q_hl[:, a, h, :], KT[:, b, h // 2, cols],
                                                    start=False, stop=(j == len(PAIRS) - 1))
                    last.then_inc(s_s_mm, 1)
                for i, ready in enumerate((s_f_hi, s_f_lo)):
                    pe.wait_ge(s_f_pad, r + 1)
                    pe.wait_ge(ready, r + 1)
                    for k in range(T):
                        at = 2048 * (i + 1) + k * P
                        last = nc.tensor.transpose(PS16[:, at:at + P], f_hl[:, i, k * P:(k + 1) * P], ident[:, :])
                    last.then_inc(s_ft_mm, 1)
                pe.wait_ge(s_ft_hi, r + 1)
                for a, b in PAIRS:
                    if a == 1:
                        pe.wait_ge(s_ft_lo, r + 1)
                    for k in range(T):
                        last = nc.tensor.matmul(PS[:, 0, :], f_t[:, a, k, :], UHL[:, b, k, :],
                                                start=((a, b) == PAIRS[0] and k == 0),
                                                stop=((a, b) == PAIRS[-1] and k == T - 1))
                last.then_inc(s_y_mm, 1)

            def layer1_start(put):
                for k in range(-5, T):
                    if put and k + 5 < T:
                        if k >= -3:
                            pe.wait_ge(s_placed, k + 4)
                        for i in range(2):
                            last = nc.tensor.matmul(PS[:, (k + 5) % 2, :], row_hot[:, (k + 5) * P:(k + 6) * P],
                                                    put_hl[:, i, :], start=(i == 0), stop=(i == 1))
                        last.then_inc(s_put_mm, 1)
                    if k < 0:
                        continue
                    pe.wait_ge(s_sym_ready, (k + 1) if put else T + k + 1)
                    pe.wait_ge(s_u_lo, k + 1)
                    for t in range(W1_AT_ONCE):
                        for i in range(2):
                            last = nc.tensor.matmul(PS[:, w1_bank(t), :], SYM[:, k, t * P:(t + 1) * P],
                                                    UHL[:, i, k, :], start=(k == 0 and i == 0),
                                                    stop=(k == T - 1 and i == 1))
                        if k == T - 1:
                            last.then_inc(s_prod_mm, 1)

            with pe.If(many > P):
                pe.wait_ge(s_rank_ready, 2)
                nc.tensor.matmul(PS[:, 5, 0:2], hot[1][0:EP, 0, :], pair[:, 0, :], start=False, stop=True)
                with pe.Fori(AHEAD + 4, T) as t:
                    adj_x(t)
                pe.wait_ge(s_base_out, 2 + T)
                for t in range(T):
                    pe.wait_ge(s_x_lo, t + 1)
                    pe.wait_ge(s_xt_out, t + 1)
                    turn_rows(t, (t % 4) * 1024, UHL).then_inc(s_xt_mm, 1)
                pe.wait_ge(s_xt_out, 4 + T)
                with pe.Fori(0, C) as m:
                    for n in range(G):
                        pe.wait_ge(s_kf_ready, G * m + n + 1)
                        product(PS[:, 2 + n, 0:GW], lambda i, c: WKT[:, i, c, ds(m * P, P)],
                                lambda i, c: XT[:, i, c, n * GW:(n + 1) * GW], C).then_inc(s_kp_mm, 1)
                pe.wait_ge(s_kf_ready, G * C + G)
                pe.sem_inc(s_hots_free, 2)

                def relations(t, j, first=False, end=False):
                    for i in range(2):
                        pe.wait_ge(s_hots_made, 2 * (t * EC + j * 2 + i + 1))
                        for n in range(G):
                            last = nc.tensor.matmul(PS[:, 2 + n, 0:GW], all_sub[i][0:EP, :],
                                                    all_obj[i][0:EP, n * GW:(n + 1) * GW],
                                                    start=(first and i == 0), stop=(end and i == 1))
                        last.then_inc(s_hots_free, 1)
                    if end:
                        return last

                with pe.Fori(0, T) as t:
                    relations(t, 0, first=True)
                    with pe.Fori(1, EC // 2 - 1) as j:
                        relations(t, j)
                    relations(t, EC // 2 - 1, end=True)
                    pe.wait_ge(s_hots_free, (t + 1) * EC + 2)
                    nc.tensor.matmul(PS[:, 5, 0:1], ident[:, :], ones[:, 0:1], start=True, stop=True)\
                        .then_inc(s_w_mm, 1)
                    attend(t)
                layer1_start(put=False)
            with pe.Else():
                pe.sem_inc(s_xt_mm, T)
                take_slots(4)
                pe.wait_ge(s_sub_ready, 2)
                nc.tensor.matmul(PS[:, 6, 0:P], row_b, ident[:, :], start=True, stop=True)
                nc.tensor.matmul(PS[:, 6, P:2 * P], obj_b, ident[:, :], start=True, stop=True).then_inc(s_sub_mm, 1)
                pe.wait_ge(s_row_ready, 1 + T)
                for t in range(T):
                    last = nc.tensor.matmul(PS[:, 4, 0:1], hot_down[:, t, :], row_n16[:, t:t + 1], start=(t == 0),
                                            stop=(t == T - 1))
                last.then_inc(s_row_mm, 1)
                pe.wait_ge(s_same_ready, 2)
                pe.wait_ge(s_xc_lo, 1)
                for j in range(2):
                    for i in range(2):
                        for c in range(C):
                            at = 6144 + 1024 * j + (i * C + c) * P
                            last = nc.tensor.transpose(PS16[:, at:at + P], pair_hl[:, i, j, c * P:(c + 1) * P],
                                                       ident[:, :])
                    last.then_inc(s_xct_mm, 1)
                pair_c = pair_t.rearrange("p j (i c n) -> p j i c n", i=2, c=C)
                for j, (weight, out) in enumerate(((WQT, s_xct_out), (WKT, s_xct_lo))):
                    pe.wait_ge(out, 1)
                    product(PS[:, 2 + j, :], lambda i, c: pair_c[:, j, i, c, :], lambda i, c: weight[:, i, c, :], C)\
                        .then_inc(s_q_mm, 1)
                adj_x(T - 2)
                pe.wait_ge(s_attb_ready, 1)
                for h in range(HEADS):
                    last = nc.tensor.matmul(PS[:, 4 + h // 4, (h % 4) * P:(h % 4 + 1) * P], att_b[:, h, :],
                                            identf[:, :], start=True, stop=True)
                last.then_inc(s_att_mm, 1)
                adj_x(T - 1)
                pe.wait_ge(s_d_ready, 1)
                nc.tensor.matmul(PS[:, 6, 0:2 * HEADS], same, d_hl[:, :], start=True, stop=True).then_inc(s_sum_mm, 1)
                pe.wait_ge(s_put_ready, 2)
                for t in range(T):
                    last = nc.tensor.matmul(PS[:, 7, 3 * t:3 * t + 3], put_hot[:, t * P:(t + 1) * P], w_hl[:, 0:3],
                                            start=True, stop=True)
                last.then_inc(s_has_mm, 1)
                pe.wait_ge(s_y_lo, 1)
                pe.wait_ge(s_base_out, 2 + T)
                layer1_start(put=True)

            for t in range(W1_AT_ONCE, T):
                if t >= W1_AT_ONCE + 2:
                    pe.wait_ge(s_w1_lo, t - 1)
                graph_product(PS[:, w1_bank(t), :], SYM, t, UHL).then_inc(s_prod_mm, 1)
            pe.wait_ge(s_w1_lo, T)
            pe.wait_ge(s_wst_lo, 6)
            pe.wait_ge(s_moved, 16)

            def adj_product(n, t, slot, late=False):
                pe.wait_ge(s_ln_r, n * T + t - 1)
                rhs = VHL if n == 1 else SHL
                for k in range(T):
                    if late and k == T - 1:
                        pe.wait_ge(s_rows_lo, 2 + T)
                    for i in range(2):
                        last = nc.tensor.matmul(PS[:, slot, :], AT[:, k, ds(t * P, P)], rhs[:, i, k, :],
                                                start=(k == 0 and i == 0), stop=(k == T - 1 and i == 1))
                last.then_inc(s_prod_mm, 1)

            def turn_step(n, t, slot):
                pe.wait_ge(s_x_lo, n * T + t + 1)
                pe.wait_ge(s_xt_out, n * (T + 2) + 2 + t + 1)
                turn_tile(slot).then_inc(s_xt_mm, 1)

            def rows_step(n, t, slot):
                pe.wait_ge(s_xt_out, n * (T + 2) + 4 + t + 1)
                pe.wait_ge(s_rows_lo, (n - 1) * T + t + 1)
                weight = W2HL if n == 1 else WVT
                product(PS[:, 4 + slot, :], lambda i, c: XT[:, i, c, ds(t * P, P)], lambda i, c: weight[:, i, c, :], C)\
                    .then_inc(s_rows_mm, 1)

            def queries(n):
                with pe.Fori(0, C) as m:
                    pe.wait_ge(s_qf_ready, C * n + m + 1)
                    product(PS[:, ds(6 + m % 2, 1), 0:GW].rearrange("p a n -> p (a n)"),
                            lambda i, c: GW3[:, i, c, ds(m * P, P)],
                            lambda i, c: XT[:, i, c, n * GW:(n + 1) * GW], C).then_inc(s_qt_mm, 1)

            for n in (1, 2):
                if n == 2:
                    pe.wait_ge(s_rows_lo, 1 + T)
                adj_product(n, 0, 0, late=(n == 2))
                adj_product(n, 1, 1)
                if n == 1:
                    pe.wait_ge(s_wv_lo, 1)
                    for m in range(C):
                        if m >= 2:
                            pe.wait_ge(s_wvt_out, m - 1)
                        turn_weight(wv_hl, m, 6144 + (m % 2) * 1024).then_inc(s_wvt_mm, 1)
                else:
                    pe.wait_ge(s_wvt_out, C)
                adj_product(n, 2, 0)
                turn_step(n, 0, 0)
                with pe.Fori(1, T // 2) as j:
                    adj_product(n, 2 * j + 1, 1)
                    turn_step(n, 2 * j - 1, 1)
                    rows_step(n, 2 * j - 2, 0)
                    adj_product(n, 2 * j + 2, 0)
                    turn_step(n, 2 * j, 0)
                    rows_step(n, 2 * j - 1, 1)
                turn_step(n, T - 2, 1)
                rows_step(n, T - 3, 0)
                rows_step(n, T - 2, 1)
                turn_step(n, T - 1, 0)
                if n == 2:
                    queries(0)
                rows_step(n, T - 1, 0)

            def scores(t):
                pe.wait_ge(s_t3_ready, t + 1)
                for n in range(G):
                    last = product(PS[:, n, 0:GW], lambda i, c: QT[:, i, c, ds(t * P, P)],
                                   lambda i, c: XT[:, i, c, n * GW:(n + 1) * GW], C)
                last.then_inc(s_z_mm, 1)

            def turn(t):
                for i, ready, read in ((0, s_ph_ready, s_pt_hi), (1, s_pl_ready, s_pt_lo)):
                    pe.wait_ge(ready, t + 1)
                    if not isinstance(t, int) or t > 0:
                        pe.wait_ge(read, t)
                    for k in range(T):
                        at = 3072 + 2048 * i + k * P
                        last = nc.tensor.transpose(PS16[:, at:at + P], prob_hl[:, i, k * P:(k + 1) * P], ident[:, :])
                    last.then_inc(s_pt_mm, 1)

            def attend3(t, out=7):
                pe.wait_ge(s_pt_hi, t + 1)
                pe.wait_ge(s_pt_lo, t + 1)
                if out == 7 and (not isinstance(t, int) or t > 0):
                    pe.wait_ge(s_o_ready, t)
                product(PS[:, out, :], lambda i, k: turned(t % 2, i)[:, k * P:(k + 1) * P],
                        lambda i, k: VHL[:, i, k, :], T).then_inc(s_o_mm, 1)

            pe.wait_ge(s_pad3, 2)
            pe.wait_ge(s_qt_done, 2 + C)
            scores(0)
            queries(1)
            pe.wait_ge(s_qf_ready, 2 + 2 * C)
            turn(0)
            scores(1)
            pe.wait_ge(s_pt_lo, 1)
            queries(2)
            scores(2)
            pe.wait_ge(s_qf_ready, 2 + 3 * C)
            pe.wait_ge(s_rows_lo, 2 * T + 2)
            turn(1)
            attend3(0)
            pe.wait_ge(s_qt_done, 2 + 3 * C)
            with pe.Fori(3, T) as t:
                scores(t)
                turn(t - 1)
                attend3(t - 2)
            turn(T - 1)
            attend3(T - 2)
            attend3(T - 1, out=0)



_INS = ["x", "adj", "L0_gnn_rel_pair_index", "L0_gnn_Wq", "L0_gnn_bq", "L0_gnn_Wk", "L0_gnn_bk", "L2_gnn_weight",
        "L2_gnn_bias", "L3_gnn_W_q", "L3_gnn_b_q", "L3_gnn_W_k", "L3_gnn_b_k", "L3_gnn_W_v", "L3_gnn_b_v"]


def kernel(**inputs):
    import numpy as _np
    import concourse.bacc as _bacc
    from concourse import mybir as _mybir
    from concourse.bass_utils import run_bass_kernel_spmd as _run

    nc = _bacc.Bacc("TRN2", target_bir_lowering=False, num_devices=1)
    arrays, args = {}, []
    for name in _INS:
        a = _np.ascontiguousarray(inputs[name])
        arrays[f"in_{name}"] = a
        args.append(nc.dram_tensor(f"in_{name}", a.shape, _mybir.dt.from_np(a.dtype), kind="ExternalInput").ap())
    args.append(nc.dram_tensor("out_0", (N, D), F32, kind="ExternalOutput").ap())
    build(nc, *args)
    r = _run(nc, [arrays], core_ids=[0])
    return r.results[0]["out_0"]
```
